# Optimizing a Trainium2 kernel written in Bass

```python
import numpy as np
import jax
import jax.numpy as jnp

def _softmax(x, axis=-1):
    return jax.nn.softmax(x, axis=axis)

def _gelu(x):
    return jax.nn.gelu(x, approximate=True)

def _silu(x):
    return jax.nn.silu(x)

def _sigmoid(x):
    return jax.nn.sigmoid(x)

def _layernorm(x, axis=-1, eps=1e-05):
    m = jnp.mean(x, axis=axis, keepdims=True)
    v = jnp.var(x, axis=axis, keepdims=True)
    return (x - m) / jnp.sqrt(v + eps)

def _scatter_add(tgt, idx, src, axis=0):
    return tgt.at[idx].add(src)

def _segment_sum(src, seg, n):
    return jax.ops.segment_sum(src, seg, n)
kernel_name = 'mk_pixart_resid_d2_seqx_r8_e3317f'

def setup_inputs(seed: int=0):
    np.random.seed(seed)
    _w = jnp.asarray

    def _rec_inputs():
        import jax
        import jax.numpy as jnp
        _rk = jax.random.key(seed)
        x = -0.0002928 + 1 * jax.random.normal(jax.random.fold_in(_rk, 1), (4, 256, 128), jnp.float32)
        _lenS = 256 - jax.random.randint(jax.random.fold_in(_rk, 7), (4,), 0, max(1, 256 // 4) + 1, jnp.int32)
        _lenS2 = 64 - jax.random.randint(jax.random.fold_in(_rk, 8), (4,), 0, max(1, 64 // 4) + 1, jnp.int32)
        _ctx_1024P = jax.random.normal(jax.random.fold_in(_rk, 11), (4, 16, 128), jnp.float32)
        _ctx_1024c = jax.random.dirichlet(jax.random.fold_in(_rk, 511), 0.3 * jnp.ones((16,), jnp.float32), (4, 64))
        _ctx_1024t = jnp.einsum('bsk,bkd->bsd', _ctx_1024c, _ctx_1024P)
        _ctx_1024t = _ctx_1024t * jax.lax.rsqrt(jnp.mean(jnp.square(_ctx_1024t)) + 1e-12) * 0.953939
        ctx_1024 = -1.39393e-06 + 0.999914 * (_ctx_1024t + 0.3 * jax.random.normal(jax.random.fold_in(_rk, 611), (4, 64, 128), jnp.float32))
        condB_tau = jax.random.uniform(jax.random.fold_in(_rk, 12), (4,), jnp.float32, 0.0, 1.23395)
        fside_BxS2_0 = -0.00205293 + 0.99739 * jax.random.normal(jax.random.fold_in(_rk, 13), (4, 64), jnp.float32)
        return (x, ctx_1024, condB_tau, fside_BxS2_0)
    x, ctx_1024, condB_tau, fside_BxS2_0 = _rec_inputs()

    def _L0_xcond_setup():
        import jax, jax.numpy as jnp
        import numpy as np
        B, S, D, H = (2, 256, 128, 16)
        DK = D // H

        def _split_heads(x):
            b, s, _ = x.shape
            return x.reshape(b, s, H, DK).transpose(0, 2, 1, 3)
        key = jax.random.key(seed)
        ks = jax.random.split(key, 14)
        inp = {'query': jax.random.normal(ks[0], (B, S, D), jnp.float32), 'key': jax.random.normal(ks[1], (B, S, D), jnp.float32), 'value': jax.random.normal(ks[2], (B, S, D), jnp.float32), 'tau': jax.random.uniform(ks[3], (B, 1), jnp.float32, 0.5, 1.5), 'delta': jax.random.normal(ks[4], (B, S), jnp.float32)}
        sc = 1.0 / np.sqrt(D)
        for i, name in enumerate(['q', 'k', 'v', 'o']):
            inp[f'W{name}'] = jax.random.normal(ks[5 + 2 * i], (D, D), jnp.float32) * sc
            inp[f'b{name}'] = jax.random.normal(ks[6 + 2 * i], (D,), jnp.float32) * 0.01
        return inp
    _L0_xcond_all = _L0_xcond_setup()
    _L0_xcond_in = {k: v for k, v in _L0_xcond_all.items() if k in ('Wq', 'bq', 'Wk', 'bk', 'Wv', 'bv', 'Wo', 'bo')}
    del _L0_xcond_all

    def _L0_ffn_setup():
        import jax, jax.numpy as jnp
        import numpy as np
        B, S, D = (2, 256, 128)
        I = 64
        E = 16
        TOP_K = 2

        def _mlp(x, wg, wu, wd):
            return jnp.einsum('bsi,id->bsd', jax.nn.silu(x @ wg) * (x @ wu), wd)
        key = jax.random.key(seed)
        ks = jax.random.split(key, 10)
        sc_d = 1.0 / np.sqrt(D)
        sc_i = 1.0 / np.sqrt(I)
        return {'x': jax.random.normal(ks[0], (B, S, D), dtype=jnp.float32), 'gate_w': jax.random.normal(ks[1], (D, E), dtype=jnp.float32) * sc_d, 'gate_b': jnp.zeros((E,), dtype=jnp.float32), 'shared_wg': jax.random.normal(ks[2], (D, I), dtype=jnp.float32) * sc_d, 'shared_wu': jax.random.normal(ks[3], (D, I), dtype=jnp.float32) * sc_d, 'shared_wd': jax.random.normal(ks[4], (I, D), dtype=jnp.float32) * sc_i, 'experts_wg': jax.random.normal(ks[5], (E, D, I), dtype=jnp.float32) * sc_d, 'experts_wu': jax.random.normal(ks[6], (E, D, I), dtype=jnp.float32) * sc_d, 'experts_wd': jax.random.normal(ks[7], (E, I, D), dtype=jnp.float32) * sc_i}
    _L0_ffn_all = _L0_ffn_setup()
    _L0_ffn_in = {k: v for k, v in _L0_ffn_all.items() if k in ('gate_w', 'gate_b', 'shared_wg', 'shared_wu', 'shared_wd', 'experts_wg', 'experts_wu', 'experts_wd')}
    del _L0_ffn_all

    def _L1_xcond_setup():
        import jax, jax.numpy as jnp
        import numpy as np
        D_MODEL = 128
        N_HEADS = 16
        key = jax.random.key(seed)
        ks = jax.random.split(key, 16)
        B, L, S, D = (4, 256, 256, D_MODEL)
        inp = {'q': jax.random.normal(ks[0], (B, L, D), jnp.float32), 'k': jax.random.normal(ks[1], (B, S, D), jnp.float32), 'v': jax.random.normal(ks[2], (B, S, D), jnp.float32), 'tau': jax.random.uniform(ks[3], (B, 1), jnp.float32, 0.5, 1.5), 'delta': jax.random.normal(ks[4], (B, S), jnp.float32)}
        s = 1.0 / np.sqrt(D)
        inp['Wq'] = jax.random.normal(ks[5], (D, D), jnp.float32) * s
        inp['bq'] = jnp.zeros((D,), jnp.float32)
        inp['Wk'] = jax.random.normal(ks[6], (D, D), jnp.float32) * s
        inp['bk'] = jnp.zeros((D,), jnp.float32)
        inp['Wv'] = jax.random.normal(ks[7], (D, D), jnp.float32) * s
        inp['bv'] = jnp.zeros((D,), jnp.float32)
        inp['Wo'] = jax.random.normal(ks[8], (D, D), jnp.float32) * s
        inp['bo'] = jnp.zeros((D,), jnp.float32)
        return inp
    _L1_xcond_all = _L1_xcond_setup()
    _L1_xcond_in = {k: v for k, v in _L1_xcond_all.items() if k in ('Wq', 'bq', 'Wk', 'bk', 'Wv', 'bv', 'Wo', 'bo')}
    del _L1_xcond_all

    def _L1_ffn_setup():
        import jax, jax.numpy as jnp
        import numpy as np
        DIM = 128
        NUM_EXPERTS = 8
        HIDDEN = 512
        CAP_FACTOR = 2.0
        B, S = (4, 256)
        key = jax.random.key(seed)
        ks = jax.random.split(key, 6)
        scale_r = 1.0 / np.sqrt(DIM)
        scale_1 = 1.0 / np.sqrt(DIM)
        scale_2 = 1.0 / np.sqrt(HIDDEN)
        return {'x': jax.random.normal(ks[0], (B, S, DIM), dtype=jnp.float32), 'router_w': jax.random.uniform(ks[1], (NUM_EXPERTS, DIM), jnp.float32, -scale_r, scale_r), 'w1': jax.random.uniform(ks[2], (NUM_EXPERTS, DIM, HIDDEN), jnp.float32, -scale_1, scale_1), 'b1': jax.random.uniform(ks[3], (NUM_EXPERTS, HIDDEN), jnp.float32, -scale_1, scale_1), 'w2': jax.random.uniform(ks[4], (NUM_EXPERTS, HIDDEN, DIM), jnp.float32, -scale_2, scale_2), 'b2': jax.random.uniform(ks[5], (NUM_EXPERTS, DIM), jnp.float32, -scale_2, scale_2)}
    _L1_ffn_all = _L1_ffn_setup()
    _L1_ffn_in = {k: v for k, v in _L1_ffn_all.items() if k in ('router_w', 'w1', 'b1', 'w2', 'b2')}
    del _L1_ffn_all
    return {'x': x, 'ctx_1024': ctx_1024, 'condB_tau': condB_tau, 'fside_BxS2_0': fside_BxS2_0, 'L0_xcond_Wq': _L0_xcond_in['Wq'], 'L0_xcond_bq': _L0_xcond_in['bq'], 'L0_xcond_Wk': _L0_xcond_in['Wk'], 'L0_xcond_bk': _L0_xcond_in['bk'], 'L0_xcond_Wv': _L0_xcond_in['Wv'], 'L0_xcond_bv': _L0_xcond_in['bv'], 'L0_xcond_Wo': _L0_xcond_in['Wo'], 'L0_xcond_bo': _L0_xcond_in['bo'], 'L0_ffn_gate_w': _L0_ffn_in['gate_w'], 'L0_ffn_gate_b': _L0_ffn_in['gate_b'], 'L0_ffn_shared_wg': _L0_ffn_in['shared_wg'], 'L0_ffn_shared_wu': _L0_ffn_in['shared_wu'], 'L0_ffn_shared_wd': _L0_ffn_in['shared_wd'], 'L0_ffn_experts_wg': _L0_ffn_in['experts_wg'], 'L0_ffn_experts_wu': _L0_ffn_in['experts_wu'], 'L0_ffn_experts_wd': _L0_ffn_in['experts_wd'], 'L1_xcond_Wq': _L1_xcond_in['Wq'], 'L1_xcond_bq': _L1_xcond_in['bq'], 'L1_xcond_Wk': _L1_xcond_in['Wk'], 'L1_xcond_bk': _L1_xcond_in['bk'], 'L1_xcond_Wv': _L1_xcond_in['Wv'], 'L1_xcond_bv': _L1_xcond_in['bv'], 'L1_xcond_Wo': _L1_xcond_in['Wo'], 'L1_xcond_bo': _L1_xcond_in['bo'], 'L1_ffn_router_w': _L1_ffn_in['router_w'], 'L1_ffn_w1': _L1_ffn_in['w1'], 'L1_ffn_b1': _L1_ffn_in['b1'], 'L1_ffn_w2': _L1_ffn_in['w2'], 'L1_ffn_b2': _L1_ffn_in['b2']}

def reference(x, ctx_1024, condB_tau, fside_BxS2_0, L0_xcond_Wq, L0_xcond_bq, L0_xcond_Wk, L0_xcond_bk, L0_xcond_Wv, L0_xcond_bv, L0_xcond_Wo, L0_xcond_bo, L0_ffn_gate_w, L0_ffn_gate_b, L0_ffn_shared_wg, L0_ffn_shared_wu, L0_ffn_shared_wd, L0_ffn_experts_wg, L0_ffn_experts_wu, L0_ffn_experts_wd, L1_xcond_Wq, L1_xcond_bq, L1_xcond_Wk, L1_xcond_bk, L1_xcond_Wv, L1_xcond_bv, L1_xcond_Wo, L1_xcond_bo, L1_ffn_router_w, L1_ffn_w1, L1_ffn_b1, L1_ffn_w2, L1_ffn_b2):
    import jax
    import jax.numpy as jnp

    def _L0_xcond_ref(query, key, value, tau, delta, Wq, bq, Wk, bk, Wv, bv, Wo, bo):
        import jax, jax.numpy as jnp
        import numpy as np
        B, S, D, H = (2, 256, 128, 16)
        DK = D // H

        def _split_heads(x):
            b, s, _ = x.shape
            return x.reshape(b, s, H, DK).transpose(0, 2, 1, 3)
        q = _split_heads(query @ Wq.T + bq)
        k = _split_heads(key @ Wk.T + bk)
        v = _split_heads(value @ Wv.T + bv)
        scores = jnp.einsum('bhqd,bhkd->bhqk', q, k)
        scores = scores * tau[:, :, None, None] + delta[:, None, None, :]
        scores = scores / jnp.sqrt(jnp.asarray(DK, scores.dtype))
        p_attn = jax.nn.softmax(scores, axis=-1)
        x = jnp.einsum('bhqk,bhkd->bhqd', p_attn, v)
        x = x.transpose(0, 2, 1, 3).reshape(query.shape[0], -1, H * DK)
        return x @ Wo.T + bo

    def _L0_ffn_ref(x, gate_w, gate_b, shared_wg, shared_wu, shared_wd, experts_wg, experts_wu, experts_wd):
        import jax, jax.numpy as jnp
        import numpy as np
        B, S, D = (2, 256, 128)
        I = 64
        E = 16
        TOP_K = 2

        def _mlp(x, wg, wu, wd):
            return jnp.einsum('bsi,id->bsd', jax.nn.silu(x @ wg) * (x @ wu), wd)
        router_logits = jax.nn.sigmoid(x @ gate_w + gate_b)
        expert_values, expert_indices = jax.lax.top_k(router_logits, k=TOP_K)
        expert_values = expert_values / jnp.sum(expert_values, axis=-1, keepdims=True)
        hg = jnp.einsum('bsd,edi->bsei', x, experts_wg)
        hu = jnp.einsum('bsd,edi->bsei', x, experts_wu)
        all_outputs = jnp.einsum('bsei,eid->bsed', jax.nn.silu(hg) * hu, experts_wd)
        selected = jnp.take_along_axis(all_outputs, expert_indices[..., None], axis=2)
        expert_weighted = jnp.sum(expert_values[..., None] * selected, axis=2)
        return x + _mlp(x, shared_wg, shared_wu, shared_wd) + expert_weighted

    def _L1_xcond_ref(q, k, v, tau, delta, Wq, bq, Wk, bk, Wv, bv, Wo, bo):
        import jax, jax.numpy as jnp
        import numpy as np
        D_MODEL = 128
        N_HEADS = 16
        B, L, D = q.shape
        S = k.shape[1]
        H = N_HEADS
        E = D // H
        qh = (q @ Wq.T + bq).reshape(B, L, H, E)
        kh = (k @ Wk.T + bk).reshape(B, S, H, E)
        vh = (v @ Wv.T + bv).reshape(B, S, H, E)
        scale = 1.0 / np.sqrt(E).astype(np.float32)
        scores = jnp.einsum('blhe,bshe->bhls', qh, kh)
        scores = scores * tau[:, None, None, :] + delta[:, None, None, :]
        a = jax.nn.softmax(scale * scores, axis=-1)
        out = jnp.einsum('bhls,bshd->blhd', a, vh).reshape(B, L, D)
        return out @ Wo.T + bo

    def _L1_ffn_ref(x, router_w, w1, b1, w2, b2):
        import jax, jax.numpy as jnp
        import numpy as np
        DIM = 128
        NUM_EXPERTS = 8
        HIDDEN = 512
        CAP_FACTOR = 2.0
        B, S = (4, 256)
        Bz, Sz, Dz = x.shape
        E = router_w.shape[0]
        capacity = max(1, int(Sz * CAP_FACTOR / E) + 1)
        scores = jax.nn.softmax(jnp.einsum('bsd,ed->bse', x, router_w), axis=-1)
        scores_t = jnp.swapaxes(scores, 1, 2)
        gate_vals, sel_idx = jax.lax.top_k(scores_t, capacity)
        b_idx = jnp.arange(Bz)[:, None, None]
        tokens = x[b_idx, sel_idx]
        h = jnp.einsum('becd,edh->bech', tokens, w1) + b1[None, :, None, :]
        h = jax.nn.gelu(h, approximate=False)
        y = jnp.einsum('bech,ehd->becd', h, w2) + b2[None, :, None, :]
        gated = y * gate_vals[..., None]
        out = jnp.zeros_like(x).at[b_idx, sel_idx].add(gated)
        return out
    x = x + _L0_xcond_ref(_layernorm(x, axis=-1), ctx_1024, ctx_1024, condB_tau[:, None], fside_BxS2_0, L0_xcond_Wq, L0_xcond_bq, L0_xcond_Wk, L0_xcond_bk, L0_xcond_Wv, L0_xcond_bv, L0_xcond_Wo, L0_xcond_bo)
    x = x + _L0_ffn_ref(_layernorm(x, axis=-1), L0_ffn_gate_w, L0_ffn_gate_b, L0_ffn_shared_wg, L0_ffn_shared_wu, L0_ffn_shared_wd, L0_ffn_experts_wg, L0_ffn_experts_wu, L0_ffn_experts_wd)
    x = x + _L1_xcond_ref(_layernorm(x, axis=-1), ctx_1024, ctx_1024, condB_tau[:, None], fside_BxS2_0, L1_xcond_Wq, L1_xcond_bq, L1_xcond_Wk, L1_xcond_bk, L1_xcond_Wv, L1_xcond_bv, L1_xcond_Wo, L1_xcond_bo)
    x = x + _L1_ffn_ref(_layernorm(x, axis=-1), L1_ffn_router_w, L1_ffn_w1, L1_ffn_b1, L1_ffn_w2, L1_ffn_b2)
    return x

_drawn_inputs = setup_inputs


def setup_inputs(seed=0):
    import zlib

    import numpy as np

    out = dict(_drawn_inputs(seed))
    spreads = {'L0_ffn_gate_b': (0.0, 0.1),
     'L1_xcond_bq': (0.0, 0.8),
     'L1_xcond_bk': (0.0, 2.0),
     'L1_xcond_bv': (0.0, 0.1),
     'L1_xcond_bo': (0.0, 0.1)}
    factors = {'L0_xcond_bq': 15.93,
     'L0_xcond_bk': 64.0,
     'L0_xcond_bo': 2.949,
     'L1_ffn_b1': 21.786,
     'L1_ffn_b2': 8.0}
    for name, (base, spread) in spreads.items():
        noise = np.random.default_rng([zlib.crc32(name.encode()), seed]).standard_normal(out[name].shape)
        drawn = base * np.exp(spread * noise) if base else spread * noise
        out[name] = jnp.asarray(drawn.astype(out[name].dtype))
    for name, factor in factors.items():
        out[name] = (out[name] * factor).astype(out[name].dtype)
    return out
```

```python
from contextlib import ExitStack

import concourse.bass as bass
import numpy as np
from concourse import mybir

F32 = mybir.dt.float32
BF16 = mybir.dt.bfloat16
U32 = mybir.dt.uint32
I32 = mybir.dt.int32
ALU = mybir.AluOpType
ACT = mybir.ActivationFunctionType
AX = mybir.AxisListType

P = 128
B, S, D = 4, 256, 128
S2 = 64
H, DK = 16, 8
NL = 2
NH = 2
BH = B // NH
QT = S // P
TH = BH * QT
TOK = TH * P
NP = H // 2
PR = 2 * DK
PARTS = 3
KSTK = 6 * PR
KROWS = KSTK + PARTS
QPART = (0, 0, 0, 1, 1, 2)
KPART = (0, 1, 2, 0, 1, 0)
E0, I0 = 16, 64
NC0 = E0 * I0 // P
E1, HID = 8, 512
NJ = HID // P
CAP = max(1, int(S * 2.0 / E1) + 1)
SLOTS = E1 * CAP
NM = 5
MS = SLOTS // NM
assert MS * NM == SLOTS and MS <= P
EPS = 1e-5
ISQ = float(1.0 / np.sqrt(np.float32(DK)))
ATT_G = (0, 1, 4, 5)

C_BQ, C_BK, C_B1, C_B2, C_GW, C_RW = 0, 2, 4, 4 + E1 * NJ, 4 + E1 * NJ + E1, 4 + E1 * NJ + E1 + E0
C_N = C_RW + E1
R_BV, R_BO, R_GB, R_TAU = 0, 2 * D, 4 * D, 4 * D + E0
R_N = R_TAU + B
F_ID, F_MASK, F_SLOT, F_E0, F_S = 0, P, P + 2, P + 2 + CAP, P + 2 + CAP + E0
F_N = F_S + S


def build(nc, x, ctxT, wT, cols, rows, delta, wg, wu, wd, wds, w1, w2, fconst, selection, out):
    q_scratch = nc.dram_tensor("q_scratch", [NH, PARTS, P, TOK], BF16, kind="Internal").ap()
    k_scratch = nc.dram_tensor("k_scratch", [NL, PARTS, P, B * 2 * S2], BF16, kind="Internal").ap()
    x_tiles = x.rearrange("b (q p) d -> (b q) p d", p=P)
    out_tiles = out.rearrange("b (q p) d -> (b q) p d", p=P)

    with ExitStack() as ctx:
        def sb(name, shape, dt=F32):
            return ctx.enter_context(nc.sbuf_tensor(name, shape, dt))

        def sem(name):
            return ctx.enter_context(nc.semaphore(name))

        wT_sb = sb("wT_sb", [P, NL, 4, D])
        ctx_sb = sb("ctx_sb", [P, B, 2, S2])
        cols_sb = sb("cols_sb", [P, C_N])
        rows_sb = sb("rows_sb", [P, R_N])
        fc = sb("fc", [P, F_N])
        ident_b = sb("ident_b", [P, P], BF16)
        sel_b = sb("sel_b", [PARTS * H, NP * P], BF16)
        ones_b = sb("ones_b", [PARTS, TOK], BF16)
        wg_sb = sb("wg_sb", [P, E0 + 1, I0])
        wu_sb = sb("wu_sb", [P, E0 + 1, I0])
        wd_sb = sb("wd_sb", [P, NC0 + 1, D])
        w1_sb = sb("w1_sb", [P, E1, HID])
        w2_sb = sb("w2_sb", [P, E1, NJ, D])
        ident = fc[:, F_ID:F_ID + P]
        mask2 = fc[:, F_MASK:F_MASK + 2]
        iota_slot = fc[:, F_SLOT:F_SLOT + CAP]
        iota_e0 = fc[:, F_E0:F_E0 + E0]
        iota_s = fc[0:2 * E1, F_S:F_S + S]
        sel = sel_b[:].rearrange("r (j c) -> r j c", j=NP)
        xs = [sb(f"xs{h}", [P, TH, D]) for h in range(NH)]
        xn = [sb(f"xn{h}", [P, TH, D]) for h in range(NH)]
        xb = [sb(f"xb{h}", [P, TH, D]) for h in range(NH)]
        xnT = [sb(f"xnT{h}", [P, TOK]) for h in range(NH)]
        bn6 = sb("bn6", [P, TH, 6])
        mv = [sb(f"mv{h}", [P, TH, 2]) for h in range(NH)]
        veps = sb("veps", [P, TH])
        rstd = sb("rstd", [P, TH])
        rstd_t = sb("rstd_t", [P, TH])
        q_rest = sb("q_rest", [P, TOK])
        q_parts = [sb(f"q_parts{h}", [P, PARTS, TOK], BF16) for h in range(NH)]
        q_stack = [sb(f"q_stack{h}", [KROWS, NP, TOK], BF16) for h in range(NH)]
        tau_s = sb("tau_s", [P, B])
        k32 = sb("k32", [P, B, S2])
        k_part = sb("k_part", [P, PARTS, B, S2], BF16)
        k_rest = sb("k_rest", [P, B, S2])
        k_masked = [sb(f"k_masked{l}", [P, PARTS, B, 2, S2], BF16) for l in range(NL)]
        k_stack = [sb(f"k_stack{l}", [KROWS, NP, B, 2 * S2], BF16) for l in range(NL)]
        v_blk = [sb(f"v_blk{l}", [P, B, NP, 2, DK + 1]) for l in range(NL)]
        dl32 = sb("dl32", [1, B, S2])
        dl_rest = sb("dl_rest", [1, B, S2])
        dl_parts = sb("dl_parts", [1, PARTS, B, 2, S2], BF16)
        negmax = sb("negmax", [P, TH, H])
        nm_parts = [sb(f"nm_parts{i}", [P, QT, PARTS, H], BF16) for i in range(BH)]
        nm_rest = sb("nm_rest", [P, QT, H])
        nmT = [sb(f"nmT{i}", [PARTS * H, S], BF16) for i in range(BH)]
        probs_sb = sb("probs_sb", [P, BH, NP, S])
        probs = [probs_sb[:, i] for i in range(BH)]
        rsum = sb("rsum", [P, TH, H])
        att = sb("att", [P, TH, H, DK])
        attT = sb("attT", [P, TOK])
        lg = sb("lg", [P, TH, E0])
        th = sb("th", [P, TH, E0])
        sig = sb("sig", [P, TH, E0])
        top8 = sb("top8", [P, TH, 8])
        top_ix = sb("top_ix", [P, TH, 8], U32)
        top_ixf = sb("top_ixf", [P, TH, 8])
        vsum = sb("vsum", [P, TH])
        vrec = sb("vrec", [P, TH])
        vnorm = sb("vnorm", [P, TH, 2])
        pick = sb("pick", [P, TH, 2, E0])
        wgt = sb("wgt", [P, TH, E0])
        wgt_rest = sb("wgt_rest", [P, TH, E0])
        wgt_parts = sb("wgt_parts", [P, TH, PARTS, E0], BF16)
        wgtT = sb("wgtT", [PARTS * E0, TOK], BF16)
        sg = [sb(f"sg{i}", [P, TOK]) for i in range(2)]
        hid0 = [sb(f"hid0{h}", [P, NC0 + 1, TOK]) for h in range(NH)]
        rmax = sb("rmax", [P, TH])
        rdif = sb("rdif", [P, TH, E1])
        rexp = sb("rexp", [P, TH, E1])
        rtot = sb("rtot", [P, TH])
        rrec = sb("rrec", [P, TH])
        score = [sb(f"score{h}", [P, QT, BH, E1]) for h in range(NH)]
        sT = sb("sT", [BH * E1, S])
        work = sb("work", [BH * E1, S])
        m8 = sb("m8", [BH * E1, 8])
        m8ix = sb("m8ix", [BH * E1, 8], U32)
        m8ixf = sb("m8ixf", [BH * E1, 8])
        chosen = sb("chosen", [BH * E1, S])
        ones_s = sb("ones_s", [BH * E1, S])
        slot_n = sb("slot_n", [BH * E1, S])
        slot = sb("slot", [BH * E1, S])
        slotT = sb("slotT", [P, QT, BH, E1])
        W1H, W1X = QT * BH * SLOTS, BH * SLOTS
        free0 = hid0[0][:].rearrange("p c s -> p (c s)")
        free1 = hid0[1][:].rearrange("p c s -> p (c s)")
        sel32 = free0[0:PARTS * H, 0:NP * P]
        onehot = [free0[:, h * W1H:(h + 1) * W1H].rearrange("p (q b e c) -> p q b e c", q=QT, b=BH, e=E1)
                  for h in range(NH)]
        gated = free1[:, 0:W1H].rearrange("p (q b e c) -> p q b e c", q=QT, b=BH, e=E1)
        xsel = free1[:, W1H:W1H + W1X].rearrange("p (e b c) -> p e b c", e=E1, b=BH)
        yT = free1[:, W1H + W1X:W1H + 2 * W1X].rearrange("p (b e c) -> p b e c", b=BH, e=E1)
        free2 = probs_sb[0:MS].rearrange("p i j s -> p (i j s)")
        gatedT = free2[:, 0:TH * NM * P].rearrange("m (i s) -> m i s", s=P)
        y = free2[:, TH * NM * P:TH * NM * P + BH * NM * D].rearrange("m (i d) -> m i d", d=D)
        free3 = wg_sb[:].rearrange("p e i -> p (e i)")
        hid1 = [free3[:, i * NJ * BH * CAP:(i + 1) * NJ * BH * CAP].rearrange("p (j c) -> p j c", j=NJ) for i in range(2)]

        ps = ctx.enter_context(nc.psum_tensor("ps", [P, 8, 512], F32))
        ps7b = ps[:, 7, :].bitcast(BF16)

        ld_x = [sem(f"ld_x{h}") for h in range(NH)]
        ld_ctx = sem("ld_ctx")
        ld_wT = [sem(f"ld_wT{l}") for l in range(NL)]
        ld_cols = sem("ld_cols")
        ld_rows = sem("ld_rows")
        ld_fc = sem("ld_fc")
        ld_sel = sem("ld_sel")
        ld_delta = sem("ld_delta")
        ld_gu = sem("ld_gu")
        ld_down = sem("ld_down")
        ld_w1 = sem("ld_w1")
        ld_w2 = sem("ld_w2")
        q_hi_ready = sem("q_hi_ready")
        q_mid_ready = sem("q_mid_ready")
        q_lo_ready = sem("q_lo_ready")
        q_out = [sem(f"q_out{c}") for c in range(PARTS)]
        q_stacked = [sem(f"q_stacked{h}") for h in range(NH)]
        k_parts_ready = sem("k_parts_ready")
        k_out = [sem(f"k_out{c}") for c in range(PARTS)]
        k_stacked = [sem(f"k_stacked{l}") for l in range(NL)]
        delta_ready = sem("delta_ready")
        ones_ready = sem("ones_ready")
        ones_stacked = [sem(f"ones_stacked{h}") for h in range(NH)]
        bf16_ready = sem("bf16_ready")
        dve_step = sem("dve_step")
        pool_step = sem("pool_step")
        stats_ready = sem("stats_ready")
        xn_ready = sem("xn_ready")
        xb_ready = sem("xb_ready")
        xT_done = sem("xT_done")
        xnT_ready = sem("xnT_ready")
        x_ready = sem("x_ready")
        fill_done = sem("fill_done")
        kv_done = sem("kv_done")
        k32_ready = sem("k32_ready")
        v_ready = sem("v_ready")
        q_rest_ready = sem("q_rest_ready")
        q_done = sem("q_done")
        s1_done = sem("s1_done")
        max_ready = sem("max_ready")
        nm_ready = sem("nm_ready")
        nmT_done = sem("nmT_done")
        nmT_ready = sem("nmT_ready")
        s2_done = sem("s2_done")
        probs_ready = sem("probs_ready")
        av_done = sem("av_done")
        att_ready = sem("att_ready")
        attT_done = sem("attT_done")
        attT_ready = sem("attT_ready")
        wo_done = sem("wo_done")
        gate_done = sem("gate_done")
        gate_lg = sem("gate_lg")
        gate_th = sem("gate_th")
        wgt_ready = sem("wgt_ready")
        wgtT_done = sem("wgtT_done")
        wgtT_ready = sem("wgtT_ready")
        up0_done = sem("up0_done")
        wb_done = sem("wb_done")
        silu_ready = sem("silu_ready")
        gu_ready = sem("gu_ready")
        hid0_ready = sem("hid0_ready")
        down0_done = sem("down0_done")
        router_done = sem("router_done")
        rdif_ready = sem("rdif_ready")
        rexp_ready = sem("rexp_ready")
        score_ready = sem("score_ready")
        scoreT_done = sem("scoreT_done")
        sT_ready = sem("sT_ready")
        slot_ready = sem("slot_ready")
        slotT_done = sem("slotT_done")
        slotT_ready = sem("slotT_ready")
        onehot_ready = sem("onehot_ready")
        gated_ready = sem("gated_ready")
        gather_done = sem("gather_done")
        xsel_ready = sem("xsel_ready")
        gatedT_done = sem("gatedT_done")
        gatedT_ready = sem("gatedT_ready")
        up1_done = sem("up1_done")
        hid1_ready = sem("hid1_ready")
        down1_done = sem("down1_done")
        yT_ready = sem("yT_ready")
        yTT_done = sem("yTT_done")
        y_ready = sem("y_ready")
        scatter_done = sem("scatter_done")
        out_ready = sem("out_ready")
        stored = sem("stored")

        B01, B23, B4, B5, B6, B7 = range(6)

        block = ctx.enter_context(nc.Block())

        @block.sync
        def _(sp):
            def load_x(h):
                sp.dma_start(xs[h][:], x_tiles[TH * h:TH * h + TH].rearrange("t p d -> p t d")).then_inc(ld_x[h], 16)

            load_x(0)
            for e in range(2):
                sp.dma_start(ctx_sb[:, :, e, :], ctxT.rearrange("d (b k) -> d b k", b=B)).then_inc(ld_ctx, 16)
            sp.dma_start(fc[:], fconst).then_inc(ld_fc, 16)
            load_x(1)
            sp.dma_start(sel32, selection).then_inc(ld_sel, 16)

            def k_bounce(l):
                for c in range(PARTS):
                    sp.wait_ge(k_parts_ready, PARTS * l + c + 1)
                    sp.dma_start(k_scratch[l, c], k_masked[l][:, c].rearrange("p b e k -> p (b e k)")).then_inc(k_out[c], 16)
                for c in range(PARTS):
                    sp.wait_ge(k_out[c], 16 * (l + 1))
                    src = k_scratch[l, c].rearrange("(j r) n -> r j n", r=PR)
                    for i in range(len(KPART)):
                        if KPART[i] == c:
                            dst = k_stack[l][PR * i:PR * (i + 1)].rearrange("r j b n -> r j (b n)")
                            sp.dma_start(dst, src).then_inc(k_stacked[l], 16)

            def q_bounce(a):
                h = a % NH
                for c, ready in enumerate((q_hi_ready, q_mid_ready, q_lo_ready)):
                    sp.wait_ge(ready, a + 1)
                    sp.dma_start(q_scratch[h, c], q_parts[h][:, c, :]).then_inc(q_out[c], 16)
                for c in range(PARTS):
                    sp.wait_ge(q_out[c], 16 * (a + 1))
                    src = q_scratch[h, c].rearrange("(j r) n -> r j n", r=PR)
                    for i in range(len(QPART)):
                        if QPART[i] == c:
                            sp.dma_start(q_stack[h][PR * i:PR * (i + 1)], src).then_inc(q_stacked[h], 16)

            def ones_rows(h):
                src = ones_b[:, None, :].broadcast_to([PARTS, NP, TOK])
                sp.dma_start(q_stack[h][KSTK:KROWS], src).then_inc(ones_stacked[h], 16)

            def delta_rows(l):
                for c in range(PARTS):
                    src = dl_parts[0:1, c].rearrange("a b e k -> a (b e k)")[:, None, :].broadcast_to([1, NP, B * 2 * S2])
                    dst = k_stack[l][KSTK + c:KSTK + c + 1].rearrange("r j b n -> r j (b n)")
                    sp.dma_start(dst, src).then_inc(k_stacked[l], 16)
            sp.wait_ge(ones_ready, 1)
            ones_rows(0)
            sp.wait_ge(delta_ready, 1)
            delta_rows(0)
            k_bounce(0)
            q_bounce(0)
            ones_rows(1)
            q_bounce(1)
            delta_rows(1)
            k_bounce(1)
            q_bounce(2)
            q_bounce(3)
            for n in range(NH * TH):
                sp.wait_ge(out_ready, n + 1)
                sp.dma_start(out_tiles[n], xb[n // TH][:, n % TH, :]).then_inc(stored, 16)
            sp.wait_ge(stored, 16 * NH * TH)

        @block.gpsimd
        def _(pool):
            steps = [0]

            def link(ins):
                steps[0] += 1
                ins.then_inc(pool_step, 1)
                pool.wait_ge(pool_step, steps[0])

            pool.dma_start(dl32[:], delta.rearrange("b k -> (b k)").rearrange("(a b k) -> a b k", a=1, b=B)).then_inc(ld_delta, 16)
            pool.memset(ones_b[:], 1.0).then_inc(ones_ready, 1)
            pool.wait_ge(ones_ready, 1)
            pool.wait_ge(ld_delta, 16)
            link(pool.tensor_scalar(dl32[:], dl32[:], ISQ, None, ALU.mult))
            link(pool.tensor_copy(dl_parts[:, 0, :, 0, :], dl32[:]))
            pool.tensor_copy(dl_parts[:, 0, :, 1, :], dl_parts[:, 0, :, 0, :])
            link(pool.tensor_tensor(dl_rest[:], dl32[:], dl_parts[:, 0, :, 0, :], ALU.subtract))
            link(pool.tensor_copy(dl_parts[:, 1, :, 0, :], dl_rest[:]))
            pool.tensor_copy(dl_parts[:, 1, :, 1, :], dl_parts[:, 1, :, 0, :])
            link(pool.tensor_tensor(dl_rest[:], dl_rest[:], dl_parts[:, 1, :, 0, :], ALU.subtract))
            pool.tensor_copy(dl_parts[:, 2, :, 0, :], dl_rest[:])
            pool.tensor_copy(dl_parts[:, 2, :, 1, :], dl_rest[:]).then_inc(delta_ready, 1)
            link(pool.memset(ones_s[:], 1.0))
            for l in range(NL):
                link(pool.memset(v_blk[l][:], 0.0))
                link(pool.memset(v_blk[l][0:S2, :, :, 0, DK:DK + 1], 1.0))
                pool.memset(v_blk[l][S2:2 * S2, :, :, 1, DK:DK + 1], 1.0).then_inc(fill_done, 1)
                pool.wait_ge(fill_done, l + 1)
            def residual_base(g):
                h = g % NH
                if g in ATT_G:
                    l = ATT_G.index(g) // NH
                    bo = rows_sb[:, R_BO + l * D:R_BO + (l + 1) * D][:, None, :].broadcast_to([P, TH, D])
                    if g < NH:
                        pool.wait_ge(ld_x[h], 16)
                        pool.wait_ge(ld_rows, 16)
                    else:
                        pool.wait_ge(x_ready, g - 1)
                    pool.tensor_tensor(xb[h][:], xs[h][:], bo, ALU.add).then_inc(xb_ready, 1)
                elif g < 6:
                    pool.wait_ge(xn_ready, TH * (g + 1))
                    pool.tensor_tensor(xb[h][:], xs[h][:], xn[h][:], ALU.add).then_inc(xb_ready, 1)

            def gate_onehot(f):
                pool.wait_ge(onehot_ready, f + 1)
                if f:
                    pool.wait_ge(gatedT_done, 5 * f)
                sc = score[f][:].rearrange("p q b e -> p (q b e)")[:, :, None].broadcast_to([P, TH * E1, CAP])
                pool.tensor_tensor(gated[:].rearrange("p q b e c -> p (q b e) c"),
                                   onehot[f][:].rearrange("p q b e c -> p (q b e) c"), sc, ALU.mult).then_inc(gated_ready, 1)

            for g in range(6):
                residual_base(g)
            gate_onehot(0)
            gate_onehot(1)

        @block.scalar
        def _(act):
            act.dma_start(wT_sb[:, 0], wT[:, 0]).then_inc(ld_wT[0], 16)
            act.dma_start(cols_sb[:], cols).then_inc(ld_cols, 16)
            act.dma_start(rows_sb[:], rows.partition_broadcast(P)).then_inc(ld_rows, 16)

            def xnT_copy(g):
                act.wait_ge(xT_done, g + 1)
                act.activation(xnT[g % NH][:], ps[:, 7, :], ACT.Copy).then_inc(xnT_ready, 1)

            def q_hi(a):
                l, h = a // NH, a % NH
                act.wait_ge(q_done, a + 1)
                if a == 0:
                    act.wait_ge(ld_cols, 16)
                act.activation(q_parts[h][:, 0, :], ps[:, 7, :], ACT.Identity,
                               bias=cols_sb[:, C_BQ + l:C_BQ + l + 1]).then_inc(q_hi_ready, 1)

            def nmT_copy(a, bl):
                act.wait_ge(nmT_done, BH * a + bl + 1)
                act.activation(nmT[bl][:], ps7b[0:PARTS * H, 0:S], ACT.Copy).then_inc(nmT_ready, 1)

            def softmax_exp(a, bl):
                if a:
                    act.wait_ge(av_done, TH * (a - 1) + QT * (bl + 1))
                for n in range(NP // 2):
                    act.wait_ge(s2_done, (NP // 2) * (BH * a + bl) + n + 1)
                    act.activation(probs[bl][:, 2 * n:2 * n + 2, :],
                                   ps[:, 4 + n % 2, :].rearrange("p (j s) -> p j s", j=2),
                                   ACT.Exp).then_inc(probs_ready, 1)

            def attT_copy(a):
                act.wait_ge(attT_done, a + 1)
                act.activation(attT[:], ps[:, 6, :], ACT.Copy).then_inc(attT_ready, 1)

            def gate_tanh(f):
                act.wait_ge(gate_lg, f + 1)
                act.activation(th[:], lg[:], ACT.Tanh, scale=0.5).then_inc(gate_th, 1)

            def wgtT_copy(f):
                act.wait_ge(wgtT_done, f + 1)
                act.activation(wgtT[:], ps7b[0:PARTS * E0, 0:TOK], ACT.Copy).then_inc(wgtT_ready, 1)

            def silu(n):
                c = (NC0, *range(NC0))[n % (NC0 + 1)]
                m = I0 if c == NC0 else P
                act.wait_ge(up0_done, n + 1)
                f, i = divmod(n - 2, NC0 + 1)
                if n > 2:
                    act.wait_ge(hid0_ready, NC0 * f + i)
                act.activation(sg[n % 2][0:m, :], ps[0:m, 2 * (n % 2), :], ACT.Silu).then_inc(silu_ready, 1)

            def router_exp(f):
                act.wait_ge(rdif_ready, f + 1)
                act.activation(rexp[:], rdif[:], ACT.Exp).then_inc(rexp_ready, 1)

            def gelu(f, e):
                u = e % 2
                act.wait_ge(up1_done, E1 * f + e + 1)
                for j in range(NJ):
                    src = ps[:, 2 * u + j // 2, (j % 2) * BH * CAP:(j % 2 + 1) * BH * CAP]
                    ins = act.activation(hid1[u][:, j, :], src, ACT.Gelu,
                                         bias=cols_sb[:, C_B1 + NJ * e + j:C_B1 + NJ * e + j + 1])
                ins.then_inc(hid1_ready, 1)

            def gatedT_copy(f, n):
                act.wait_ge(gatedT_done, 5 * f + n + 1)
                act.activation(gatedT[:, 4 * n:4 * n + 4, :], ps[0:MS, 6 + n % 2, :].rearrange("m (i s) -> m i s", i=4),
                               ACT.Copy).then_inc(gatedT_ready, 1)

            def xsel_copy(f):
                for bl in range(BH):
                    for k in range(2):
                        act.wait_ge(gather_done, 2 * (BH * f + bl) + k + 1)
                        src = ps[:, 2 * bl + k, 0:4 * CAP].rearrange("p (e c) -> p e c", e=4)
                        ins = act.activation(xsel[:, 4 * k:4 * k + 4, bl, :], src, ACT.Copy)
                    ins.then_inc(xsel_ready, 1)

            def attention(a, before_exp=(), hook=(), hook_late=()):
                for step in before_exp:
                    step()
                nmT_copy(a, 0)
                softmax_exp(a, 0)
                nmT_copy(a, 1)
                for step in hook:
                    step()
                softmax_exp(a, 1)
                for step in hook_late:
                    step()

            def experts1(f, hooks):
                for n in range(5):
                    gatedT_copy(f, n)
                for e in range(E1):
                    gelu(f, e)
                    for step in hooks.get(e, ()):
                        step()

            xnT_copy(0)
            q_hi(0)
            xnT_copy(1)
            q_hi(1)
            act.dma_start(wT_sb[:, 1], wT[:, 1]).then_inc(ld_wT[1], 16)
            act.dma_start(wg_sb[:], wg).then_inc(ld_gu, 16)
            act.dma_start(wu_sb[:], wu).then_inc(ld_gu, 16)
            act.wait_ge(ld_sel, 16)
            act.activation(sel_b[:], sel32, ACT.Copy).then_inc(bf16_ready, 1)
            act.wait_ge(ld_fc, 16)
            act.activation(ident_b[:], ident, ACT.Copy).then_inc(bf16_ready, 1)
            attention(0)
            act.dma_start(wd_sb[:, 0:NC0], wd).then_inc(ld_down, 16)
            act.dma_start(wd_sb[0:I0, NC0], wds).then_inc(ld_down, 16)
            act.dma_start(w1_sb[:], w1).then_inc(ld_w1, 16)
            act.dma_start(w2_sb[:], w2).then_inc(ld_w2, 16)
            attention(1, before_exp=[lambda: attT_copy(0)], hook_late=[lambda: xnT_copy(2), lambda: gate_tanh(0)])
            silu(0)
            attT_copy(1)
            wgtT_copy(0)
            for n in range(1, NC0 + 1):
                silu(n)
                if n == 4:
                    xnT_copy(3)
                    gate_tanh(1)
            silu(NC0 + 1)
            wgtT_copy(1)
            for n in range(1, NC0 + 1):
                silu(NC0 + 1 + n)
                if n == 5:
                    xnT_copy(4)
                    q_hi(2)
            attention(2, hook_late=[lambda: xnT_copy(5), lambda: q_hi(3)])
            attention(3, before_exp=[lambda: attT_copy(2)], hook_late=[lambda: xnT_copy(6), lambda: router_exp(0)])
            attT_copy(3)
            xsel_copy(0)
            experts1(0, {1: [lambda: xnT_copy(7), lambda: router_exp(1)]})
            xsel_copy(1)
            experts1(1, {})

        @block.vector
        def _(dve):
            steps = [0]

            def mark(ins):
                steps[0] += 1
                ins.then_inc(dve_step, 1)

            def settle():
                dve.wait_ge(dve_step, steps[0])

            def link(ins):
                mark(ins)
                settle()

            def stats(g):
                h = g % NH
                if g < NH:
                    dve.wait_ge(ld_x[h], 16)
                else:
                    dve.wait_ge(x_ready, g - 1)
                if g:
                    dve.wait_ge(stats_ready, g)
                for t in range(TH):
                    mark(dve.bn_stats(bn6[:, t, :], xs[h][:, t, :]))
                settle()
                for t in range(TH):
                    ins = dve.bn_aggr(mv[h][:, t, :], bn6[:, t, :])
                ins.then_inc(stats_ready, 1)

            def normalise(g):
                h = g % NH
                dve.wait_ge(stats_ready, g + 1)
                if g:
                    dve.wait_ge(xn_ready, TH * g)
                link(dve.tensor_scalar(veps[:], mv[h][:, :, 1], EPS, None, ALU.add))
                link(dve.tensor_scalar(rstd_t[:].bitcast(I32), veps[:].bitcast(I32), 1, None, ALU.arith_shift_right))
                link(dve.tensor_scalar(rstd[:].bitcast(I32), rstd_t[:].bitcast(I32), -1.0, float(0x5F3759DF), ALU.mult, ALU.add))
                for _ in range(3):
                    link(dve.scalar_tensor_tensor(rstd_t[:], rstd[:], -0.5, veps[:], ALU.mult, ALU.mult))
                    link(dve.tensor_tensor(rstd_t[:], rstd_t[:], rstd[:], ALU.mult))
                    link(dve.scalar_tensor_tensor(rstd[:], rstd_t[:], 1.5, rstd[:], ALU.add, ALU.mult))
                for t in range(TH):
                    dve.tensor_scalar(xn[h][:, t, :], xs[h][:, t, :], mv[h][:, t, 0:1], rstd[:, t:t + 1],
                                      ALU.subtract, ALU.mult).then_inc(xn_ready, 1)

            def k_prep(l):
                dve.wait_ge(kv_done, 2 * l + 1)
                if l == 0:
                    dve.wait_ge(ld_rows, 16)
                    dve.wait_ge(ld_cols, 16)
                    dve.wait_ge(ld_fc, 16)
                    link(dve.tensor_scalar(tau_s[:], rows_sb[:, R_TAU:R_TAU + B], ISQ, None, ALU.mult))
                if l:
                    dve.wait_ge(k_parts_ready, PARTS * l)
                for b in range(B):
                    ins = dve.tensor_scalar(k32[:, b, :], ps[:, 4, b * S2:(b + 1) * S2],
                                            cols_sb[:, C_BK + l:C_BK + l + 1], tau_s[:, b:b + 1], ALU.add, ALU.mult)
                    if b == B - 1:
                        ins.then_inc(k32_ready, 1)
                    else:
                        mark(ins)
                dve.wait_ge(k32_ready, l + 1)
                settle()
                rest = k32
                for c in range(PARTS):
                    link(dve.tensor_copy(k_part[:, c], rest[:]))
                    for e in range(2):
                        ins = dve.tensor_scalar(k_masked[l][:, c, :, e, :], k_part[:, c], mask2[:, e:e + 1], None, ALU.mult)
                    ins.then_inc(k_parts_ready, 1)
                    if c < PARTS - 1:
                        link(dve.tensor_tensor(k_rest[:], rest[:], k_part[:, c], ALU.subtract))
                        rest = k_rest

            def v_prep(l):
                dve.wait_ge(kv_done, 2 * l + 2)
                dve.wait_ge(fill_done, l + 1)
                v_ps = ps[:, 5, :].rearrange("p (b j e d) -> p b j e d", b=B, j=NP, e=2)
                bv = rows_sb[:, R_BV + l * D:R_BV + (l + 1) * D].rearrange("p (j e d) -> p j e d", j=NP, e=2)
                for e in range(2):
                    r = slice(S2 * e, S2 * (e + 1))
                    ins = dve.tensor_tensor(v_blk[l][r, :, :, e, 0:DK], v_ps[r, :, :, e, :],
                                            bv[r, :, e, :][:, None, :, :].broadcast_to([S2, B, NP, DK]), ALU.add)
                    ins.then_inc(v_ready, 1)

            def q_split(a):
                l, h = a // NH, a % NH
                dve.wait_ge(q_hi_ready, a + 1)
                if a:
                    dve.wait_ge(q_lo_ready, a)
                dve.scalar_tensor_tensor(q_rest[:], ps[:, 7, :], cols_sb[:, C_BQ + l:C_BQ + l + 1], q_parts[h][:, 0, :],
                                         ALU.add, ALU.subtract).then_inc(q_rest_ready, 1)
                dve.wait_ge(q_rest_ready, a + 1)
                dve.tensor_copy(q_parts[h][:, 1, :], q_rest[:]).then_inc(q_mid_ready, 1)
                dve.wait_ge(q_mid_ready, a + 1)
                dve.tensor_tensor(q_parts[h][:, 2, :], q_rest[:], q_parts[h][:, 1, :], ALU.subtract).then_inc(q_lo_ready, 1)

            def score_max(t_all):
                t = t_all % TH
                u = t_all % 2
                dve.wait_ge(s1_done, t_all + 1)
                dve.tensor_reduce(negmax[:, t, :], ps[:, 2 * u:2 * u + 2, :].rearrange("p n (e k) -> p (n e) k", k=S2),
                                  AX.X, ALU.max, negate=True).then_inc(max_ready, 1)

            def max_parts(a, bl):
                nm = negmax[:, QT * bl:QT * bl + QT, :]
                dve.wait_ge(max_ready, TH * a + QT * (bl + 1))
                parts = nm_parts[bl]
                if a or bl:
                    dve.wait_ge(nm_ready, BH * a + bl)
                link(dve.tensor_copy(parts[:, :, 0, :], nm))
                link(dve.tensor_tensor(nm_rest[:], nm, parts[:, :, 0, :], ALU.subtract))
                link(dve.tensor_copy(parts[:, :, 1, :], nm_rest[:]))
                dve.tensor_tensor(parts[:, :, 2, :], nm_rest[:], parts[:, :, 1, :], ALU.subtract).then_inc(nm_ready, 1)

            def normalise_att(t_all):
                t = t_all % TH
                u = t % 2
                dve.wait_ge(av_done, t_all + 1)
                av = ps[:, 2 * u + t // 2, 0:H * (DK + 1)].rearrange("p (e d) -> p e d", d=DK + 1)
                if t_all >= TH:
                    dve.wait_ge(att_ready, t_all - TH + 1)
                link(dve.reciprocal(rsum[:, t], av[:, :, DK]))
                dve.tensor_tensor(att[:, t], av[:, :, 0:DK], rsum[:, t][:, :, None].broadcast_to([P, H, DK]),
                                  ALU.mult).then_inc(att_ready, 1)

            def residual(g):
                h = g % NH
                if g in ATT_G:
                    dve.wait_ge(wo_done, ATT_G.index(g) + 1)
                else:
                    dve.wait_ge(down0_done, g - 1)
                dve.wait_ge(xb_ready, g + 1)
                dve.tensor_tensor(xs[h][:], ps[:, 6, :].rearrange("p (t d) -> p t d", t=TH), xb[h][:],
                                  ALU.add).then_inc(x_ready, 1)

            def gate_logits(f):
                dve.wait_ge(gate_done, f + 1)
                gb = rows_sb[:, R_GB:R_GB + E0][:, None, :].broadcast_to([P, TH, E0])
                dve.tensor_tensor(lg[:], ps[:, 7, 0:TH * E0].rearrange("p (t e) -> p t e", t=TH), gb,
                                  ALU.add).then_inc(gate_lg, 1)

            def route(f):
                dve.wait_ge(gate_th, f + 1)
                if f:
                    dve.wait_ge(wgt_ready, f)
                link(dve.tensor_scalar(sig[:], th[:], 0.5, 0.5, ALU.mult, ALU.add))
                for t in range(TH):
                    mark(dve.max(top8[:, t, :], sig[:, t, :]))
                settle()
                for t in range(TH):
                    mark(dve.max_index(top_ix[:, t, :], top8[:, t, :], sig[:, t, :]))
                link(dve.tensor_tensor(vsum[:], top8[:, :, 0], top8[:, :, 1], ALU.add))
                mark(dve.tensor_copy(top_ixf[:], top_ix[:]))
                link(dve.reciprocal(vrec[:], vsum[:]))
                mark(dve.tensor_tensor(vnorm[:], top8[:, :, 0:2], vrec[:][:, :, None].broadcast_to([P, TH, 2]), ALU.mult))
                link(dve.tensor_tensor(pick[:], iota_e0[:, None, None, :].broadcast_to([P, TH, 2, E0]),
                                       top_ixf[:, :, 0:2][:, :, :, None].broadcast_to([P, TH, 2, E0]), ALU.is_equal))
                link(dve.tensor_tensor(pick[:], pick[:], vnorm[:][:, :, :, None].broadcast_to([P, TH, 2, E0]), ALU.mult))
                link(dve.tensor_tensor(wgt[:], pick[:, :, 0, :], pick[:, :, 1, :], ALU.add))
                link(dve.tensor_copy(wgt_parts[:, :, 0, :], wgt[:]))
                link(dve.tensor_tensor(wgt_rest[:], wgt[:], wgt_parts[:, :, 0, :], ALU.subtract))
                link(dve.tensor_copy(wgt_parts[:, :, 1, :], wgt_rest[:]))
                dve.tensor_tensor(wgt_parts[:, :, 2, :], wgt_rest[:], wgt_parts[:, :, 1, :],
                                  ALU.subtract).then_inc(wgt_ready, 1)

            def hidden0(n):
                f, i = divmod(n, NC0 + 1)
                c = (NC0, *range(NC0))[i]
                u = n % 2
                dve.wait_ge(silu_ready, n + 1)
                if c == NC0:
                    dve.tensor_tensor(hid0[f][0:I0, c, :], sg[u][0:I0, :], ps[0:I0, 2 * u + 1, :],
                                      ALU.mult).then_inc(gu_ready, 1)
                    return
                dve.tensor_tensor(sg[u][:], sg[u][:], ps[:, 2 * u + 1, :], ALU.mult).then_inc(gu_ready, 1)
                dve.wait_ge(wb_done, NC0 * f + c + 1)
                dve.wait_ge(gu_ready, n + 1)
                dve.tensor_tensor(hid0[f][:, c, :], sg[u][:], ps[:, 4 + c % 2, :], ALU.mult).then_inc(hid0_ready, 1)

            def router_softmax(f):
                dve.wait_ge(router_done, f + 1)
                r = ps[:, 7, 0:TH * E1].rearrange("p (t e) -> p t e", t=TH)
                if f:
                    dve.wait_ge(rexp_ready, f)
                link(dve.tensor_reduce(rmax[:], r, AX.X, ALU.max))
                dve.tensor_tensor(rdif[:], r, rmax[:][:, :, None].broadcast_to([P, TH, E1]),
                                  ALU.subtract).then_inc(rdif_ready, 1)

            def router_scores(f):
                dve.wait_ge(rexp_ready, f + 1)
                if f:
                    dve.wait_ge(score_ready, f)
                link(dve.tensor_reduce(rtot[:], rexp[:], AX.X, ALU.add))
                link(dve.reciprocal(rrec[:], rtot[:]))
                dve.tensor_tensor(score[f][:].rearrange("p q b e -> p b q e"),
                                  rexp[:].rearrange("p (b q) e -> p b q e", b=BH),
                                  rrec[:].rearrange("p (b q) -> p b q", b=BH)[:, :, :, None].broadcast_to([P, BH, QT, E1]),
                                  ALU.mult).then_inc(score_ready, 1)

            def choose(f):
                dve.wait_ge(scoreT_done, f + 1)
                if f:
                    dve.wait_ge(slot_ready, f)
                dve.tensor_copy(sT[:], ps[0:BH * E1, 7, 0:S]).then_inc(sT_ready, 1)
                dve.wait_ge(sT_ready, f + 1)
                cur = sT
                for _ in range(CAP // 8):
                    link(dve.max(m8[:], cur[:]))
                    link(dve.match_replace(work[:], m8[:], cur[:], -1.0))
                    cur = work
                assert CAP % 8 == 1
                link(dve.max(m8[:], work[:]))
                link(dve.max_index(m8ix[:], m8[:], work[:]))
                link(dve.tensor_copy(m8ixf[:], m8ix[:]))
                link(dve.tensor_scalar(chosen[:], iota_s, m8ixf[:, 0:1], None, ALU.is_equal))
                link(dve.scalar_tensor_tensor(chosen[:], work[:], -1.0, chosen[:], ALU.is_equal, ALU.add))
                link(dve.tensor_tensor_scan(slot_n[:], ones_s[:], chosen[:], 0.0, ALU.mult, ALU.add))
                dve.tensor_tensor(slot[:], slot_n[:], chosen[:], ALU.mult).then_inc(slot_ready, 1)

            def make_onehot(f):
                dve.wait_ge(slotT_done, f + 1)
                if f:
                    dve.wait_ge(onehot_ready, f)
                dve.tensor_copy(slotT[:].rearrange("p q b e -> p (q b e)"), ps[:, 7, 0:TH * E1]).then_inc(slotT_ready, 1)
                dve.wait_ge(slotT_ready, f + 1)
                dve.tensor_tensor(onehot[f][:].rearrange("p q b e c -> p (q b e) c"),
                                  iota_slot[:, None, :].broadcast_to([P, TH * E1, CAP]),
                                  slotT[:].rearrange("p q b e -> p (q b e)")[:, :, None].broadcast_to([P, TH * E1, CAP]),
                                  ALU.is_equal).then_inc(onehot_ready, 1)

            def y_bias(f, e):
                dve.wait_ge(down1_done, E1 * f + e + 1)
                if f and e == 0:
                    dve.wait_ge(yTT_done, 2 * f)
                src = ps[:, 4 + e % 2, 0:BH * CAP].rearrange("p (b c) -> p b c", b=BH)
                dve.tensor_scalar(yT[:, :, e, :], src, cols_sb[:, C_B2 + e:C_B2 + e + 1], None,
                                  ALU.add).then_inc(yT_ready, 1)

            def y_copy(f):
                for u, n in ((0, 8), (1, 2)):
                    dve.wait_ge(yTT_done, 2 * f + u + 1)
                    src = ps[0:MS, 2 * u:2 * u + 2, :].rearrange("m n (i d) -> m (n i) d", d=D)[:, 0:n, :]
                    dve.tensor_copy(y[:, 8 * u:8 * u + n, :], src).then_inc(y_ready, 1)

            def finish(f):
                for t in range(TH):
                    dve.wait_ge(scatter_done, TH * f + t + 1)
                    dve.tensor_tensor(xb[f][:, t, :], ps[:, 4 + t, 0:D], xs[f][:, t, :], ALU.add).then_inc(out_ready, 1)

            def attention(a, after_scores=(), before_values=(), after_values=()):
                for bl in range(BH):
                    for qt in range(QT):
                        score_max(TH * a + QT * bl + qt)
                    max_parts(a, bl)
                for step in after_scores:
                    step()
                for t in range(2):
                    normalise_att(TH * a + t)
                for step in before_values:
                    step()
                for t in range(2, TH):
                    normalise_att(TH * a + t)
                for step in after_values:
                    step()

            stats(0)
            normalise(0)
            k_prep(0)
            q_split(0)
            stats(1)
            normalise(1)
            v_prep(0)
            q_split(1)
            attention(0)
            attention(1, after_scores=[lambda: residual(0), lambda: stats(2), lambda: normalise(2)], before_values=[lambda: gate_logits(0)])
            route(0)
            hidden0(0)
            residual(1)
            stats(3)
            normalise(3)
            k_prep(1)
            v_prep(1)
            for n in range(1, NC0 + 1):
                hidden0(n)
                if n == 4:
                    gate_logits(1)
                    route(1)
            hidden0(NC0 + 1)
            residual(2)
            stats(4)
            normalise(4)
            for n in range(1, NC0 + 1):
                hidden0(NC0 + 1 + n)
                if n == 5:
                    q_split(2)
            residual(3)
            stats(5)
            normalise(5)
            attention(2, before_values=[lambda: q_split(3)])
            attention(3, after_scores=[lambda: residual(4), lambda: stats(6), lambda: normalise(6)],
                      before_values=[lambda: router_softmax(0)])
            router_scores(0)
            residual(5)
            stats(7)
            normalise(7)
            choose(0)
            make_onehot(0)
            for e in range(E1):
                y_bias(0, e)
                if e == 1:
                    router_softmax(1)
                if e == 2:
                    router_scores(1)
                    choose(1)
                if e == 5:
                    make_onehot(1)
            y_copy(0)
            finish(0)
            for e in range(E1):
                y_bias(1, e)
            y_copy(1)
            finish(1)

        @block.tensor
        def _(pe):
            reader = {}

            def claim(banks, read, count):
                if banks in reader:
                    pe.wait_ge(*reader[banks])
                reader[banks] = read, count

            def turn_x(g):
                h = g % NH
                claim(B7, xnT_ready, g + 1)
                if g == 0:
                    pe.wait_ge(ld_fc, 16)
                for t in range(TH):
                    pe.wait_ge(xn_ready, TH * g + t + 1)
                    ins = pe.transpose(ps[:, 7, t * P:(t + 1) * P], xn[h][:, t, :], ident)
                ins.then_inc(xT_done, 1)

            def project_q(a):
                l, h = a // NH, a % NH
                claim(B7, q_rest_ready, a + 1)
                if h == 0:
                    pe.wait_ge(ld_wT[l], 16)
                pe.matmul(ps[:, 7, :], wT_sb[:, l, 0, :], xnT[h][:], start=True, stop=True).then_inc(q_done, 1)

            def project_kv(l):
                if l == 0:
                    pe.wait_ge(ld_ctx, 32)
                    pe.wait_ge(ld_wT[0], 16)
                else:
                    pe.wait_ge(ld_wT[1], 16)
                claim(B4, k32_ready, l + 1)
                pe.matmul(ps[:, 4, 0:B * S2].rearrange("p (b k) -> p b k", b=B), wT_sb[:, l, 1, :], ctx_sb[:, :, 0, :],
                          start=True, stop=True).then_inc(kv_done, 1)
                claim(B5, v_ready, 2 * (l + 1))
                for b in range(B):
                    ins = pe.matmul(ps[:, 5, b * D:(b + 1) * D], ctx_sb[:, b].rearrange("d e k -> d (e k)"), wT_sb[:, l, 2, :], start=True, stop=True)
                ins.then_inc(kv_done, 1)

            def scores(a, t):
                l, h, b = a // NH, a % NH, BH * (a % NH) + t // QT
                u = t % 2
                claim(B01 + u, max_ready, TH * a + t + 1)
                if t == 0:
                    pe.wait_ge(q_stacked[h], 16 * 6 * (l + 1))
                    if l == 0:
                        pe.wait_ge(ones_stacked[h], 16)
                    if h == 0:
                        pe.wait_ge(k_stacked[l], 16 * (6 + PARTS))
                for j in range(NP):
                    ins = pe.matmul(ps[:, 2 * u + j // 4, (j % 4) * P:(j % 4 + 1) * P],
                                    q_stack[h][:, j, t * P:(t + 1) * P], k_stack[l][:, j, b, :], start=True, stop=True)
                ins.then_inc(s1_done, 1)

            def turn_max(a, bl):
                claim(B7, nmT_ready, BH * a + bl + 1)
                pe.wait_ge(nm_ready, BH * a + bl + 1)
                if a == 0 and bl == 0:
                    pe.wait_ge(bf16_ready, 2)
                for qt in range(QT):
                    ins = pe.transpose(ps7b[0:PARTS * H, qt * P:(qt + 1) * P],
                                       nm_parts[bl][:, qt].rearrange("p c e -> p (c e)"), ident_b[:])
                ins.then_inc(nmT_done, 1)

            def scores_T(a, bl, n):
                l, h, b = a // NH, a % NH, BH * (a % NH) + bl
                claim(B4 + n % 2, probs_ready, (NP // 2) * (BH * a + bl) + n + 1)
                if n == 0:
                    pe.wait_ge(nmT_ready, BH * a + bl + 1)
                for i in range(2):
                    j = 2 * n + i
                    dst = ps[:, 4 + n % 2, i * S:(i + 1) * S]
                    pe.matmul(dst, k_stack[l][:, j, b, :], q_stack[h][:, j, bl * S:(bl + 1) * S], start=True, stop=False)
                    ins = pe.matmul(dst, sel[:, j, :], nmT[bl][:], start=False, stop=True)
                ins.then_inc(s2_done, 1)

            def values(a, t):
                l, b, bl, qt = a // NH, BH * (a % NH) + t // QT, t // QT, t % QT
                u = t % 2
                claim(B01 + u, att_ready, TH * a + t + 1)
                if t == 0 and a % NH == 0:
                    pe.wait_ge(v_ready, 2 * (l + 1))
                if qt == 0:
                    pe.wait_ge(probs_ready, (NP // 2) * (BH * a + bl + 1))
                for j in range(NP):
                    ins = pe.matmul(ps[:, 2 * u + t // 2, j * 2 * (DK + 1):(j + 1) * 2 * (DK + 1)],
                                    probs[bl][:, j, qt * P:(qt + 1) * P],
                                    v_blk[l][:, b, j].rearrange("p e d -> p (e d)"), start=True, stop=True)
                ins.then_inc(av_done, 1)

            def project_out(a):
                l = a // NH
                claim(B6, attT_ready, a + 1)
                pe.wait_ge(att_ready, TH * (a + 1))
                for t in range(TH):
                    ins = pe.transpose(ps[:, 6, t * P:(t + 1) * P], att[:, t].rearrange("p e d -> p (e d)"), ident)
                ins.then_inc(attT_done, 1)
                claim(B6, x_ready, ATT_G[a] + 1)
                for t in range(TH):
                    ins = pe.matmul(ps[:, 6, t * D:(t + 1) * D], attT[:, t * P:(t + 1) * P], wT_sb[:, l, 3, :],
                                    start=True, stop=True)
                ins.then_inc(wo_done, 1)

            def attention(a, after_scores=(), before_values=()):
                for t in range(TH):
                    scores(a, t)
                for step in after_scores:
                    step()
                turn_max(a, 0)
                for n in range(4):
                    scores_T(a, 0, n)
                turn_max(a, 1)
                values(a, 0)
                scores_T(a, 1, 0)
                scores_T(a, 1, 1)
                values(a, 1)
                scores_T(a, 1, 2)
                scores_T(a, 1, 3)
                for step in before_values:
                    step()
                values(a, 2)
                values(a, 3)

            def gate(f):
                claim(B7, gate_lg, f + 1)
                for t in range(TH):
                    ins = pe.matmul(ps[:, 7, t * E0:(t + 1) * E0], xnT[f][:, t * P:(t + 1) * P],
                                    cols_sb[:, C_GW:C_GW + E0], start=True, stop=True)
                ins.then_inc(gate_done, 1)

            def turn_weights(f):
                pe.wait_ge(wgt_ready, f + 1)
                claim(B7, wgtT_ready, f + 1)
                for t in range(TH):
                    ins = pe.transpose(ps7b[0:PARTS * E0, t * P:(t + 1) * P],
                                       wgt_parts[:, t].rearrange("p c e -> p (c e)"), ident_b[:])
                ins.then_inc(wgtT_done, 1)

            def up0(n):
                f, i = divmod(n, NC0 + 1)
                c = (NC0, *range(NC0))[i]
                u = n % 2
                m = I0 if c == NC0 else P
                e = slice(2 * c, 2 * c + m // I0)
                if n == 0:
                    pe.wait_ge(ld_gu, 32)
                claim(B01 + u, gu_ready, n + 1)
                for k, w in enumerate((wg_sb, wu_sb)):
                    ins = pe.matmul(ps[0:m, 2 * u + k, :], w[:, e, :].rearrange("d e i -> d (e i)"), xnT[f][:],
                                    start=True, stop=True)
                ins.then_inc(up0_done, 1)
                if c < NC0:
                    claim(B4 + c % 2, hid0_ready, NC0 * f + c + 1)
                    if c == 0:
                        pe.wait_ge(wgtT_ready, f + 1)
                    pe.matmul(ps[:, 4 + c % 2, :], sel[:, c, :], wgtT[:], start=True, stop=True).then_inc(wb_done, 1)

            def down0(f):
                claim(B6, x_ready, NH + f + 1)
                if f == 0:
                    pe.wait_ge(ld_down, 32)
                pe.wait_ge(gu_ready, (NC0 + 1) * (f + 1))
                pe.wait_ge(hid0_ready, NC0 * (f + 1))
                for t in range(TH):
                    for c in range(NC0 + 1):
                        k = I0 if c == NC0 else P
                        ins = pe.matmul(ps[:, 6, t * D:(t + 1) * D], hid0[f][0:k, c, t * P:(t + 1) * P], wd_sb[0:k, c, :],
                                        start=(c == 0), stop=(c == NC0))
                ins.then_inc(down0_done, 1)

            def router(f):
                claim(B7, rdif_ready, f + 1)
                for t in range(TH):
                    ins = pe.matmul(ps[:, 7, t * E1:(t + 1) * E1], xnT[f][:, t * P:(t + 1) * P],
                                    cols_sb[:, C_RW:C_RW + E1], start=True, stop=True)
                ins.then_inc(router_done, 1)

            def turn_scores(f):
                pe.wait_ge(score_ready, f + 1)
                claim(B7, sT_ready, f + 1)
                for qt in range(QT):
                    ins = pe.transpose(ps[0:BH * E1, 7, qt * P:(qt + 1) * P],
                                       score[f][:, qt].rearrange("p b e -> p (b e)"), ident)
                ins.then_inc(scoreT_done, 1)

            def turn_slots(f):
                pe.wait_ge(slot_ready, f + 1)
                claim(B7, slotT_ready, f + 1)
                for qt in range(QT):
                    ins = pe.transpose(ps[:, 7, qt * BH * E1:(qt + 1) * BH * E1], slot[:, qt * P:(qt + 1) * P],
                                       ident[0:BH * E1, 0:BH * E1])
                ins.then_inc(slotT_done, 1)

            def gather(f):
                pe.wait_ge(onehot_ready, f + 1)
                for bl in range(BH):
                    claim(B01 + bl, xsel_ready, BH * f + bl + 1)
                    for k in range(2):
                        for qt in range(QT):
                            ins = pe.matmul(ps[:, 2 * bl + k, 0:4 * CAP], xn[f][:, QT * bl + qt, :],
                                            onehot[f][:, qt, bl, 4 * k:4 * k + 4].rearrange("p e c -> p (e c)"),
                                            start=(qt == 0), stop=(qt == QT - 1))
                        ins.then_inc(gather_done, 1)

            def turn_gated(f):
                pe.wait_ge(gated_ready, f + 1)
                for n in range(5):
                    claim(B6 + n % 2, gatedT_ready, 5 * f + n + 1)
                    for i in range(4 * n, 4 * n + 4):
                        t, m = divmod(i, NM)
                        src = gated[:, t % QT, t // QT].rearrange("p e c -> p (e c)")[:, m * MS:(m + 1) * MS]
                        ins = pe.transpose(ps[0:MS, 6 + n % 2, (i % 4) * P:(i % 4 + 1) * P], src, ident)
                    ins.then_inc(gatedT_done, 1)

            def up1(f, e):
                u = e % 2
                claim(B01 + u, hid1_ready, E1 * f + e + 1)
                if e == 0:
                    pe.wait_ge(xsel_ready, BH * (f + 1))
                    if f == 0:
                        pe.wait_ge(ld_w1, 16)
                for j in range(NJ):
                    ins = pe.matmul(ps[:, 2 * u + j // 2, (j % 2) * BH * CAP:(j % 2 + 1) * BH * CAP],
                                    w1_sb[:, e, j * P:(j + 1) * P], xsel[:, e].rearrange("p b c -> p (b c)"),
                                    start=True, stop=True)
                ins.then_inc(up1_done, 1)

            def down1(f, e):
                u = e % 2
                claim(B4 + u, yT_ready, E1 * f + e + 1)
                pe.wait_ge(hid1_ready, E1 * f + e + 1)
                if f == 0 and e == 0:
                    pe.wait_ge(ld_w2, 16)
                for j in range(NJ):
                    ins = pe.matmul(ps[:, 4 + u, 0:BH * CAP], w2_sb[:, e, j, :], hid1[u][:, j, :],
                                    start=(j == 0), stop=(j == NJ - 1))
                ins.then_inc(down1_done, 1)

            def experts1(f, hooks):
                gather(f)
                turn_gated(f)
                up1(f, 0)
                for e in range(E1):
                    if e + 1 < E1:
                        up1(f, e + 1)
                    down1(f, e)
                    for step in hooks.get(e, ()):
                        step()
                pe.wait_ge(yT_ready, E1 * (f + 1))
                for u, n in ((0, 8), (1, 2)):
                    claim(B01 + u, y_ready, 2 * f + u + 1)
                    for i in range(8 * u, 8 * u + n):
                        bl, m = divmod(i, NM)
                        src = yT[:, bl].rearrange("p e c -> p (e c)")[:, m * MS:(m + 1) * MS]
                        ins = pe.transpose(ps[0:MS, i // 4, (i % 4) * D:(i % 4 + 1) * D], src, ident)
                    ins.then_inc(yTT_done, 1)
                pe.wait_ge(gatedT_ready, 5 * (f + 1))
                pe.wait_ge(y_ready, 2 * (f + 1))
                for t in range(TH):
                    claim(B4 + t, out_ready, TH * f + t + 1)
                    bl = t // QT
                    for m in range(NM):
                        ins = pe.matmul(ps[:, 4 + t, 0:D], gatedT[:, NM * t + m, :], y[:, NM * bl + m, :],
                                        start=(m == 0), stop=(m == NM - 1))
                    ins.then_inc(scatter_done, 1)

            project_kv(0)
            turn_x(0)
            project_q(0)
            turn_x(1)
            project_q(1)
            attention(0)
            attention(1, after_scores=[lambda: project_out(0)], before_values=[lambda: turn_x(2), lambda: gate(0)])
            up0(0)
            project_out(1)
            project_kv(1)
            turn_weights(0)
            for n in range(1, NC0 + 1):
                up0(n)
                if n == 4:
                    turn_x(3)
                    gate(1)
            up0(NC0 + 1)
            turn_weights(1)
            down0(0)
            for n in range(1, NC0 + 1):
                up0(NC0 + 1 + n)
                if n == 5:
                    turn_x(4)
                    project_q(2)
            down0(1)
            attention(2, before_values=[lambda: turn_x(5), lambda: project_q(3)])
            attention(3, after_scores=[lambda: project_out(2)], before_values=[lambda: turn_x(6), lambda: router(0)])
            project_out(3)
            turn_scores(0)
            turn_slots(0)
            experts1(0, {1: [lambda: turn_x(7), lambda: router(1)], 2: [lambda: turn_scores(1)],
                         5: [lambda: turn_slots(1)]})
            experts1(1, {})


def host_constants():
    f = np.zeros((P, F_N), np.float32)
    f[:, F_ID:F_ID + P] = np.eye(P)
    f[:, F_MASK] = (np.arange(P) // DK) % 2 == 0
    f[:, F_MASK + 1] = (np.arange(P) // DK) % 2 == 1
    f[:, F_SLOT:F_SLOT + CAP] = np.arange(1, CAP + 1)
    f[:, F_E0:F_E0 + E0] = np.arange(E0)
    f[:, F_S:F_S + S] = np.arange(S)
    b = np.zeros((PARTS * H, NP * P), np.float32)
    for r in range(PARTS * H):
        j, e = divmod(r % H, 2)
        b[r, j * P + e * S2:j * P + (e + 1) * S2] = 1
    return f, b


def kernel(x, ctx_1024, condB_tau, fside_BxS2_0,
           L0_xcond_Wq, L0_xcond_bq, L0_xcond_Wk, L0_xcond_bk, L0_xcond_Wv, L0_xcond_bv, L0_xcond_Wo, L0_xcond_bo,
           L0_ffn_gate_w, L0_ffn_gate_b, L0_ffn_shared_wg, L0_ffn_shared_wu, L0_ffn_shared_wd,
           L0_ffn_experts_wg, L0_ffn_experts_wu, L0_ffn_experts_wd,
           L1_xcond_Wq, L1_xcond_bq, L1_xcond_Wk, L1_xcond_bk, L1_xcond_Wv, L1_xcond_bv, L1_xcond_Wo, L1_xcond_bo,
           L1_ffn_router_w, L1_ffn_w1, L1_ffn_b1, L1_ffn_w2, L1_ffn_b2):
    import concourse.bacc as _bacc
    from concourse.bass_utils import run_bass_kernel_spmd as _run

    a = np.ascontiguousarray
    fconst, selection = host_constants()
    ws = [[L0_xcond_Wq, L0_xcond_Wk, L0_xcond_Wv, L0_xcond_Wo], [L1_xcond_Wq, L1_xcond_Wk, L1_xcond_Wv, L1_xcond_Wo]]
    arrays = {
        "x": a(x),
        "ctxT": a(np.asarray(ctx_1024).reshape(B * S2, D).T),
        "wT": a(np.stack([np.stack([np.asarray(w).T for w in l], 1) for l in ws], 1)),
        "cols": a(np.concatenate([
            np.stack([L0_xcond_bq, L1_xcond_bq, L0_xcond_bk, L1_xcond_bk], 1),
            np.asarray(L1_ffn_b1).reshape(E1 * NJ, P).T, np.asarray(L1_ffn_b2).T,
            np.asarray(L0_ffn_gate_w), np.asarray(L1_ffn_router_w).T], 1)),
        "rows": a(np.concatenate([L0_xcond_bv, L1_xcond_bv, L0_xcond_bo, L1_xcond_bo, L0_ffn_gate_b, condB_tau])),
        "delta": a(fside_BxS2_0),
        "wg": a(np.concatenate([L0_ffn_experts_wg, np.asarray(L0_ffn_shared_wg)[None]]).transpose(1, 0, 2)),
        "wu": a(np.concatenate([L0_ffn_experts_wu, np.asarray(L0_ffn_shared_wu)[None]]).transpose(1, 0, 2)),
        "wd": a(np.asarray(L0_ffn_experts_wd).reshape(NC0, P, D).transpose(1, 0, 2)),
        "wds": a(L0_ffn_shared_wd),
        "w1": a(np.asarray(L1_ffn_w1).transpose(1, 0, 2)),
        "w2": a(np.asarray(L1_ffn_w2).reshape(E1, NJ, P, D).transpose(2, 0, 1, 3)),
        "fconst": fconst,
        "selection": selection,
    }
    nc = _bacc.Bacc("TRN2", target_bir_lowering=False, num_devices=1)
    args = [nc.dram_tensor(f"in_{n}", v.shape, mybir.dt.from_np(v.dtype), kind="ExternalInput").ap()
            for n, v in arrays.items()]
    args.append(nc.dram_tensor("out_x", (B, S, D), F32, kind="ExternalOutput").ap())
    build(nc, *args)
    r = _run(nc, [{f"in_{n}": v for n, v in arrays.items()}], core_ids=[0])
    return r.results[0]["out_x"]
```

```python
from contextlib import ExitStack

import concourse.bass as bass
import numpy as np
from concourse import mybir

F32 = mybir.dt.float32
BF16 = mybir.dt.bfloat16
U32 = mybir.dt.uint32
I32 = mybir.dt.int32
ALU = mybir.AluOpType
ACT = mybir.ActivationFunctionType
AX = mybir.AxisListType

P = 128
B, S, D = 4, 256, 128
S2 = 64
H, DK = 16, 8
NL = 2
NH = 2
BH = B // NH
QT = S // P
TH = BH * QT
TOK = TH * P
NP = H // 2
PR = 2 * DK
PARTS = 3
KSTK = 6 * PR
KROWS = KSTK + PARTS
QPART = (0, 0, 0, 1, 1, 2)
KPART = (0, 1, 2, 0, 1, 0)
E0, I0 = 16, 64
NC0 = E0 * I0 // P
E1, HID = 8, 512
NJ = HID // P
CAP = max(1, int(S * 2.0 / E1) + 1)
SLOTS = E1 * CAP
NM = 5
MS = SLOTS // NM
assert MS * NM == SLOTS and MS <= P
EPS = 1e-5
ISQ = float(1.0 / np.sqrt(np.float32(DK)))
ATT_G = (0, 1, 4, 5)

C_BQ, C_BK, C_B1, C_B2, C_GW, C_RW = 0, 2, 4, 4 + E1 * NJ, 4 + E1 * NJ + E1, 4 + E1 * NJ + E1 + E0
C_N = C_RW + E1
R_BV, R_BO, R_GB, R_TAU = 0, 2 * D, 4 * D, 4 * D + E0
R_N = R_TAU + B
F_ID, F_MASK, F_SLOT, F_E0, F_S = 0, P, P + 2, P + 2 + CAP, P + 2 + CAP + E0
F_N = F_S + S


def build(nc, x, ctxT, wT, cols, rows, delta, wg, wu, wd, wds, w1, w2, fconst, selection, out):
    q_scratch = nc.dram_tensor("q_scratch", [NH, PARTS, P, TOK], BF16, kind="Internal").ap()
    k_scratch = nc.dram_tensor("k_scratch", [NL, PARTS, P, B * 2 * S2], BF16, kind="Internal").ap()
    x_tiles = x.rearrange("b (q p) d -> (b q) p d", p=P)
    out_tiles = out.rearrange("b (q p) d -> (b q) p d", p=P)

    with ExitStack() as ctx:
        def sb(name, shape, dt=F32):
            return ctx.enter_context(nc.sbuf_tensor(name, shape, dt))

        def sem(name):
            return ctx.enter_context(nc.semaphore(name))

        wT_sb = sb("wT_sb", [P, NL, 4, D])
        ctx_sb = sb("ctx_sb", [P, B, 2, S2])
        cols_sb = sb("cols_sb", [P, C_N])
        rows_sb = sb("rows_sb", [P, R_N])
        fc = sb("fc", [P, F_N])
        ident_b = sb("ident_b", [P, P], BF16)
        sel_b = sb("sel_b", [PARTS * H, NP * P], BF16)
        ones_b = sb("ones_b", [PARTS, TOK], BF16)
        wg_sb = sb("wg_sb", [P, E0 + 1, I0])
        wu_sb = sb("wu_sb", [P, E0 + 1, I0])
        wd_sb = sb("wd_sb", [P, NC0 + 1, D])
        w1_sb = sb("w1_sb", [P, E1, HID])
        w2_sb = sb("w2_sb", [P, E1, NJ, D])
        ident = fc[:, F_ID:F_ID + P]
        mask2 = fc[:, F_MASK:F_MASK + 2]
        iota_slot = fc[:, F_SLOT:F_SLOT + CAP]
        iota_e0 = fc[:, F_E0:F_E0 + E0]
        iota_s = fc[0:2 * E1, F_S:F_S + S]
        sel = sel_b[:].rearrange("r (j c) -> r j c", j=NP)
        xs = [sb(f"xs{h}", [P, TH, D]) for h in range(NH)]
        xn = [sb(f"xn{h}", [P, TH, D]) for h in range(NH)]
        xb = [sb(f"xb{h}", [P, TH, D]) for h in range(NH)]
        xnT = [sb(f"xnT{h}", [P, TOK]) for h in range(NH)]
        bn6 = sb("bn6", [P, TH, 6])
        mv = [sb(f"mv{h}", [P, TH, 2]) for h in range(NH)]
        veps = sb("veps", [P, TH])
        rstd = sb("rstd", [P, TH])
        rstd_t = sb("rstd_t", [P, TH])
        q_rest = sb("q_rest", [P, TOK])
        q_parts = [sb(f"q_parts{h}", [P, PARTS, TOK], BF16) for h in range(NH)]
        q_stack = [sb(f"q_stack{h}", [KROWS, NP, TOK], BF16) for h in range(NH)]
        tau_s = sb("tau_s", [P, B])
        k32 = sb("k32", [P, B, S2])
        k_part = sb("k_part", [P, PARTS, B, S2], BF16)
        k_rest = sb("k_rest", [P, B, S2])
        k_masked = [sb(f"k_masked{l}", [P, PARTS, B, 2, S2], BF16) for l in range(NL)]
        k_stack = [sb(f"k_stack{l}", [KROWS, NP, B, 2 * S2], BF16) for l in range(NL)]
        v_blk = [sb(f"v_blk{l}", [P, B, NP, 2, DK + 1]) for l in range(NL)]
        dl32 = sb("dl32", [1, B, S2])
        dl_rest = sb("dl_rest", [1, B, S2])
        dl_parts = sb("dl_parts", [1, PARTS, B, 2, S2], BF16)
        negmax = sb("negmax", [P, TH, H])
        nm_parts = [sb(f"nm_parts{i}", [P, QT, PARTS, H], BF16) for i in range(BH)]
        nm_rest = sb("nm_rest", [P, QT, H])
        nmT = [sb(f"nmT{i}", [PARTS * H, S], BF16) for i in range(BH)]
        probs_sb = sb("probs_sb", [P, BH, NP, S])
        probs = [probs_sb[:, i] for i in range(BH)]
        rsum = sb("rsum", [P, TH, H])
        att = sb("att", [P, TH, H, DK])
        attT = sb("attT", [P, TOK])
        lg = sb("lg", [P, TH, E0])
        th = sb("th", [P, TH, E0])
        sig = sb("sig", [P, TH, E0])
        top8 = sb("top8", [P, TH, 8])
        top_ix = sb("top_ix", [P, TH, 8], U32)
        top_ixf = sb("top_ixf", [P, TH, 8])
        vsum = sb("vsum", [P, TH])
        vrec = sb("vrec", [P, TH])
        vnorm = sb("vnorm", [P, TH, 2])
        pick = sb("pick", [P, TH, 2, E0])
        wgt = sb("wgt", [P, TH, E0])
        wgt_rest = sb("wgt_rest", [P, TH, E0])
        wgt_parts = sb("wgt_parts", [P, TH, PARTS, E0], BF16)
        wgtT = sb("wgtT", [PARTS * E0, TOK], BF16)
        sg = [sb(f"sg{i}", [P, TOK]) for i in range(2)]
        hid0 = [sb(f"hid0{h}", [P, NC0 + 1, TOK]) for h in range(NH)]
        rmax = sb("rmax", [P, TH])
        rdif = sb("rdif", [P, TH, E1])
        rexp = sb("rexp", [P, TH, E1])
        rtot = sb("rtot", [P, TH])
        rrec = sb("rrec", [P, TH])
        score = [sb(f"score{h}", [P, QT, BH, E1]) for h in range(NH)]
        sT = sb("sT", [BH * E1, S])
        work = sb("work", [BH * E1, S])
        m8 = sb("m8", [BH * E1, 8])
        m8ix = sb("m8ix", [BH * E1, 8], U32)
        m8ixf = sb("m8ixf", [BH * E1, 8])
        chosen = sb("chosen", [BH * E1, S])
        ones_s = sb("ones_s", [BH * E1, S])
        slot_n = sb("slot_n", [BH * E1, S])
        slot = sb("slot", [BH * E1, S])
        slotT = sb("slotT", [P, QT, BH, E1])
        W1H, W1X = QT * BH * SLOTS, BH * SLOTS
        free0 = hid0[0][:].rearrange("p c s -> p (c s)")
        free1 = hid0[1][:].rearrange("p c s -> p (c s)")
        sel32 = free0[0:PARTS * H, 0:NP * P]
        onehot = [free0[:, h * W1H:(h + 1) * W1H].rearrange("p (q b e c) -> p q b e c", q=QT, b=BH, e=E1)
                  for h in range(NH)]
        gated = free1[:, 0:W1H].rearrange("p (q b e c) -> p q b e c", q=QT, b=BH, e=E1)
        xsel = free1[:, W1H:W1H + W1X].rearrange("p (e b c) -> p e b c", e=E1, b=BH)
        yT = free1[:, W1H + W1X:W1H + 2 * W1X].rearrange("p (b e c) -> p b e c", b=BH, e=E1)
        free2 = probs_sb[0:MS].rearrange("p i j s -> p (i j s)")
        gatedT = free2[:, 0:TH * NM * P].rearrange("m (i s) -> m i s", s=P)
        y = free2[:, TH * NM * P:TH * NM * P + BH * NM * D].rearrange("m (i d) -> m i d", d=D)
        free3 = wg_sb[:].rearrange("p e i -> p (e i)")
        hid1 = [free3[:, i * NJ * BH * CAP:(i + 1) * NJ * BH * CAP].rearrange("p (j c) -> p j c", j=NJ) for i in range(2)]

        ps = ctx.enter_context(nc.psum_tensor("ps", [P, 8, 512], F32))

        ld_x = [sem(f"ld_x{h}") for h in range(NH)]
        ld_ctx = sem("ld_ctx")
        ld_wT = [sem(f"ld_wT{l}") for l in range(NL)]
        ld_cols = sem("ld_cols")
        ld_rows = sem("ld_rows")
        ld_fc = sem("ld_fc")
        ld_sel = sem("ld_sel")
        ld_delta = sem("ld_delta")
        ld_gu = sem("ld_gu")
        ld_down = sem("ld_down")
        ld_w1 = sem("ld_w1")
        ld_w2 = sem("ld_w2")
        q_hi_ready = sem("q_hi_ready")
        q_mid_ready = sem("q_mid_ready")
        q_lo_ready = sem("q_lo_ready")
        q_out = [sem(f"q_out{c}") for c in range(PARTS)]
        q_stacked = [sem(f"q_stacked{h}") for h in range(NH)]
        k_parts_ready = sem("k_parts_ready")
        k_out = [sem(f"k_out{c}") for c in range(PARTS)]
        k_stacked = [sem(f"k_stacked{l}") for l in range(NL)]
        delta_ready = sem("delta_ready")
        ones_ready = sem("ones_ready")
        ones_stacked = [sem(f"ones_stacked{h}") for h in range(NH)]
        bf16_ready = sem("bf16_ready")
        dve_step = sem("dve_step")
        pool_step = sem("pool_step")
        stats_ready = sem("stats_ready")
        xn_ready = sem("xn_ready")
        xb_ready = sem("xb_ready")
        xT_done = sem("xT_done")
        xnT_ready = sem("xnT_ready")
        x_ready = sem("x_ready")
        fill_done = sem("fill_done")
        k_done = sem("k_done")
        v_done = sem("v_done")
        k32_ready = sem("k32_ready")
        v_ready = sem("v_ready")
        q_rest_ready = sem("q_rest_ready")
        q_done = sem("q_done")
        s1_done = sem("s1_done")
        max_ready = sem("max_ready")
        nm_ready = sem("nm_ready")
        nmT_done = sem("nmT_done")
        nmT_ready = sem("nmT_ready")
        s2_done = sem("s2_done")
        probs_ready = sem("probs_ready")
        av_done = sem("av_done")
        att_ready = sem("att_ready")
        attT_done = sem("attT_done")
        attT_ready = sem("attT_ready")
        wo_done = sem("wo_done")
        gate_done = sem("gate_done")
        gate_lg = sem("gate_lg")
        gate_th = sem("gate_th")
        wgt_ready = sem("wgt_ready")
        wgtT_done = sem("wgtT_done")
        wgtT_ready = sem("wgtT_ready")
        up0_done = sem("up0_done")
        wb_done = sem("wb_done")
        th0_ready = sem("th0_ready")
        gu_ready = sem("gu_ready")
        hid0_ready = sem("hid0_ready")
        down0_done = sem("down0_done")
        router_done = sem("router_done")
        rdif_ready = sem("rdif_ready")
        rexp_ready = sem("rexp_ready")
        score_ready = sem("score_ready")
        scoreT_done = sem("scoreT_done")
        sT_ready = sem("sT_ready")
        slot_ready = sem("slot_ready")
        slotT_done = sem("slotT_done")
        slotT_ready = sem("slotT_ready")
        onehot_ready = sem("onehot_ready")
        gated_ready = sem("gated_ready")
        gather_done = sem("gather_done")
        xsel_ready = sem("xsel_ready")
        gatedT_done = sem("gatedT_done")
        gatedT_ready = sem("gatedT_ready")
        up1_done = sem("up1_done")
        hid1_ready = sem("hid1_ready")
        down1_done = sem("down1_done")
        yT_ready = sem("yT_ready")
        yTT_done = sem("yTT_done")
        y_ready = sem("y_ready")
        scatter_done = sem("scatter_done")
        out_ready = sem("out_ready")
        stored = sem("stored")

        block = ctx.enter_context(nc.Block())

        @block.sync
        def _(sp):
            def load_x(h):
                sp.dma_start(xs[h][:], x_tiles[TH * h:TH * h + TH].rearrange("t p d -> p t d")).then_inc(ld_x[h], 16)

            load_x(0)
            for e in range(2):
                sp.dma_start(ctx_sb[:, :, e, :], ctxT.rearrange("d (b k) -> d b k", b=B)).then_inc(ld_ctx, 16)
            sp.dma_start(fc[:], fconst).then_inc(ld_fc, 16)
            load_x(1)
            sp.dma_start(sel32, selection).then_inc(ld_sel, 16)

            def k_bounce(l):
                for c in range(PARTS):
                    sp.wait_ge(k_parts_ready, PARTS * l + c + 1)
                    sp.dma_start(k_scratch[l, c], k_masked[l][:, c].rearrange("p b e k -> p (b e k)")).then_inc(k_out[c], 16)
                for c in range(PARTS):
                    sp.wait_ge(k_out[c], 16 * (l + 1))
                    src = k_scratch[l, c].rearrange("(j r) n -> r j n", r=PR)
                    for i in range(len(KPART)):
                        if KPART[i] == c:
                            dst = k_stack[l][PR * i:PR * (i + 1)].rearrange("r j b n -> r j (b n)")
                            sp.dma_start(dst, src).then_inc(k_stacked[l], 16)

            def q_bounce(a):
                h = a % NH
                for c, ready in enumerate((q_hi_ready, q_mid_ready, q_lo_ready)):
                    sp.wait_ge(ready, a + 1)
                    sp.dma_start(q_scratch[h, c], q_parts[h][:, c, :]).then_inc(q_out[c], 16)
                for c in range(PARTS):
                    sp.wait_ge(q_out[c], 16 * (a + 1))
                    src = q_scratch[h, c].rearrange("(j r) n -> r j n", r=PR)
                    for i in range(len(QPART)):
                        if QPART[i] == c:
                            sp.dma_start(q_stack[h][PR * i:PR * (i + 1)], src).then_inc(q_stacked[h], 16)

            def ones_rows(h):
                src = ones_b[:, None, :].broadcast_to([PARTS, NP, TOK])
                sp.dma_start(q_stack[h][KSTK:KROWS], src).then_inc(ones_stacked[h], 16)

            def delta_rows(l):
                for c in range(PARTS):
                    src = dl_parts[0:1, c].rearrange("a b e k -> a (b e k)")[:, None, :].broadcast_to([1, NP, B * 2 * S2])
                    dst = k_stack[l][KSTK + c:KSTK + c + 1].rearrange("r j b n -> r j (b n)")
                    sp.dma_start(dst, src).then_inc(k_stacked[l], 16)
            sp.wait_ge(ones_ready, 1)
            ones_rows(0)
            sp.wait_ge(delta_ready, 1)
            delta_rows(0)
            k_bounce(0)
            q_bounce(0)
            ones_rows(1)
            q_bounce(1)
            delta_rows(1)
            k_bounce(1)
            q_bounce(2)
            q_bounce(3)
            for n in range(NH * TH):
                sp.wait_ge(out_ready, n + 1)
                sp.dma_start(out_tiles[n], xb[n // TH][:, n % TH, :]).then_inc(stored, 16)
            sp.wait_ge(stored, 16 * NH * TH)

        @block.gpsimd
        def _(pool):
            steps = [0]

            def link(ins):
                steps[0] += 1
                ins.then_inc(pool_step, 1)
                pool.wait_ge(pool_step, steps[0])

            pool.dma_start(dl32[:], delta.rearrange("b k -> (b k)").rearrange("(a b k) -> a b k", a=1, b=B)).then_inc(ld_delta, 16)
            pool.memset(ones_b[:], 1.0).then_inc(ones_ready, 1)
            pool.wait_ge(ones_ready, 1)
            pool.wait_ge(ld_delta, 16)
            link(pool.tensor_scalar(dl32[:], dl32[:], ISQ, None, ALU.mult))
            link(pool.tensor_copy(dl_parts[:, 0, :, 0, :], dl32[:]))
            pool.tensor_copy(dl_parts[:, 0, :, 1, :], dl_parts[:, 0, :, 0, :])
            link(pool.tensor_tensor(dl_rest[:], dl32[:], dl_parts[:, 0, :, 0, :], ALU.subtract))
            link(pool.tensor_copy(dl_parts[:, 1, :, 0, :], dl_rest[:]))
            pool.tensor_copy(dl_parts[:, 1, :, 1, :], dl_parts[:, 1, :, 0, :])
            link(pool.tensor_tensor(dl_rest[:], dl_rest[:], dl_parts[:, 1, :, 0, :], ALU.subtract))
            pool.tensor_copy(dl_parts[:, 2, :, 0, :], dl_rest[:])
            pool.tensor_copy(dl_parts[:, 2, :, 1, :], dl_rest[:]).then_inc(delta_ready, 1)
            link(pool.memset(ones_s[:], 1.0))
            for l in range(NL):
                link(pool.memset(v_blk[l][:], 0.0))
                link(pool.memset(v_blk[l][0:S2, :, :, 0, DK:DK + 1], 1.0))
                pool.memset(v_blk[l][S2:2 * S2, :, :, 1, DK:DK + 1], 1.0).then_inc(fill_done, 1)
                pool.wait_ge(fill_done, l + 1)
            def residual_base(g):
                h = g % NH
                if g in ATT_G:
                    l = ATT_G.index(g) // NH
                    bo = rows_sb[:, R_BO + l * D:R_BO + (l + 1) * D][:, None, :].broadcast_to([P, TH, D])
                    if g < NH:
                        pool.wait_ge(ld_x[h], 16)
                        pool.wait_ge(ld_rows, 16)
                    else:
                        pool.wait_ge(x_ready, g - 1)
                    pool.tensor_tensor(xb[h][:], xs[h][:], bo, ALU.add).then_inc(xb_ready, 1)
                elif g < 6:
                    pool.wait_ge(xn_ready, TH * (g + 1))
                    pool.tensor_tensor(xb[h][:], xs[h][:], xn[h][:], ALU.add).then_inc(xb_ready, 1)

            def gate_onehot(f):
                pool.wait_ge(onehot_ready, BH * (f + 1))
                if f:
                    pool.wait_ge(gatedT_done, 5 * f)
                sc = score[f][:].rearrange("p q b e -> p (q b e)")[:, :, None].broadcast_to([P, TH * E1, CAP])
                pool.tensor_tensor(gated[:].rearrange("p q b e c -> p (q b e) c"),
                                   onehot[f][:].rearrange("p q b e c -> p (q b e) c"), sc, ALU.mult).then_inc(gated_ready, 1)

            for g in range(6):
                residual_base(g)
            gate_onehot(0)
            gate_onehot(1)

        @block.scalar
        def _(act):
            act.dma_start(wT_sb[:, 0], wT[:, 0]).then_inc(ld_wT[0], 16)
            act.dma_start(cols_sb[:], cols).then_inc(ld_cols, 16)
            act.dma_start(rows_sb[:], rows.partition_broadcast(P)).then_inc(ld_rows, 16)
            act.dma_start(wT_sb[:, 1], wT[:, 1]).then_inc(ld_wT[1], 16)

            def load_later_weights():
                act.dma_start(wg_sb[:], wg).then_inc(ld_gu, 16)
                act.dma_start(wu_sb[:], wu).then_inc(ld_gu, 16)

            def load_down():
                act.dma_start(wd_sb[:, 0:NC0], wd).then_inc(ld_down, 16)
                act.dma_start(wd_sb[0:I0, NC0], wds).then_inc(ld_down, 16)

            def load_experts1():
                act.dma_start(w1_sb[:], w1).then_inc(ld_w1, 16)
                act.dma_start(w2_sb[:], w2).then_inc(ld_w2, 16)

            def narrow_constants():
                act.wait_ge(ld_sel, 16)
                act.activation(sel_b[:], sel32, ACT.Copy).then_inc(bf16_ready, 1)
                act.wait_ge(ld_fc, 16)
                act.activation(ident_b[:], ident, ACT.Copy).then_inc(bf16_ready, 1)

            def xnT_copy(g, bank):
                act.wait_ge(xT_done, g + 1)
                act.activation(xnT[g % NH][:], ps[:, bank, :], ACT.Copy).then_inc(xnT_ready, 1)

            def q_hi(a, bank):
                l, h = a // NH, a % NH
                act.wait_ge(q_done, a + 1)
                if a == 0:
                    act.wait_ge(ld_cols, 16)
                act.activation(q_parts[h][:, 0, :], ps[:, bank, :], ACT.Identity,
                               bias=cols_sb[:, C_BQ + l:C_BQ + l + 1]).then_inc(q_hi_ready, 1)

            def nmT_copy(a, bl, bank):
                act.wait_ge(nmT_done, BH * a + bl + 1)
                act.activation(nmT[bl][:], ps[:, bank, :].bitcast(BF16)[0:PARTS * H, 0:S], ACT.Copy).then_inc(nmT_ready, 1)

            def exp(a, bl, n, bank):
                if a and n == 0:
                    act.wait_ge(av_done, TH * (a - 1) + QT * (bl + 1))
                act.wait_ge(s2_done, (NP // 2) * (BH * a + bl) + n + 1)
                act.activation(probs[bl][:, 2 * n:2 * n + 2, :], ps[:, bank, :].rearrange("p (j s) -> p j s", j=2),
                               ACT.Exp).then_inc(probs_ready, 1)

            def attT_copy(a, bank):
                act.wait_ge(attT_done, a + 1)
                act.activation(attT[:], ps[:, bank, :], ACT.Copy).then_inc(attT_ready, 1)

            def gate_tanh(f):
                act.wait_ge(gate_lg, f + 1)
                act.activation(th[:], lg[:], ACT.Tanh, scale=0.5).then_inc(gate_th, 1)

            def wgtT_copy(f, bank):
                act.wait_ge(wgtT_done, f + 1)
                act.activation(wgtT[:], ps[:, bank, :].bitcast(BF16)[0:PARTS * E0, 0:TOK], ACT.Copy).then_inc(wgtT_ready, 1)

            def tanh0(n, bank):
                m = I0 if n % (NC0 + 1) == 0 else P
                act.wait_ge(up0_done, n + 1)
                f, i = divmod(n - 2, NC0 + 1)
                if n >= 2:
                    if i:
                        act.wait_ge(hid0_ready, NC0 * f + i)
                    else:
                        act.wait_ge(gu_ready, n - 1)
                act.activation(sg[n % 2][0:m, :], ps[0:m, bank, :], ACT.Tanh, scale=0.5).then_inc(th0_ready, 1)

            def router_exp(f):
                act.wait_ge(rdif_ready, f + 1)
                act.activation(rexp[:], rdif[:], ACT.Exp).then_inc(rexp_ready, 1)

            def xsel_copy(f, bl, bank):
                for k in range(2):
                    act.wait_ge(gather_done, 2 * (BH * f + bl) + k + 1)
                    src = ps[:, bank + k, 0:4 * CAP].rearrange("p (e c) -> p e c", e=4)
                    ins = act.activation(xsel[:, 4 * k:4 * k + 4, bl, :], src, ACT.Copy)
                ins.then_inc(xsel_ready, 1)

            def gatedT_copy(f, n, bank):
                act.wait_ge(gatedT_done, 5 * f + n + 1)
                act.activation(gatedT[:, 4 * n:4 * n + 4, :], ps[0:MS, bank, :].rearrange("m (i s) -> m i s", i=4),
                               ACT.Copy).then_inc(gatedT_ready, 1)

            def gelu(f, e, bank):
                n = E1 * f + e
                act.wait_ge(up1_done, n + 1)
                if n >= 2:
                    act.wait_ge(down1_done, n - 1)
                for j in range(NJ):
                    src = ps[:, bank + j // 2, (j % 2) * BH * CAP:(j % 2 + 1) * BH * CAP]
                    ins = act.activation(hid1[e % 2][:, j, :], src, ACT.Gelu,
                                         bias=cols_sb[:, C_B1 + NJ * e + j:C_B1 + NJ * e + j + 1])
                ins.then_inc(hid1_ready, 1)

            for step, *at in (
                (xnT_copy, 0, 4), (q_hi, 0, 7), (xnT_copy, 1, 7), (q_hi, 1, 7), (load_later_weights,),
                (narrow_constants,), (nmT_copy, 0, 0, 6), (exp, 0, 0, 0, 5), (exp, 0, 0, 1, 7), (nmT_copy, 0, 1, 5),
                (exp, 0, 0, 2, 4), (exp, 0, 0, 3, 6), (load_down,), (exp, 0, 1, 0, 7), (exp, 0, 1, 1, 5),
                (nmT_copy, 1, 0, 7), (exp, 0, 1, 2, 5), (exp, 0, 1, 3, 4), (load_experts1,), (exp, 1, 0, 0, 6),
                (exp, 1, 0, 1, 7), (nmT_copy, 1, 1, 5), (exp, 1, 0, 2, 7), (exp, 1, 0, 3, 5), (attT_copy, 0, 4),
                (exp, 1, 1, 0, 6), (exp, 1, 1, 1, 7), (exp, 1, 1, 2, 5), (exp, 1, 1, 3, 6), (xnT_copy, 2, 6),
                (gate_tanh, 0), (attT_copy, 1, 4), (tanh0, 0, 0), (tanh0, 1, 2), (wgtT_copy, 0, 7), (tanh0, 2, 0),
                (tanh0, 3, 2), (tanh0, 4, 0), (xnT_copy, 3, 4), (tanh0, 5, 2), (tanh0, 6, 0), (tanh0, 7, 2),
                (gate_tanh, 1), (tanh0, 8, 0), (tanh0, 9, 2), (tanh0, 10, 0), (tanh0, 11, 0), (wgtT_copy, 1, 6),
                (xnT_copy, 4, 7), (tanh0, 12, 2), (tanh0, 13, 0), (q_hi, 2, 7), (tanh0, 14, 2), (tanh0, 15, 0),
                (tanh0, 16, 2), (tanh0, 17, 0), (nmT_copy, 2, 0, 6), (nmT_copy, 2, 1, 5), (exp, 2, 0, 0, 7),
                (exp, 2, 0, 1, 6), (exp, 2, 0, 2, 5), (exp, 2, 0, 3, 4), (exp, 2, 1, 0, 7), (exp, 2, 1, 1, 6),
                (exp, 2, 1, 2, 5), (exp, 2, 1, 3, 4), (xnT_copy, 5, 6), (q_hi, 3, 4), (attT_copy, 2, 5),
                (xnT_copy, 6, 7), (nmT_copy, 3, 0, 5), (router_exp, 0), (exp, 3, 0, 0, 4), (exp, 3, 0, 1, 7),
                (nmT_copy, 3, 1, 5), (exp, 3, 0, 2, 6), (exp, 3, 0, 3, 4), (exp, 3, 1, 0, 5), (exp, 3, 1, 1, 7),
                (exp, 3, 1, 2, 6), (exp, 3, 1, 3, 7), (attT_copy, 3, 5), (xsel_copy, 0, 0, 0), (xsel_copy, 0, 1, 2),
                (xnT_copy, 7, 7), (gelu, 0, 0, 0), (gelu, 0, 1, 2), (router_exp, 1), (gelu, 0, 2, 0),
                (gelu, 0, 3, 2), (gatedT_copy, 0, 0, 5), (gatedT_copy, 0, 1, 6), (gatedT_copy, 0, 2, 7),
                (gatedT_copy, 0, 3, 4), (gelu, 0, 4, 0), (gelu, 0, 5, 2), (gatedT_copy, 0, 4, 7), (gelu, 0, 6, 0),
                (gelu, 0, 7, 2), (xsel_copy, 1, 0, 0), (xsel_copy, 1, 1, 0), (gelu, 1, 0, 0), (gelu, 1, 1, 2),
                (gelu, 1, 2, 0), (gelu, 1, 3, 2), (gelu, 1, 4, 0), (gelu, 1, 5, 2), (gelu, 1, 6, 0), (gelu, 1, 7, 2),
                (gatedT_copy, 1, 0, 7), (gatedT_copy, 1, 1, 6), (gatedT_copy, 1, 2, 4), (gatedT_copy, 1, 3, 5),
                (gatedT_copy, 1, 4, 7),
            ):
                step(*at)

        @block.vector
        def _(dve):
            steps = [0]

            def mark(ins):
                steps[0] += 1
                ins.then_inc(dve_step, 1)

            def settle():
                dve.wait_ge(dve_step, steps[0])

            def link(ins):
                mark(ins)
                settle()

            def stats(g):
                h = g % NH
                if g < NH:
                    dve.wait_ge(ld_x[h], 16)
                else:
                    dve.wait_ge(x_ready, g - 1)
                if g:
                    dve.wait_ge(stats_ready, g)
                for t in range(TH):
                    mark(dve.bn_stats(bn6[:, t, :], xs[h][:, t, :]))
                settle()
                for t in range(TH):
                    ins = dve.bn_aggr(mv[h][:, t, :], bn6[:, t, :])
                ins.then_inc(stats_ready, 1)

            def normalise(g):
                h = g % NH
                dve.wait_ge(stats_ready, g + 1)
                if g:
                    dve.wait_ge(xn_ready, TH * g)
                link(dve.tensor_scalar(veps[:], mv[h][:, :, 1], EPS, None, ALU.add))
                link(dve.tensor_scalar(rstd_t[:].bitcast(I32), veps[:].bitcast(I32), 1, None, ALU.arith_shift_right))
                link(dve.tensor_scalar(rstd[:].bitcast(I32), rstd_t[:].bitcast(I32), -1.0, float(0x5F3759DF), ALU.mult, ALU.add))
                for _ in range(3):
                    link(dve.scalar_tensor_tensor(rstd_t[:], rstd[:], -0.5, veps[:], ALU.mult, ALU.mult))
                    link(dve.tensor_tensor(rstd_t[:], rstd_t[:], rstd[:], ALU.mult))
                    link(dve.scalar_tensor_tensor(rstd[:], rstd_t[:], 1.5, rstd[:], ALU.add, ALU.mult))
                for t in range(TH):
                    dve.tensor_scalar(xn[h][:, t, :], xs[h][:, t, :], mv[h][:, t, 0:1], rstd[:, t:t + 1],
                                      ALU.subtract, ALU.mult).then_inc(xn_ready, 1)

            def k_prep(l, bank):
                dve.wait_ge(k_done, l + 1)
                if l == 0:
                    dve.wait_ge(ld_rows, 16)
                    dve.wait_ge(ld_cols, 16)
                    dve.wait_ge(ld_fc, 16)
                    link(dve.tensor_scalar(tau_s[:], rows_sb[:, R_TAU:R_TAU + B], ISQ, None, ALU.mult))
                if l:
                    dve.wait_ge(k_parts_ready, PARTS * l)
                for b in range(B):
                    ins = dve.tensor_scalar(k32[:, b, :], ps[:, bank, b * S2:(b + 1) * S2],
                                            cols_sb[:, C_BK + l:C_BK + l + 1], tau_s[:, b:b + 1], ALU.add, ALU.mult)
                    if b == B - 1:
                        ins.then_inc(k32_ready, 1)
                    else:
                        mark(ins)
                dve.wait_ge(k32_ready, l + 1)
                settle()
                rest = k32
                for c in range(PARTS):
                    link(dve.tensor_copy(k_part[:, c], rest[:]))
                    for e in range(2):
                        ins = dve.tensor_scalar(k_masked[l][:, c, :, e, :], k_part[:, c], mask2[:, e:e + 1], None, ALU.mult)
                    ins.then_inc(k_parts_ready, 1)
                    if c < PARTS - 1:
                        link(dve.tensor_tensor(k_rest[:], rest[:], k_part[:, c], ALU.subtract))
                        rest = k_rest

            def v_prep(l, bank):
                dve.wait_ge(v_done, l + 1)
                dve.wait_ge(fill_done, l + 1)
                v_ps = ps[:, bank, :].rearrange("p (b j e d) -> p b j e d", b=B, j=NP, e=2)
                bv = rows_sb[:, R_BV + l * D:R_BV + (l + 1) * D].rearrange("p (j e d) -> p j e d", j=NP, e=2)
                for e in range(2):
                    r = slice(S2 * e, S2 * (e + 1))
                    ins = dve.tensor_tensor(v_blk[l][r, :, :, e, 0:DK], v_ps[r, :, :, e, :],
                                            bv[r, :, e, :][:, None, :, :].broadcast_to([S2, B, NP, DK]), ALU.add)
                    ins.then_inc(v_ready, 1)

            def q_split(a, bank):
                l, h = a // NH, a % NH
                dve.wait_ge(q_hi_ready, a + 1)
                if a:
                    dve.wait_ge(q_lo_ready, a)
                dve.scalar_tensor_tensor(q_rest[:], ps[:, bank, :], cols_sb[:, C_BQ + l:C_BQ + l + 1], q_parts[h][:, 0, :],
                                         ALU.add, ALU.subtract).then_inc(q_rest_ready, 1)

            def q_split2(a):
                h = a % NH
                dve.wait_ge(q_rest_ready, a + 1)
                dve.tensor_copy(q_parts[h][:, 1, :], q_rest[:]).then_inc(q_mid_ready, 1)
                dve.wait_ge(q_mid_ready, a + 1)
                dve.tensor_tensor(q_parts[h][:, 2, :], q_rest[:], q_parts[h][:, 1, :], ALU.subtract).then_inc(q_lo_ready, 1)

            def score_max(a, t, bank):
                dve.wait_ge(s1_done, TH * a + t + 1)
                dve.tensor_reduce(negmax[:, t, :], ps[:, bank:bank + 2, :].rearrange("p n (e k) -> p (n e) k", k=S2),
                                  AX.X, ALU.max, negate=True).then_inc(max_ready, 1)

            def max_parts(a, bl):
                nm = negmax[:, QT * bl:QT * bl + QT, :]
                dve.wait_ge(max_ready, TH * a + QT * (bl + 1))
                parts = nm_parts[bl]
                if a or bl:
                    dve.wait_ge(nm_ready, BH * a + bl)
                link(dve.tensor_copy(parts[:, :, 0, :], nm))
                link(dve.tensor_tensor(nm_rest[:], nm, parts[:, :, 0, :], ALU.subtract))
                link(dve.tensor_copy(parts[:, :, 1, :], nm_rest[:]))
                dve.tensor_tensor(parts[:, :, 2, :], nm_rest[:], parts[:, :, 1, :], ALU.subtract).then_inc(nm_ready, 1)

            def normalise_att(a, t, bank):
                t_all = TH * a + t
                dve.wait_ge(av_done, t_all + 1)
                av = ps[:, bank, 0:H * (DK + 1)].rearrange("p (e d) -> p e d", d=DK + 1)
                if t_all >= TH:
                    dve.wait_ge(att_ready, t_all - TH + 1)
                link(dve.reciprocal(rsum[:, t], av[:, :, DK]))
                dve.tensor_tensor(att[:, t], av[:, :, 0:DK], rsum[:, t][:, :, None].broadcast_to([P, H, DK]),
                                  ALU.mult).then_inc(att_ready, 1)

            def residual(g, bank):
                h = g % NH
                if g in ATT_G:
                    dve.wait_ge(wo_done, ATT_G.index(g) + 1)
                else:
                    dve.wait_ge(down0_done, g - 1)
                dve.wait_ge(xb_ready, g + 1)
                dve.tensor_tensor(xs[h][:], ps[:, bank, :].rearrange("p (t d) -> p t d", t=TH), xb[h][:],
                                  ALU.add).then_inc(x_ready, 1)

            def gate_logits(f, bank):
                dve.wait_ge(gate_done, f + 1)
                gb = rows_sb[:, R_GB:R_GB + E0][:, None, :].broadcast_to([P, TH, E0])
                dve.tensor_tensor(lg[:], ps[:, bank, 0:TH * E0].rearrange("p (t e) -> p t e", t=TH), gb,
                                  ALU.add).then_inc(gate_lg, 1)

            def route(f):
                dve.wait_ge(gate_th, f + 1)
                if f:
                    dve.wait_ge(wgt_ready, f)
                link(dve.tensor_scalar(sig[:], th[:], 0.5, 0.5, ALU.mult, ALU.add))
                for t in range(TH):
                    mark(dve.max(top8[:, t, :], sig[:, t, :]))
                settle()
                for t in range(TH):
                    mark(dve.max_index(top_ix[:, t, :], top8[:, t, :], sig[:, t, :]))
                link(dve.tensor_tensor(vsum[:], top8[:, :, 0], top8[:, :, 1], ALU.add))
                mark(dve.tensor_copy(top_ixf[:], top_ix[:]))
                link(dve.reciprocal(vrec[:], vsum[:]))
                mark(dve.tensor_tensor(vnorm[:], top8[:, :, 0:2], vrec[:][:, :, None].broadcast_to([P, TH, 2]), ALU.mult))
                link(dve.tensor_tensor(pick[:], iota_e0[:, None, None, :].broadcast_to([P, TH, 2, E0]),
                                       top_ixf[:, :, 0:2][:, :, :, None].broadcast_to([P, TH, 2, E0]), ALU.is_equal))
                link(dve.tensor_tensor(pick[:], pick[:], vnorm[:][:, :, :, None].broadcast_to([P, TH, 2, E0]), ALU.mult))
                link(dve.tensor_tensor(wgt[:], pick[:, :, 0, :], pick[:, :, 1, :], ALU.add))
                link(dve.tensor_copy(wgt_parts[:, :, 0, :], wgt[:]))
                link(dve.tensor_tensor(wgt_rest[:], wgt[:], wgt_parts[:, :, 0, :], ALU.subtract))
                link(dve.tensor_copy(wgt_parts[:, :, 1, :], wgt_rest[:]))
                dve.tensor_tensor(wgt_parts[:, :, 2, :], wgt_rest[:], wgt_parts[:, :, 1, :],
                                  ALU.subtract).then_inc(wgt_ready, 1)

            def gate_up0(n, bank):
                f, u = n // (NC0 + 1), n % 2
                shared = n % (NC0 + 1) == 0
                m = I0 if shared else P
                dst = hid0[f][0:m, NC0, :] if shared else sg[u][:]
                dve.wait_ge(th0_ready, n + 1)
                link(dve.scalar_tensor_tensor(sg[u][0:m, :], sg[u][0:m, :], 1.0, ps[0:m, bank, :], ALU.add, ALU.mult))
                dve.scalar_tensor_tensor(dst, sg[u][0:m, :], 0.5, ps[0:m, bank + 1, :], ALU.mult,
                                         ALU.mult).then_inc(gu_ready, 1)

            def weigh0(f, c, bank):
                n = (NC0 + 1) * f + 1 + c
                dve.wait_ge(wb_done, NC0 * f + c + 1)
                dve.wait_ge(gu_ready, n + 1)
                dve.tensor_tensor(hid0[f][:, c, :], sg[n % 2][:], ps[:, bank, :], ALU.mult).then_inc(hid0_ready, 1)

            def router_softmax(f, bank):
                dve.wait_ge(router_done, f + 1)
                r = ps[:, bank, 0:TH * E1].rearrange("p (t e) -> p t e", t=TH)
                if f:
                    dve.wait_ge(rexp_ready, f)
                link(dve.tensor_reduce(rmax[:], r, AX.X, ALU.max))
                dve.tensor_tensor(rdif[:], r, rmax[:][:, :, None].broadcast_to([P, TH, E1]),
                                  ALU.subtract).then_inc(rdif_ready, 1)

            def router_scores(f):
                dve.wait_ge(rexp_ready, f + 1)
                if f:
                    dve.wait_ge(score_ready, f)
                link(dve.tensor_reduce(rtot[:], rexp[:], AX.X, ALU.add))
                link(dve.reciprocal(rrec[:], rtot[:]))
                dve.tensor_tensor(score[f][:].rearrange("p q b e -> p b q e"),
                                  rexp[:].rearrange("p (b q) e -> p b q e", b=BH),
                                  rrec[:].rearrange("p (b q) -> p b q", b=BH)[:, :, :, None].broadcast_to([P, BH, QT, E1]),
                                  ALU.mult).then_inc(score_ready, 1)

            def choose_start(f, bank):
                dve.wait_ge(scoreT_done, f + 1)
                if f:
                    dve.wait_ge(slot_ready, f)
                dve.tensor_copy(sT[:], ps[0:BH * E1, bank, 0:S]).then_inc(sT_ready, 1)

            def choose_round(f, r):
                if r == 0:
                    dve.wait_ge(sT_ready, f + 1)
                cur = work if r else sT
                link(dve.max(m8[:], cur[:]))
                link(dve.match_replace(work[:], m8[:], cur[:], -1.0))

            def choose_end(f):
                assert CAP % 8 == 1
                link(dve.max(m8[:], work[:]))
                link(dve.max_index(m8ix[:], m8[:], work[:]))
                link(dve.tensor_copy(m8ixf[:], m8ix[:]))
                link(dve.tensor_scalar(chosen[:], iota_s, m8ixf[:, 0:1], None, ALU.is_equal))
                link(dve.scalar_tensor_tensor(chosen[:], work[:], -1.0, chosen[:], ALU.is_equal, ALU.add))
                link(dve.tensor_tensor_scan(slot_n[:], ones_s[:], chosen[:], 0.0, ALU.mult, ALU.add))
                dve.tensor_tensor(slot[:], slot_n[:], chosen[:], ALU.mult).then_inc(slot_ready, 1)

            def slotT_copy(f, bank):
                dve.wait_ge(slotT_done, f + 1)
                if f:
                    dve.wait_ge(onehot_ready, BH * f)
                dve.tensor_copy(slotT[:].rearrange("p q b e -> p (q b e)"),
                                ps[:, bank, 0:TH * E1]).then_inc(slotT_ready, 1)

            def make_onehot(f, bl):
                dve.wait_ge(slotT_ready, f + 1)
                dve.tensor_tensor(onehot[f][:, :, bl], iota_slot[:, None, None, :].broadcast_to([P, QT, E1, CAP]),
                                  slotT[:, :, bl][:, :, :, None].broadcast_to([P, QT, E1, CAP]),
                                  ALU.is_equal).then_inc(onehot_ready, 1)

            def y_bias(f, e, bank):
                dve.wait_ge(down1_done, E1 * f + e + 1)
                if f and e == 0:
                    dve.wait_ge(yTT_done, 2 * f)
                src = ps[:, bank, 0:BH * CAP].rearrange("p (b c) -> p b c", b=BH)
                dve.tensor_scalar(yT[:, :, e, :], src, cols_sb[:, C_B2 + e:C_B2 + e + 1], None,
                                  ALU.add).then_inc(yT_ready, 1)

            def y_copy(f, u, bank):
                n = (8, 2)[u]
                dve.wait_ge(yTT_done, 2 * f + u + 1)
                if f and u == 0:
                    dve.wait_ge(scatter_done, TH * f)
                src = ps[0:MS, bank:bank + 2 - u, :].rearrange("m n (i d) -> m (n i) d", d=D)[:, 0:n, :]
                dve.tensor_copy(y[:, 8 * u:8 * u + n, :], src).then_inc(y_ready, 1)

            def finish(f, t, bank):
                dve.wait_ge(scatter_done, TH * f + t + 1)
                dve.tensor_tensor(xb[f][:, t, :], ps[:, bank, 0:D], xs[f][:, t, :], ALU.add).then_inc(out_ready, 1)

            for step, *at in (
                (stats, 0), (normalise, 0), (k_prep, 0, 7), (stats, 1), (normalise, 1), (q_split, 0, 7),
                (q_split2, 0), (v_prep, 0, 6), (k_prep, 1, 5), (q_split, 1, 7), (q_split2, 1), (v_prep, 1, 4),
                (score_max, 0, 0, 0), (score_max, 0, 1, 2), (max_parts, 0, 0), (score_max, 0, 2, 0),
                (score_max, 0, 3, 2), (max_parts, 0, 1), (score_max, 1, 0, 0), (score_max, 1, 1, 2),
                (max_parts, 1, 0), (score_max, 1, 2, 0), (normalise_att, 0, 0, 4), (normalise_att, 0, 1, 6),
                (score_max, 1, 3, 0), (max_parts, 1, 1), (normalise_att, 0, 2, 4), (normalise_att, 0, 3, 6),
                (residual, 0, 4), (stats, 2), (normalise, 2), (normalise_att, 1, 0, 7), (normalise_att, 1, 1, 5),
                (normalise_att, 1, 2, 4), (normalise_att, 1, 3, 7), (gate_logits, 0, 5), (route, 0),
                (gate_up0, 0, 0), (residual, 1, 6), (stats, 3), (gate_up0, 1, 2), (weigh0, 0, 0, 5),
                (gate_up0, 2, 0), (normalise, 3), (weigh0, 0, 1, 4), (gate_up0, 3, 2), (gate_up0, 4, 0),
                (weigh0, 0, 2, 6), (weigh0, 0, 3, 7), (gate_up0, 5, 2), (weigh0, 0, 4, 5), (gate_up0, 6, 0),
                (weigh0, 0, 5, 4), (gate_logits, 1, 6), (gate_up0, 7, 2), (weigh0, 0, 6, 7), (gate_up0, 8, 0),
                (weigh0, 0, 7, 5), (route, 1), (gate_up0, 9, 2), (gate_up0, 10, 0), (residual, 2, 4), (stats, 4),
                (normalise, 4), (gate_up0, 11, 0), (weigh0, 1, 0, 5), (weigh0, 1, 1, 4), (gate_up0, 12, 2),
                (weigh0, 1, 2, 6), (gate_up0, 13, 0), (weigh0, 1, 3, 5), (q_split, 2, 7), (q_split2, 2),
                (gate_up0, 14, 2), (weigh0, 1, 4, 4), (gate_up0, 15, 0), (weigh0, 1, 5, 6), (gate_up0, 16, 2),
                (weigh0, 1, 6, 5), (gate_up0, 17, 0), (weigh0, 1, 7, 7), (score_max, 2, 0, 2), (score_max, 2, 1, 0),
                (max_parts, 2, 0), (score_max, 2, 2, 0), (score_max, 2, 3, 2), (max_parts, 2, 1), (residual, 3, 4),
                (stats, 5), (normalise, 5), (normalise_att, 2, 0, 7), (normalise_att, 2, 1, 5), (q_split, 3, 4),
                (q_split2, 3), (normalise_att, 2, 2, 7), (normalise_att, 2, 3, 6), (residual, 4, 4), (stats, 6),
                (normalise, 6), (score_max, 3, 0, 0), (score_max, 3, 1, 2), (max_parts, 3, 0), (score_max, 3, 2, 0),
                (router_softmax, 0, 6), (score_max, 3, 3, 2), (max_parts, 3, 1), (router_scores, 0),
                (choose_start, 0, 7), (choose_round, 0, 0), (choose_round, 0, 1), (choose_round, 0, 2),
                (choose_round, 0, 3), (choose_round, 0, 4), (choose_round, 0, 5), (choose_round, 0, 6),
                (normalise_att, 3, 0, 4), (choose_round, 0, 7), (normalise_att, 3, 1, 5), (choose_end, 0),
                (normalise_att, 3, 2, 6), (normalise_att, 3, 3, 7), (slotT_copy, 0, 4), (make_onehot, 0, 0),
                (make_onehot, 0, 1), (residual, 5, 6), (stats, 7), (normalise, 7), (router_softmax, 1, 4),
                (y_bias, 0, 0, 4), (router_scores, 1), (y_bias, 0, 1, 4), (choose_start, 1, 4), (choose_round, 1, 0),
                (choose_round, 1, 1), (choose_round, 1, 2), (choose_round, 1, 3), (choose_round, 1, 4),
                (choose_round, 1, 5), (choose_round, 1, 6), (choose_round, 1, 7), (choose_end, 1), (y_bias, 0, 2, 5),
                (y_bias, 0, 3, 6), (y_bias, 0, 4, 4), (slotT_copy, 1, 5), (make_onehot, 1, 0), (make_onehot, 1, 1),
                (y_bias, 0, 5, 7), (y_bias, 0, 6, 6), (y_bias, 0, 7, 4), (y_copy, 0, 0, 2), (y_copy, 0, 1, 5),
                (finish, 0, 0, 7), (finish, 0, 1, 6), (y_bias, 1, 0, 4), (y_bias, 1, 1, 5), (y_bias, 1, 2, 7),
                (y_bias, 1, 3, 6), (y_bias, 1, 4, 4), (finish, 0, 2, 5), (y_bias, 1, 5, 7), (finish, 0, 3, 6),
                (y_bias, 1, 6, 4), (y_bias, 1, 7, 5), (y_copy, 1, 0, 0), (y_copy, 1, 1, 6), (finish, 1, 0, 4),
                (finish, 1, 1, 5), (finish, 1, 2, 6), (finish, 1, 3, 7),
            ):
                step(*at)

        @block.tensor
        def _(pe):
            reader = {}

            def claim(banks, read, count):
                for wait in {reader[b] for b in banks if b in reader}:
                    pe.wait_ge(*wait)
                for b in banks:
                    reader[b] = read, count

            def turn_x(g, bank):
                h = g % NH
                claim([bank], xnT_ready, g + 1)
                if g == 0:
                    pe.wait_ge(ld_fc, 16)
                for t in range(TH):
                    pe.wait_ge(xn_ready, TH * g + t + 1)
                    ins = pe.transpose(ps[:, bank, t * P:(t + 1) * P], xn[h][:, t, :], ident)
                ins.then_inc(xT_done, 1)

            def project_q(a, bank):
                l, h = a // NH, a % NH
                claim([bank], q_rest_ready, a + 1)
                pe.wait_ge(xnT_ready, ATT_G[a] + 1)
                if h == 0:
                    pe.wait_ge(ld_wT[l], 16)
                pe.matmul(ps[:, bank, :], wT_sb[:, l, 0, :], xnT[h][:], start=True, stop=True).then_inc(q_done, 1)

            def project_k(l, bank):
                if l == 0:
                    pe.wait_ge(ld_ctx, 32)
                pe.wait_ge(ld_wT[l], 16)
                claim([bank], k32_ready, l + 1)
                pe.matmul(ps[:, bank, 0:B * S2].rearrange("p (b k) -> p b k", b=B), wT_sb[:, l, 1, :], ctx_sb[:, :, 0, :],
                          start=True, stop=True).then_inc(k_done, 1)

            def project_v(l, bank):
                claim([bank], v_ready, 2 * (l + 1))
                pe.wait_ge(ld_wT[l], 16)
                for b in range(B):
                    ins = pe.matmul(ps[:, bank, b * D:(b + 1) * D], ctx_sb[:, b].rearrange("d e k -> d (e k)"),
                                    wT_sb[:, l, 2, :], start=True, stop=True)
                ins.then_inc(v_done, 1)

            def scores(a, t, bank):
                l, h, b = a // NH, a % NH, BH * (a % NH) + t // QT
                claim([bank, bank + 1], max_ready, TH * a + t + 1)
                if t == 0:
                    pe.wait_ge(q_stacked[h], 16 * 6 * (l + 1))
                    if l == 0:
                        pe.wait_ge(ones_stacked[h], 16)
                    if h == 0:
                        pe.wait_ge(k_stacked[l], 16 * (6 + PARTS))
                for j in range(NP):
                    ins = pe.matmul(ps[:, bank + j // 4, (j % 4) * P:(j % 4 + 1) * P],
                                    q_stack[h][:, j, t * P:(t + 1) * P], k_stack[l][:, j, b, :], start=True, stop=True)
                ins.then_inc(s1_done, 1)

            def turn_max(a, bl, bank):
                claim([bank], nmT_ready, BH * a + bl + 1)
                pe.wait_ge(nm_ready, BH * a + bl + 1)
                if a == 0 and bl == 0:
                    pe.wait_ge(bf16_ready, 2)
                dst = ps[:, bank, :].bitcast(BF16)
                for qt in range(QT):
                    ins = pe.transpose(dst[0:PARTS * H, qt * P:(qt + 1) * P],
                                       nm_parts[bl][:, qt].rearrange("p c e -> p (c e)"), ident_b[:])
                ins.then_inc(nmT_done, 1)

            def scores_T(a, bl, n, bank):
                l, h, b = a // NH, a % NH, BH * (a % NH) + bl
                claim([bank], probs_ready, (NP // 2) * (BH * a + bl) + n + 1)
                if n == 0:
                    pe.wait_ge(nmT_ready, BH * a + bl + 1)
                for i in range(2):
                    j = 2 * n + i
                    dst = ps[:, bank, i * S:(i + 1) * S]
                    pe.matmul(dst, k_stack[l][:, j, b, :], q_stack[h][:, j, bl * S:(bl + 1) * S], start=True, stop=False)
                    ins = pe.matmul(dst, sel[:, j, :], nmT[bl][:], start=False, stop=True)
                ins.then_inc(s2_done, 1)

            def values(a, t, bank):
                l, b, bl, qt = a // NH, BH * (a % NH) + t // QT, t // QT, t % QT
                claim([bank], att_ready, TH * a + t + 1)
                if t == 0 and a % NH == 0:
                    pe.wait_ge(v_ready, 2 * (l + 1))
                if qt == 0:
                    pe.wait_ge(probs_ready, (NP // 2) * (BH * a + bl + 1))
                for j in range(NP):
                    ins = pe.matmul(ps[:, bank, j * 2 * (DK + 1):(j + 1) * 2 * (DK + 1)],
                                    probs[bl][:, j, qt * P:(qt + 1) * P],
                                    v_blk[l][:, b, j].rearrange("p e d -> p (e d)"), start=True, stop=True)
                ins.then_inc(av_done, 1)

            def turn_att(a, bank):
                claim([bank], attT_ready, a + 1)
                pe.wait_ge(att_ready, TH * (a + 1))
                for t in range(TH):
                    ins = pe.transpose(ps[:, bank, t * P:(t + 1) * P], att[:, t].rearrange("p e d -> p (e d)"), ident)
                ins.then_inc(attT_done, 1)

            def project_out(a, bank):
                claim([bank], x_ready, ATT_G[a] + 1)
                pe.wait_ge(attT_ready, a + 1)
                for t in range(TH):
                    ins = pe.matmul(ps[:, bank, t * D:(t + 1) * D], attT[:, t * P:(t + 1) * P], wT_sb[:, a // NH, 3, :],
                                    start=True, stop=True)
                ins.then_inc(wo_done, 1)

            def gate(f, bank):
                claim([bank], gate_lg, f + 1)
                pe.wait_ge(xnT_ready, NH + f + 1)
                for t in range(TH):
                    ins = pe.matmul(ps[:, bank, t * E0:(t + 1) * E0], xnT[f][:, t * P:(t + 1) * P],
                                    cols_sb[:, C_GW:C_GW + E0], start=True, stop=True)
                ins.then_inc(gate_done, 1)

            def turn_weights(f, bank):
                claim([bank], wgtT_ready, f + 1)
                pe.wait_ge(wgt_ready, f + 1)
                dst = ps[:, bank, :].bitcast(BF16)
                for t in range(TH):
                    ins = pe.transpose(dst[0:PARTS * E0, t * P:(t + 1) * P],
                                       wgt_parts[:, t].rearrange("p c e -> p (c e)"), ident_b[:])
                ins.then_inc(wgtT_done, 1)

            def up0(n, bank):
                f, i = divmod(n, NC0 + 1)
                c = (NC0, *range(NC0))[i]
                m = I0 if c == NC0 else P
                e = slice(2 * c, 2 * c + m // I0)
                claim([bank, bank + 1], gu_ready, n + 1)
                if n == 0:
                    pe.wait_ge(ld_gu, 32)
                if i == 0:
                    pe.wait_ge(xnT_ready, NH + f + 1)
                for k, w in enumerate((wg_sb, wu_sb)):
                    ins = pe.matmul(ps[0:m, bank + k, :], w[:, e, :].rearrange("d e i -> d (e i)"), xnT[f][:],
                                    start=True, stop=True)
                ins.then_inc(up0_done, 1)

            def spread_weights(f, c, bank):
                claim([bank], hid0_ready, NC0 * f + c + 1)
                if c == 0:
                    pe.wait_ge(wgtT_ready, f + 1)
                pe.matmul(ps[:, bank, :], sel[:, c, :], wgtT[:], start=True, stop=True).then_inc(wb_done, 1)

            def down0(f, t, bank):
                if t == 0:
                    claim([bank], x_ready, NH + f + 1)
                    if f == 0:
                        pe.wait_ge(ld_down, 32)
                    pe.wait_ge(gu_ready, (NC0 + 1) * (f + 1))
                    pe.wait_ge(hid0_ready, NC0 * (f + 1))
                for c in range(NC0 + 1):
                    k = I0 if c == NC0 else P
                    ins = pe.matmul(ps[:, bank, t * D:(t + 1) * D], hid0[f][0:k, c, t * P:(t + 1) * P], wd_sb[0:k, c, :],
                                    start=(c == 0), stop=(c == NC0))
                if t == TH - 1:
                    ins.then_inc(down0_done, 1)

            def router(f, bank):
                claim([bank], rdif_ready, f + 1)
                pe.wait_ge(xnT_ready, 3 * NH + f + 1)
                for t in range(TH):
                    ins = pe.matmul(ps[:, bank, t * E1:(t + 1) * E1], xnT[f][:, t * P:(t + 1) * P],
                                    cols_sb[:, C_RW:C_RW + E1], start=True, stop=True)
                ins.then_inc(router_done, 1)

            def turn_scores(f, bank):
                claim([bank], sT_ready, f + 1)
                pe.wait_ge(score_ready, f + 1)
                for qt in range(QT):
                    ins = pe.transpose(ps[0:BH * E1, bank, qt * P:(qt + 1) * P],
                                       score[f][:, qt].rearrange("p b e -> p (b e)"), ident)
                ins.then_inc(scoreT_done, 1)

            def turn_slots(f, bank):
                claim([bank], slotT_ready, f + 1)
                pe.wait_ge(slot_ready, f + 1)
                for qt in range(QT):
                    ins = pe.transpose(ps[:, bank, qt * BH * E1:(qt + 1) * BH * E1], slot[:, qt * P:(qt + 1) * P],
                                       ident[0:BH * E1, 0:BH * E1])
                ins.then_inc(slotT_done, 1)

            def gather(f, bl, bank):
                claim([bank, bank + 1], xsel_ready, BH * f + bl + 1)
                pe.wait_ge(onehot_ready, BH * f + bl + 1)
                for k in range(2):
                    for qt in range(QT):
                        ins = pe.matmul(ps[:, bank + k, 0:4 * CAP], xn[f][:, QT * bl + qt, :],
                                        onehot[f][:, qt, bl, 4 * k:4 * k + 4].rearrange("p e c -> p (e c)"),
                                        start=(qt == 0), stop=(qt == QT - 1))
                    ins.then_inc(gather_done, 1)

            def turn_gated(f, n, bank):
                claim([bank], gatedT_ready, 5 * f + n + 1)
                pe.wait_ge(gated_ready, f + 1)
                for i in range(4 * n, 4 * n + 4):
                    t, m = divmod(i, NM)
                    src = gated[:, t % QT, t // QT].rearrange("p e c -> p (e c)")[:, m * MS:(m + 1) * MS]
                    ins = pe.transpose(ps[0:MS, bank, (i % 4) * P:(i % 4 + 1) * P], src, ident)
                ins.then_inc(gatedT_done, 1)

            def up1(f, e, bank):
                claim([bank, bank + 1], hid1_ready, E1 * f + e + 1)
                if e == 0:
                    pe.wait_ge(xsel_ready, BH * (f + 1))
                    if f == 0:
                        pe.wait_ge(ld_w1, 16)
                for j in range(NJ):
                    ins = pe.matmul(ps[:, bank + j // 2, (j % 2) * BH * CAP:(j % 2 + 1) * BH * CAP],
                                    w1_sb[:, e, j * P:(j + 1) * P], xsel[:, e].rearrange("p b c -> p (b c)"),
                                    start=True, stop=True)
                ins.then_inc(up1_done, 1)

            def down1(f, e, bank):
                claim([bank], yT_ready, E1 * f + e + 1)
                pe.wait_ge(hid1_ready, E1 * f + e + 1)
                if f == 0 and e == 0:
                    pe.wait_ge(ld_w2, 16)
                for j in range(NJ):
                    ins = pe.matmul(ps[:, bank, 0:BH * CAP], w2_sb[:, e, j, :], hid1[e % 2][:, j, :],
                                    start=(j == 0), stop=(j == NJ - 1))
                ins.then_inc(down1_done, 1)

            def turn_y(f, u, bank):
                claim([bank, bank + 1] if u == 0 else [bank], y_ready, 2 * f + u + 1)
                pe.wait_ge(yT_ready, E1 * (f + 1))
                for i in range((8, 2)[u]):
                    bl, m = divmod(8 * u + i, NM)
                    src = yT[:, bl].rearrange("p e c -> p (e c)")[:, m * MS:(m + 1) * MS]
                    ins = pe.transpose(ps[0:MS, bank + i // 4, (i % 4) * D:(i % 4 + 1) * D], src, ident)
                ins.then_inc(yTT_done, 1)

            def scatter(f, t, bank):
                claim([bank], out_ready, TH * f + t + 1)
                if t == 0:
                    pe.wait_ge(gatedT_ready, 5 * (f + 1))
                    pe.wait_ge(y_ready, 2 * (f + 1))
                for m in range(NM):
                    ins = pe.matmul(ps[:, bank, 0:D], gatedT[:, NM * t + m, :], y[:, NM * (t // QT) + m, :],
                                    start=(m == 0), stop=(m == NM - 1))
                ins.then_inc(scatter_done, 1)

            for step, *at in (
                (project_k, 0, 7), (project_v, 0, 6), (project_k, 1, 5), (turn_x, 0, 4), (project_v, 1, 4),
                (project_q, 0, 7), (turn_x, 1, 7), (project_q, 1, 7), (scores, 0, 0, 0), (scores, 0, 1, 2),
                (scores, 0, 2, 0), (scores, 0, 3, 2), (turn_max, 0, 0, 6), (scores_T, 0, 0, 0, 5),
                (scores_T, 0, 0, 1, 7), (scores_T, 0, 0, 2, 4), (scores_T, 0, 0, 3, 6), (turn_max, 0, 1, 5),
                (scores, 1, 0, 0), (scores, 1, 1, 2), (scores_T, 0, 1, 0, 7), (scores_T, 0, 1, 1, 5),
                (scores, 1, 2, 0), (values, 0, 0, 4), (values, 0, 1, 6), (scores, 1, 3, 0), (turn_max, 1, 0, 7),
                (scores_T, 0, 1, 2, 5), (scores_T, 0, 1, 3, 4), (scores_T, 1, 0, 0, 6), (scores_T, 1, 0, 1, 7),
                (turn_max, 1, 1, 5), (values, 0, 2, 4), (values, 0, 3, 6), (scores_T, 1, 0, 2, 7),
                (scores_T, 1, 0, 3, 5), (turn_att, 0, 4), (scores_T, 1, 1, 0, 6), (scores_T, 1, 1, 1, 7),
                (scores_T, 1, 1, 2, 5), (project_out, 0, 4), (scores_T, 1, 1, 3, 6), (values, 1, 0, 7),
                (values, 1, 1, 5), (values, 1, 2, 4), (turn_x, 2, 6), (values, 1, 3, 7), (gate, 0, 5),
                (turn_att, 1, 4), (up0, 0, 0), (project_out, 1, 6), (up0, 1, 2), (turn_weights, 0, 7), (up0, 2, 0),
                (spread_weights, 0, 0, 5), (spread_weights, 0, 1, 4), (spread_weights, 0, 2, 6),
                (spread_weights, 0, 3, 7), (up0, 3, 2), (spread_weights, 0, 4, 5), (up0, 4, 0), (turn_x, 3, 4),
                (spread_weights, 0, 5, 4), (up0, 5, 2), (up0, 6, 0), (gate, 1, 6), (up0, 7, 2), (up0, 8, 0),
                (spread_weights, 0, 6, 7), (spread_weights, 0, 7, 5), (up0, 9, 2), (up0, 10, 0), (down0, 0, 0, 4),
                (down0, 0, 1, 4), (down0, 0, 2, 4), (down0, 0, 3, 4), (up0, 11, 0), (up0, 12, 2),
                (turn_weights, 1, 6), (turn_x, 4, 7), (spread_weights, 1, 0, 5), (spread_weights, 1, 1, 4),
                (spread_weights, 1, 2, 6), (up0, 13, 0), (project_q, 2, 7), (spread_weights, 1, 3, 5),
                (spread_weights, 1, 4, 4), (up0, 14, 2), (spread_weights, 1, 5, 6), (up0, 15, 0),
                (spread_weights, 1, 6, 5), (spread_weights, 1, 7, 7), (up0, 16, 2), (up0, 17, 0), (scores, 2, 0, 2),
                (scores, 2, 1, 0), (down0, 1, 0, 4), (scores, 2, 2, 0), (scores, 2, 3, 2), (down0, 1, 1, 4),
                (turn_max, 2, 0, 6), (down0, 1, 2, 4), (turn_max, 2, 1, 5), (down0, 1, 3, 4), (scores_T, 2, 0, 0, 7),
                (scores_T, 2, 0, 1, 6), (scores_T, 2, 0, 2, 5), (scores_T, 2, 0, 3, 4), (scores_T, 2, 1, 0, 7),
                (scores_T, 2, 1, 1, 6), (scores_T, 2, 1, 2, 5), (scores_T, 2, 1, 3, 4), (values, 2, 0, 7),
                (turn_x, 5, 6), (values, 2, 1, 5), (project_q, 3, 4), (values, 2, 2, 7), (values, 2, 3, 6),
                (turn_att, 2, 5), (project_out, 2, 4), (scores, 3, 0, 0), (scores, 3, 1, 2), (turn_x, 6, 7),
                (scores, 3, 2, 0), (router, 0, 6), (scores, 3, 3, 2), (turn_max, 3, 0, 5), (scores_T, 3, 0, 0, 4),
                (scores_T, 3, 0, 1, 7), (scores_T, 3, 0, 2, 6), (turn_max, 3, 1, 5), (scores_T, 3, 0, 3, 4),
                (turn_scores, 0, 7), (scores_T, 3, 1, 0, 5), (scores_T, 3, 1, 1, 7), (scores_T, 3, 1, 2, 6),
                (values, 3, 0, 4), (values, 3, 1, 5), (scores_T, 3, 1, 3, 7), (values, 3, 2, 6), (values, 3, 3, 7),
                (turn_slots, 0, 4), (turn_att, 3, 5), (project_out, 3, 6), (gather, 0, 0, 0), (gather, 0, 1, 2),
                (turn_x, 7, 7), (up1, 0, 0, 0), (router, 1, 4), (up1, 0, 1, 2), (turn_gated, 0, 0, 5),
                (turn_gated, 0, 1, 6), (turn_gated, 0, 2, 7), (down1, 0, 0, 4), (up1, 0, 2, 0), (down1, 0, 1, 4),
                (up1, 0, 3, 2), (turn_scores, 1, 4), (turn_gated, 0, 3, 4), (up1, 0, 4, 0), (up1, 0, 5, 2),
                (down1, 0, 2, 5), (down1, 0, 3, 6), (turn_gated, 0, 4, 7), (up1, 0, 6, 0), (down1, 0, 4, 4),
                (down1, 0, 5, 7), (up1, 0, 7, 2), (turn_slots, 1, 5), (down1, 0, 6, 6), (down1, 0, 7, 4),
                (gather, 1, 0, 0), (turn_y, 0, 0, 2), (turn_y, 0, 1, 5), (gather, 1, 1, 0), (scatter, 0, 0, 7),
                (up1, 1, 0, 0), (up1, 1, 1, 2), (scatter, 0, 1, 6), (up1, 1, 2, 0), (down1, 1, 0, 4), (up1, 1, 3, 2),
                (down1, 1, 1, 5), (up1, 1, 4, 0), (down1, 1, 2, 7), (up1, 1, 5, 2), (down1, 1, 3, 6), (up1, 1, 6, 0),
                (down1, 1, 4, 4), (scatter, 0, 2, 5), (up1, 1, 7, 2), (down1, 1, 5, 7), (scatter, 0, 3, 6),
                (down1, 1, 6, 4), (down1, 1, 7, 5), (turn_gated, 1, 0, 7), (turn_gated, 1, 1, 6),
                (turn_gated, 1, 2, 4), (turn_y, 1, 0, 0), (turn_gated, 1, 3, 5), (turn_gated, 1, 4, 7),
                (turn_y, 1, 1, 6), (scatter, 1, 0, 4), (scatter, 1, 1, 5), (scatter, 1, 2, 6), (scatter, 1, 3, 7),
            ):
                step(*at)


def host_constants():
    f = np.zeros((P, F_N), np.float32)
    f[:, F_ID:F_ID + P] = np.eye(P)
    f[:, F_MASK] = (np.arange(P) // DK) % 2 == 0
    f[:, F_MASK + 1] = (np.arange(P) // DK) % 2 == 1
    f[:, F_SLOT:F_SLOT + CAP] = np.arange(1, CAP + 1)
    f[:, F_E0:F_E0 + E0] = np.arange(E0)
    f[:, F_S:F_S + S] = np.arange(S)
    b = np.zeros((PARTS * H, NP * P), np.float32)
    for r in range(PARTS * H):
        j, e = divmod(r % H, 2)
        b[r, j * P + e * S2:j * P + (e + 1) * S2] = 1
    return f, b


def kernel(x, ctx_1024, condB_tau, fside_BxS2_0,
           L0_xcond_Wq, L0_xcond_bq, L0_xcond_Wk, L0_xcond_bk, L0_xcond_Wv, L0_xcond_bv, L0_xcond_Wo, L0_xcond_bo,
           L0_ffn_gate_w, L0_ffn_gate_b, L0_ffn_shared_wg, L0_ffn_shared_wu, L0_ffn_shared_wd,
           L0_ffn_experts_wg, L0_ffn_experts_wu, L0_ffn_experts_wd,
           L1_xcond_Wq, L1_xcond_bq, L1_xcond_Wk, L1_xcond_bk, L1_xcond_Wv, L1_xcond_bv, L1_xcond_Wo, L1_xcond_bo,
           L1_ffn_router_w, L1_ffn_w1, L1_ffn_b1, L1_ffn_w2, L1_ffn_b2):
    import concourse.bacc as _bacc
    from concourse.bass_utils import run_bass_kernel_spmd as _run

    a = np.ascontiguousarray
    fconst, selection = host_constants()
    ws = [[L0_xcond_Wq, L0_xcond_Wk, L0_xcond_Wv, L0_xcond_Wo], [L1_xcond_Wq, L1_xcond_Wk, L1_xcond_Wv, L1_xcond_Wo]]
    arrays = {
        "x": a(x),
        "ctxT": a(np.asarray(ctx_1024).reshape(B * S2, D).T),
        "wT": a(np.stack([np.stack([np.asarray(w).T for w in l], 1) for l in ws], 1)),
        "cols": a(np.concatenate([
            np.stack([L0_xcond_bq, L1_xcond_bq, L0_xcond_bk, L1_xcond_bk], 1),
            np.asarray(L1_ffn_b1).reshape(E1 * NJ, P).T, np.asarray(L1_ffn_b2).T,
            np.asarray(L0_ffn_gate_w), np.asarray(L1_ffn_router_w).T], 1)),
        "rows": a(np.concatenate([L0_xcond_bv, L1_xcond_bv, L0_xcond_bo, L1_xcond_bo, L0_ffn_gate_b, condB_tau])),
        "delta": a(fside_BxS2_0),
        "wg": a(np.concatenate([L0_ffn_experts_wg, np.asarray(L0_ffn_shared_wg)[None]]).transpose(1, 0, 2)),
        "wu": a(np.concatenate([L0_ffn_experts_wu, np.asarray(L0_ffn_shared_wu)[None]]).transpose(1, 0, 2)),
        "wd": a(np.asarray(L0_ffn_experts_wd).reshape(NC0, P, D).transpose(1, 0, 2)),
        "wds": a(L0_ffn_shared_wd),
        "w1": a(np.asarray(L1_ffn_w1).transpose(1, 0, 2)),
        "w2": a(np.asarray(L1_ffn_w2).reshape(E1, NJ, P, D).transpose(2, 0, 1, 3)),
        "fconst": fconst,
        "selection": selection,
    }
    nc = _bacc.Bacc("TRN2", target_bir_lowering=False, num_devices=1)
    args = [nc.dram_tensor(f"in_{n}", v.shape, mybir.dt.from_np(v.dtype), kind="ExternalInput").ap()
            for n, v in arrays.items()]
    args.append(nc.dram_tensor("out_x", (B, S, D), F32, kind="ExternalOutput").ap())
    build(nc, *args)
    r = _run(nc, [{f"in_{n}": v for n, v in arrays.items()}], core_ids=[0])
    return r.results[0]["out_x"]
```

```python
from contextlib import ExitStack

import concourse.bass as bass
import numpy as np
from concourse import mybir

F32 = mybir.dt.float32
BF16 = mybir.dt.bfloat16
U32 = mybir.dt.uint32
ALU = mybir.AluOpType
ACT = mybir.ActivationFunctionType
AX = mybir.AxisListType

P = 128
B, S, D = 4, 256, 128
S2 = 64
H, DK = 16, 8
NL = 2
NH = 2
BH = B // NH
QT = S // P
TH = BH * QT
TOK = TH * P
NP = H // 2
PR = 2 * DK
VC = 32
PARTS = 3
KSTK = 6 * PR
KROWS = KSTK + PARTS
RUNS = ((0, 3), (3, 2), (5, 1))
E0, I0 = 16, 64
NC0 = E0 * I0 // P
E1, HID = 8, 512
NJ = HID // P
CAP = max(1, int(S * 2.0 / E1) + 1)
SLOTS = E1 * CAP
NM = 5
MS = SLOTS // NM
assert MS * NM == SLOTS and MS <= P
EPS = 1e-5
ISQ = float(1.0 / np.sqrt(np.float32(DK)))
ATT_G = (0, 1, 4, 5)

C_BQ, C_BK, C_B1, C_B2, C_GW, C_RW = 0, 2, 4, 4 + E1 * NJ, 4 + E1 * NJ + E1, 4 + E1 * NJ + E1 + E0
C_N = C_RW + E1
R_BV, R_BO, R_GB, R_TAU = 0, 2 * D, 4 * D, 4 * D + E0
R_N = R_TAU + B
F_ID, F_SLOT, F_E0, F_S = 0, P, P + CAP, P + CAP + E0
F_N = F_S + S


def build(nc, x, ctxT, wT, cols, rows, delta, wg, wu, wd, wds, w1, w2, selection, out):
    q_scratch = nc.dram_tensor("q_scratch", [NH, PARTS, P, TOK], BF16, kind="Internal").ap()
    k_scratch = nc.dram_tensor("k_scratch", [NL, PARTS, P, B, 2, S2], BF16, kind="Internal").ap()
    delta_scratch = nc.dram_tensor("delta_scratch", [PARTS, B, 2, S2], BF16, kind="Internal").ap()
    x_tiles = x.rearrange("b (q p) d -> (b q) p d", p=P)
    out_tiles = out.rearrange("b (q p) d -> (b q) p d", p=P)

    with ExitStack() as ctx:
        def sb(name, shape, dt=F32):
            return ctx.enter_context(nc.sbuf_tensor(name, shape, dt))

        def sem(name):
            return ctx.enter_context(nc.semaphore(name))

        wT_sb = sb("wT_sb", [P, NL, 4, D])
        ctx_sb = sb("ctx_sb", [P, B, 2, S2])
        cols_fc = sb("cols_fc", [P, C_N + F_N])
        rows_sb = sb("rows_sb", [P, R_N])
        zeros_b = sb("zeros_b", [P, P], BF16)
        ident_b = sb("ident_b", [P, P], BF16)
        sel_b = sb("sel_b", [PARTS * H, NP * P], BF16)
        wg_sb = sb("wg_sb", [P, E0 + 1, I0])
        wu_sb = sb("wu_sb", [P, E0 + 1, I0])
        wd_sb = sb("wd_sb", [P, NC0 + 1, D])
        w1_sb = sb("w1_sb", [P, E1, HID])
        w2_sb = sb("w2_sb", [P, E1, NJ, D])
        cols_sb = cols_fc[:, 0:C_N]
        fc = cols_fc[:, C_N:]
        ident = fc[:, F_ID:F_ID + P]
        iota_slot = fc[:, F_SLOT:F_SLOT + CAP]
        iota_e0 = fc[:, F_E0:F_E0 + E0]
        iota_s = fc[0:2 * E1, F_S:F_S + S]
        sel = sel_b[:].rearrange("r (j c) -> r j c", j=NP)
        xs = [sb(f"xs{h}", [P, TH, D]) for h in range(NH)]
        xn = [sb(f"xn{h}", [P, TH, D]) for h in range(NH)]
        xb = [sb(f"xb{h}", [P, TH, D]) for h in range(NH)]
        xnT = [sb(f"xnT{h}", [P, TOK]) for h in range(NH)]
        bn6 = sb("bn6", [P, TH, 6])
        mv = [sb(f"mv{h}", [P, TH, 2]) for h in range(NH)]
        veps = [sb(f"veps{h}", [P, TH]) for h in range(NH)]
        rstd = [sb(f"rstd{h}", [P, TH]) for h in range(NH)]
        mhalf = sb("mhalf", [P, TH])
        q_rest = sb("q_rest", [P, TOK])
        q_parts = [sb(f"q_parts{h}", [P, PARTS, TOK], BF16) for h in range(NH)]
        q_stack = [sb(f"q_stack{h}", [KROWS, NP, TOK], BF16) for h in range(NH)]
        tau_s = sb("tau_s", [P, B])
        k32 = sb("k32", [P, B, S2])
        k_part = sb("k_part", [P, PARTS, B, S2], BF16)
        k_masked = sb("k_masked", [P, PARTS, B, 2, S2], BF16)
        k_rest = sb("k_rest", [P, B, S2])
        k_stack = [sb(f"k_stack{l}", [KROWS, NP, B, 2 * S2], BF16) for l in range(NL)]
        v_pad = [sb(f"v_pad{l}", [P, B, NP, VC]) for l in range(NL)]
        v_blk = [v[:, :, :, 0:2 * (DK + 1)].rearrange("p b j (e d) -> p b j e d", e=2) for v in v_pad]
        negmax = sb("negmax", [P, TH, H])
        nm_parts = [sb(f"nm_parts{i}", [P, QT, PARTS, H], BF16) for i in range(BH)]
        nm_rest = sb("nm_rest", [P, QT, H])
        nmT = [sb(f"nmT{i}", [PARTS * H, S], BF16) for i in range(BH)]
        probs_sb = sb("probs_sb", [P, BH, NP, S])
        probs = [probs_sb[:, i] for i in range(BH)]
        att_u = [sb(f"att_u{i}", [P, TOK]) for i in range(BH)]
        rsum = sb("rsum", [P, TH, H])
        att = sb("att", [P, TH, H, DK])
        attT = sb("attT", [P, TOK])
        lg = sb("lg", [P, TH, E0])
        th = sb("th", [P, TH, E0])
        sig = sb("sig", [P, TH, E0])
        top8 = sb("top8", [P, TH, 8])
        top_ix = sb("top_ix", [P, TH, 8], U32)
        top_ixf = sb("top_ixf", [P, TH, 8])
        vsum = sb("vsum", [P, TH])
        vrec = sb("vrec", [P, TH])
        vnorm = sb("vnorm", [P, TH, 2])
        pick = sb("pick", [P, TH, 2, E0])
        wgt = sb("wgt", [P, TH, E0])
        wgt_rest = sb("wgt_rest", [P, TH, E0])
        wgt_parts = sb("wgt_parts", [P, TH, PARTS, E0], BF16)
        wgtT = sb("wgtT", [PARTS * E0, TOK], BF16)
        sg = [sb(f"sg{i}", [P, TOK]) for i in range(2)]
        hid0 = [sb(f"hid0{h}", [P, NC0 + 1, TOK]) for h in range(NH)]
        rmax = sb("rmax", [P, TH])
        rdif = sb("rdif", [P, TH, E1])
        rexp = sb("rexp", [P, TH, E1])
        rtot = sb("rtot", [P, TH])
        rrec = sb("rrec", [P, TH])
        score = [sb(f"score{h}", [P, QT, BH, E1]) for h in range(NH)]
        wb_sb = sb("wb_sb", [P, 2, TOK])
        rows4 = wb_sb[0:BH * E1].rearrange("r i (k s) -> r (i k) s", s=S)
        sT, work, chosen, slot_n = (rows4[:, i, :] for i in range(4))
        m8 = sb("m8", [BH * E1, 8])
        m8ix = sb("m8ix", [BH * E1, 8], U32)
        m8ixf = sb("m8ixf", [BH * E1, 8])
        ones_s = sb("ones_s", [BH * E1, S])
        slot = sb("slot", [BH * E1, S])
        slotT = sb("slotT", [P, QT, BH, E1])
        W1H, W1X = QT * BH * SLOTS, BH * SLOTS
        free0 = hid0[0][:].rearrange("p c s -> p (c s)")
        free1 = hid0[1][:].rearrange("p c s -> p (c s)")
        sel32 = free0[0:PARTS * H, 0:NP * P]
        early = free0[0:B, NP * P:]
        dl32, dl_rest = early[:, 0:S2], early[:, S2:2 * S2]
        dl_parts = early[:, 2 * S2:2 * S2 + PARTS * S2 // 2].bitcast(BF16).rearrange("b (c k) -> b c k", c=PARTS)
        ones_b = early[0:PARTS, 4 * S2:4 * S2 + TOK // 2].bitcast(BF16)
        onehot = [free0[:, h * W1H:(h + 1) * W1H].rearrange("p (q b e c) -> p q b e c", q=QT, b=BH, e=E1)
                  for h in range(NH)]
        gated = free1[:, 0:W1H].rearrange("p (q b e c) -> p q b e c", q=QT, b=BH, e=E1)
        xsel = free1[:, W1H:W1H + W1X].rearrange("p (e b c) -> p e b c", e=E1, b=BH)
        yT = free1[:, W1H + W1X:W1H + 2 * W1X].rearrange("p (b e c) -> p b e c", b=BH, e=E1)
        free2 = probs_sb[0:MS].rearrange("p i j s -> p (i j s)")
        gatedT = free2[:, 0:TH * NM * P].rearrange("m (i s) -> m i s", s=P)
        y = free2[:, TH * NM * P:TH * NM * P + BH * NM * D].rearrange("m (i d) -> m i d", d=D)
        free3 = wg_sb[:].rearrange("p e i -> p (e i)")
        hid1 = [free3[:, i * NJ * BH * CAP:(i + 1) * NJ * BH * CAP].rearrange("p (j c) -> p j c", j=NJ) for i in range(2)]

        ps = ctx.enter_context(nc.psum_tensor("ps", [P, 8, 512], F32))

        ld_x = [sem(f"ld_x{h}") for h in range(NH)]
        ld_ctx = sem("ld_ctx")
        ld_wT = [sem(f"ld_wT{l}") for l in range(NL)]
        ld_cols = sem("ld_cols")
        ld_rows = sem("ld_rows")
        ld_sel = sem("ld_sel")
        ld_delta = sem("ld_delta")
        ld_gu = sem("ld_gu")
        ld_down = sem("ld_down")
        ld_w1 = sem("ld_w1")
        ld_w2 = sem("ld_w2")
        q_hi_ready = sem("q_hi_ready")
        q_mid_ready = sem("q_mid_ready")
        q_lo_ready = sem("q_lo_ready")
        q_out = sem("q_out")
        q_stacked = [sem(f"q_stacked{h}") for h in range(NH)]
        k_parts_ready = sem("k_parts_ready")
        k_out = sem("k_out")
        zeros_ready = sem("zeros_ready")
        zeros_b_ready = sem("zeros_b_ready")
        k_masked_ready = sem("k_masked_ready")
        k_stacked = [sem(f"k_stacked{l}") for l in range(NL)]
        delta_ready = sem("delta_ready")
        delta_out = sem("delta_out")
        delta_stacked = [sem(f"delta_stacked{l}") for l in range(NL)]
        ones_ready = sem("ones_ready")
        ones_stacked = [sem(f"ones_stacked{h}") for h in range(NH)]
        bf16_ready = sem("bf16_ready")
        dve_step = sem("dve_step")
        pool_step = sem("pool_step")
        stats_ready = sem("stats_ready")
        rstd_ready = sem("rstd_ready")
        xn_ready = sem("xn_ready")
        xb_ready = sem("xb_ready")
        xT_done = sem("xT_done")
        xnT_ready = sem("xnT_ready")
        x_ready = sem("x_ready")
        fill_done = sem("fill_done")
        k_done = sem("k_done")
        v_done = sem("v_done")
        k32_ready = sem("k32_ready")
        v_ready = sem("v_ready")
        q_rest_ready = sem("q_rest_ready")
        q_done = sem("q_done")
        s1_done = sem("s1_done")
        max_ready = sem("max_ready")
        nm_ready = sem("nm_ready")
        nmT_done = sem("nmT_done")
        nmT_ready = sem("nmT_ready")
        s2_done = sem("s2_done")
        probs_ready = sem("probs_ready")
        av_done = sem("av_done")
        att_u_ready = sem("att_u_ready")
        att_u_turned = sem("att_u_turned")
        att_ready = sem("att_ready")
        attT_done = sem("attT_done")
        attT_ready = sem("attT_ready")
        wo_done = sem("wo_done")
        gate_done = sem("gate_done")
        gate_lg = sem("gate_lg")
        gate_th = sem("gate_th")
        wgt_ready = sem("wgt_ready")
        wgtT_done = sem("wgtT_done")
        wgtT_ready = sem("wgtT_ready")
        up0_done = sem("up0_done")
        wb_done = sem("wb_done")
        wb_ready = sem("wb_ready")
        th0_ready = sem("th0_ready")
        gu_ready = sem("gu_ready")
        hid0_ready = sem("hid0_ready")
        down0_done = sem("down0_done")
        router_done = sem("router_done")
        rdif_ready = sem("rdif_ready")
        rexp_ready = sem("rexp_ready")
        score_ready = sem("score_ready")
        scoreT_done = sem("scoreT_done")
        sT_ready = sem("sT_ready")
        slot_ready = sem("slot_ready")
        slotT_done = sem("slotT_done")
        slotT_ready = sem("slotT_ready")
        onehot_ready = sem("onehot_ready")
        gated_ready = sem("gated_ready")
        gather_done = sem("gather_done")
        xsel_ready = sem("xsel_ready")
        gatedT_done = sem("gatedT_done")
        gatedT_ready = sem("gatedT_ready")
        up1_done = sem("up1_done")
        hid1_ready = sem("hid1_ready")
        down1_done = sem("down1_done")
        yT_ready = sem("yT_ready")
        yTT_done = sem("yTT_done")
        y_ready = sem("y_ready")
        scatter_done = sem("scatter_done")
        out_ready = sem("out_ready")
        stored = sem("stored")

        block = ctx.enter_context(nc.Block())

        @block.sync
        def _(sp):
            def load_x(h):
                sp.dma_start(xs[h][:], x_tiles[TH * h:TH * h + TH].rearrange("t p d -> p t d")).then_inc(ld_x[h], 16)

            load_x(0)
            ctx_twice = ctxT.rearrange("d (b k) -> d b k", b=B)[:, :, None, :].broadcast_to([P, B, 2, S2])
            sp.dma_start(ctx_sb[:], ctx_twice).then_inc(ld_ctx, 16)
            load_x(1)
            sp.dma_start(sel32, selection).then_inc(ld_sel, 16)

            def ones_rows(h):
                src = ones_b[:, None, :].broadcast_to([PARTS, NP, TOK])
                sp.dma_start(q_stack[h][KSTK:KROWS], src).then_inc(ones_stacked[h], 16)

            def delta_write():
                sp.wait_ge(delta_ready, 1)
                for e in range(2):
                    sp.dma_start(delta_scratch.rearrange("c b e k -> b c e k")[:, :, e, :], dl_parts).then_inc(delta_out, 16)

            def delta_rows(l):
                src = delta_scratch.rearrange("c b e k -> c (b e k)")[:, None, :].broadcast_to([PARTS, NP, B * 2 * S2])
                dst = k_stack[l][KSTK:KROWS].rearrange("r j b n -> r j (b n)")
                sp.dma_start(dst, src).then_inc(delta_stacked[l], 16)

            def k_write(l):
                sp.wait_ge(k_masked_ready, 2 * (l + 1))
                sp.dma_start(k_scratch[l].rearrange("c p b e k -> p c (b e k)"),
                             k_masked[:].rearrange("p c b e k -> p c (b e k)")).then_inc(k_out, 16)

            def k_read(l):
                sp.wait_ge(k_out, 16 * (l + 1))
                for first, n in RUNS:
                    src = k_scratch[l, PARTS - n:].rearrange("c (r j) b e k -> (c r) j (b e k)", r=PR)
                    dst = k_stack[l][PR * first:PR * (first + n)].rearrange("r j b n -> r j (b n)")
                    sp.dma_start(dst, src).then_inc(k_stacked[l], 16)

            def q_write(a, c):
                h = a % NH
                sp.wait_ge((q_hi_ready, q_mid_ready, q_lo_ready)[c], a + 1)
                sp.dma_start(q_scratch[h, c], q_parts[h][:, c, :]).then_inc(q_out, 16)

            def q_read(a):
                h = a % NH
                sp.wait_ge(q_out, 16 * PARTS * (a + 1))
                for first, n in RUNS:
                    src = q_scratch[h, 0:n].rearrange("c (r j) n -> (c r) j n", r=PR)
                    sp.dma_start(q_stack[h][PR * first:PR * (first + n)], src).then_inc(q_stacked[h], 16)

            sp.wait_ge(ones_ready, 1)
            ones_rows(0)
            delta_write()
            k_write(0)
            q_write(0, 0)
            k_read(0)
            sp.wait_ge(delta_out, 32)
            delta_rows(0)
            q_write(0, 1)
            q_write(0, 2)
            q_read(0)
            ones_rows(1)
            for c in range(PARTS):
                q_write(1, c)
            q_read(1)
            k_write(1)
            k_read(1)
            delta_rows(1)
            for a in (2, 3):
                for c in range(PARTS):
                    q_write(a, c)
                q_read(a)
            for n in range(NH * TH):
                sp.wait_ge(out_ready, n + 1)
                sp.dma_start(out_tiles[n], xb[n // TH][:, n % TH, :]).then_inc(stored, 16)
            sp.wait_ge(stored, 16 * NH * TH)

        @block.gpsimd
        def _(pool):
            steps = [0]

            def link(ins):
                steps[0] += 1
                ins.then_inc(pool_step, 1)
                pool.wait_ge(pool_step, steps[0])

            pool.dma_start(dl32, delta).then_inc(ld_delta, 16)
            link(pool.memset(mhalf[:], -0.5))
            pool.memset(k_masked[:], 0.0).then_inc(zeros_ready, 1)
            pool.memset(ones_b, 1.0).then_inc(ones_ready, 1)

            def delta_parts():
                pool.wait_ge(ld_delta, 16)
                link(pool.tensor_scalar(dl32, dl32, ISQ, None, ALU.mult))
                link(pool.tensor_copy(dl_parts[:, 0, :], dl32))
                link(pool.tensor_tensor(dl_rest, dl32, dl_parts[:, 0, :], ALU.subtract))
                link(pool.tensor_copy(dl_parts[:, 1, :], dl_rest))
                pool.tensor_tensor(dl_parts[:, 2, :], dl_rest, dl_parts[:, 1, :], ALU.subtract).then_inc(delta_ready, 1)

            def fill():
                link(pool.memset(ones_s[:], 1.0))
                for l in range(NL):
                    link(pool.memset(v_pad[l][:], 0.0))
                    link(pool.memset(v_blk[l][0:S2, :, :, 0, DK:DK + 1], 1.0))
                    pool.memset(v_blk[l][S2:2 * S2, :, :, 1, DK:DK + 1], 1.0).then_inc(fill_done, 1)
                    pool.wait_ge(fill_done, l + 1)

            def root(g):
                h = g % NH
                pool.wait_ge(stats_ready, g + 1)
                if g >= NH:
                    pool.wait_ge(xn_ready, TH * (g - 1))
                link(pool.tensor_scalar(veps[h][:], mv[h][:, :, 1], EPS, None, ALU.add))
                pool.tensor_tensor(rstd[h][:], veps[h][:], mhalf[:], ALU.pow).then_inc(rstd_ready, 1)

            def residual_base(g):
                h = g % NH
                if g in ATT_G:
                    l = ATT_G.index(g) // NH
                    bo = rows_sb[:, R_BO + l * D:R_BO + (l + 1) * D][:, None, :].broadcast_to([P, TH, D])
                    if g < NH:
                        pool.wait_ge(ld_x[h], 16)
                        pool.wait_ge(ld_rows, 16)
                    else:
                        pool.wait_ge(x_ready, g - 1)
                    pool.tensor_tensor(xb[h][:], xs[h][:], bo, ALU.add).then_inc(xb_ready, 1)
                elif g < 6:
                    pool.wait_ge(xn_ready, TH * (g + 1))
                    pool.tensor_tensor(xb[h][:], xs[h][:], xn[h][:], ALU.add).then_inc(xb_ready, 1)

            def gate_onehot(f):
                pool.wait_ge(onehot_ready, BH * (f + 1))
                if f:
                    pool.wait_ge(gatedT_done, 5 * f)
                sc = score[f][:].rearrange("p q b e -> p (q b e)")[:, :, None].broadcast_to([P, TH * E1, CAP])
                pool.tensor_tensor(gated[:].rearrange("p q b e c -> p (q b e) c"),
                                   onehot[f][:].rearrange("p q b e c -> p (q b e) c"), sc, ALU.mult).then_inc(gated_ready, 1)

            def weigh0(f, c):
                n = (NC0 + 1) * f + 1 + c
                pool.wait_ge(wb_ready, NC0 * f + c + 1)
                pool.wait_ge(gu_ready, n + 1)
                pool.tensor_tensor(hid0[f][:, c, :], sg[n % 2][:], wb_sb[:, c % 2, :],
                                   ALU.mult).then_inc(hid0_ready, 1)

            def load_experts0():
                pool.wait_ge(q_stacked[1], 16 * len(RUNS))
                pool.dma_start(wg_sb[:], wg).then_inc(ld_gu, 16)
                pool.dma_start(wu_sb[:], wu).then_inc(ld_gu, 16)
                pool.dma_start(wd_sb[:, 0:NC0], wd).then_inc(ld_down, 16)
                pool.dma_start(wd_sb[0:I0, NC0], wds).then_inc(ld_down, 16)

            def load_experts1():
                pool.wait_ge(k_stacked[1], 16 * len(RUNS))
                pool.dma_start(w1_sb[:], w1).then_inc(ld_w1, 16)
                pool.dma_start(w2_sb[:], w2).then_inc(ld_w2, 16)

            for step, *at in (
                (delta_parts,), (root, 0), (fill,), (residual_base, 0), (root, 1), (residual_base, 1),
                (load_experts0,), (load_experts1,), (root, 2), (residual_base, 2), (root, 3), (weigh0, 0, 0),
                (weigh0, 0, 1), (residual_base, 3), (weigh0, 0, 2), (weigh0, 0, 3), (weigh0, 0, 4), (weigh0, 0, 5),
                (weigh0, 0, 6), (weigh0, 0, 7), (weigh0, 1, 0), (weigh0, 1, 1), (weigh0, 1, 2), (weigh0, 1, 3),
                (root, 4), (weigh0, 1, 4), (weigh0, 1, 5), (residual_base, 4), (weigh0, 1, 6), (weigh0, 1, 7),
                (root, 5), (residual_base, 5), (root, 6), (root, 7), (gate_onehot, 0), (gate_onehot, 1),
            ):
                step(*at)

        @block.scalar
        def _(act):
            act.dma_start(wT_sb[:, 0], wT[:, 0]).then_inc(ld_wT[0], 16)
            act.dma_start(cols_fc[:], cols).then_inc(ld_cols, 16)
            act.dma_start(rows_sb[:], rows.partition_broadcast(P)).then_inc(ld_rows, 16)
            act.dma_start(wT_sb[:, 1], wT[:, 1]).then_inc(ld_wT[1], 16)

            def narrow_constants():
                act.wait_ge(ld_sel, 16)
                act.activation(sel_b[:], sel32, ACT.Copy).then_inc(bf16_ready, 1)
                act.wait_ge(ld_cols, 16)
                act.activation(ident_b[:], ident, ACT.Copy).then_inc(bf16_ready, 1)

            def xnT_copy(g, bank):
                act.wait_ge(xT_done, g + 1)
                act.activation(xnT[g % NH][:], ps[:, bank, :], ACT.Copy).then_inc(xnT_ready, 1)

            def q_hi(a, bank):
                l, h = a // NH, a % NH
                act.wait_ge(q_done, a + 1)
                if a == 0:
                    act.wait_ge(ld_cols, 16)
                act.activation(q_parts[h][:, 0, :], ps[:, bank, :], ACT.Identity,
                               bias=cols_sb[:, C_BQ + l:C_BQ + l + 1]).then_inc(q_hi_ready, 1)

            def mask_k(l):
                act.wait_ge(k_parts_ready, l + 1)
                if l:
                    act.wait_ge(k_out, 16 * l)
                else:
                    act.wait_ge(zeros_ready, 1)
                for e in range(2):
                    r = slice(P // 2 * e, P // 2 * (e + 1))
                    act.activation(k_masked[r, :, :, e, :], k_part[r], ACT.Copy).then_inc(k_masked_ready, 1)

            def nmT_copy(a, bl, bank):
                act.wait_ge(nmT_done, BH * a + bl + 1)
                act.activation(nmT[bl][:], ps[:, bank, :].bitcast(BF16)[0:PARTS * H, 0:S], ACT.Copy).then_inc(nmT_ready, 1)

            def exp(a, bl, n, bank):
                if a and n == 0:
                    act.wait_ge(av_done, BH * (a - 1) + bl + 1)
                act.wait_ge(s2_done, (NP // 2) * (BH * a + bl) + n + 1)
                act.activation(probs[bl][:, 2 * n:2 * n + 2, :], ps[:, bank, :].rearrange("p (j s) -> p j s", j=2),
                               ACT.Exp).then_inc(probs_ready, 1)

            def att_u_copy(a, bl, bank):
                act.wait_ge(av_done, BH * a + bl + 1)
                if a:
                    act.wait_ge(att_u_turned, BH * (a - 1) + bl + 1)
                act.activation(att_u[bl][:], ps[:, bank, :], ACT.Copy).then_inc(att_u_ready, 1)

            def attT_copy(a, bank):
                act.wait_ge(attT_done, a + 1)
                act.activation(attT[:], ps[:, bank, :], ACT.Copy).then_inc(attT_ready, 1)

            def gate_tanh(f):
                act.wait_ge(gate_lg, f + 1)
                act.activation(th[:], lg[:], ACT.Tanh, scale=0.5).then_inc(gate_th, 1)

            def wgtT_copy(f, bank):
                act.wait_ge(wgtT_done, f + 1)
                act.activation(wgtT[:], ps[:, bank, :].bitcast(BF16)[0:PARTS * E0, 0:TOK], ACT.Copy).then_inc(wgtT_ready, 1)

            def tanh0(n, bank):
                m = I0 if n % (NC0 + 1) == 0 else P
                act.wait_ge(up0_done, n + 1)
                f, i = divmod(n - 2, NC0 + 1)
                if n >= 2:
                    if i:
                        act.wait_ge(hid0_ready, NC0 * f + i)
                    else:
                        act.wait_ge(gu_ready, n - 1)
                act.activation(sg[n % 2][0:m, :], ps[0:m, bank, :], ACT.Tanh, scale=0.5).then_inc(th0_ready, 1)

            def spread_copy(f, c, bank):
                n = NC0 * f + c
                act.wait_ge(wb_done, n + 1)
                if n >= 2:
                    act.wait_ge(hid0_ready, n - 1)
                act.activation(wb_sb[:, n % 2, :], ps[:, bank, :], ACT.Copy).then_inc(wb_ready, 1)

            def router_exp(f):
                act.wait_ge(rdif_ready, f + 1)
                act.activation(rexp[:], rdif[:], ACT.Exp).then_inc(rexp_ready, 1)

            def xsel_copy(f, bl, bank):
                for k in range(2):
                    act.wait_ge(gather_done, 2 * (BH * f + bl) + k + 1)
                    src = ps[:, bank + k, 0:4 * CAP].rearrange("p (e c) -> p e c", e=4)
                    ins = act.activation(xsel[:, 4 * k:4 * k + 4, bl, :], src, ACT.Copy)
                ins.then_inc(xsel_ready, 1)

            def gatedT_copy(f, n, bank):
                act.wait_ge(gatedT_done, 5 * f + n + 1)
                act.activation(gatedT[:, 4 * n:4 * n + 4, :], ps[0:MS, bank, :].rearrange("m (i s) -> m i s", i=4),
                               ACT.Copy).then_inc(gatedT_ready, 1)

            def gelu(f, e, bank):
                n = E1 * f + e
                act.wait_ge(up1_done, n + 1)
                if n >= 2:
                    act.wait_ge(down1_done, n - 1)
                for j in range(NJ):
                    src = ps[:, bank + j // 2, (j % 2) * BH * CAP:(j % 2 + 1) * BH * CAP]
                    ins = act.activation(hid1[e % 2][:, j, :], src, ACT.Gelu,
                                         bias=cols_sb[:, C_B1 + NJ * e + j:C_B1 + NJ * e + j + 1])
                ins.then_inc(hid1_ready, 1)

            for step, *at in (
                (mask_k, 0), (xnT_copy, 0, 7), (q_hi, 0, 7), (xnT_copy, 1, 6), (q_hi, 1, 4), (narrow_constants,),
                (mask_k, 1), (nmT_copy, 0, 0, 7), (exp, 0, 0, 0, 6), (exp, 0, 0, 1, 5), (nmT_copy, 0, 1, 6),
                (exp, 0, 0, 2, 4), (exp, 0, 0, 3, 7), (exp, 0, 1, 0, 5), (exp, 0, 1, 1, 6), (exp, 0, 1, 2, 4),
                (att_u_copy, 0, 0, 7), (exp, 0, 1, 3, 5), (nmT_copy, 1, 0, 6), (att_u_copy, 0, 1, 7),
                (exp, 1, 0, 0, 5), (exp, 1, 0, 1, 6), (exp, 1, 0, 2, 4), (exp, 1, 0, 3, 5), (attT_copy, 0, 7),
                (nmT_copy, 1, 1, 6), (att_u_copy, 1, 0, 4), (exp, 1, 1, 0, 6), (exp, 1, 1, 1, 4), (exp, 1, 1, 2, 5),
                (exp, 1, 1, 3, 6), (att_u_copy, 1, 1, 4), (xnT_copy, 2, 7), (gate_tanh, 0), (attT_copy, 1, 4),
                (tanh0, 0, 0), (tanh0, 1, 2), (wgtT_copy, 0, 5), (tanh0, 2, 0), (spread_copy, 0, 0, 6),
                (spread_copy, 0, 1, 4), (spread_copy, 0, 2, 7), (tanh0, 3, 2), (spread_copy, 0, 3, 5), (tanh0, 4, 0),
                (spread_copy, 0, 4, 6), (tanh0, 5, 2), (spread_copy, 0, 5, 4), (tanh0, 6, 0), (xnT_copy, 3, 6),
                (spread_copy, 0, 6, 7), (tanh0, 7, 2), (spread_copy, 0, 7, 5), (tanh0, 8, 0), (gate_tanh, 1),
                (tanh0, 9, 2), (tanh0, 10, 0), (wgtT_copy, 1, 7), (spread_copy, 1, 0, 5), (spread_copy, 1, 1, 4),
                (tanh0, 11, 2), (spread_copy, 1, 2, 7), (tanh0, 12, 0), (spread_copy, 1, 3, 5), (tanh0, 13, 2),
                (spread_copy, 1, 4, 4), (tanh0, 14, 0), (spread_copy, 1, 5, 7), (tanh0, 15, 2),
                (spread_copy, 1, 6, 5), (tanh0, 16, 0), (spread_copy, 1, 7, 4), (tanh0, 17, 2), (xnT_copy, 4, 6),
                (q_hi, 2, 7), (xnT_copy, 5, 4), (nmT_copy, 2, 0, 6), (q_hi, 3, 7), (exp, 2, 0, 0, 5),
                (exp, 2, 0, 1, 4), (exp, 2, 0, 2, 6), (exp, 2, 0, 3, 5), (nmT_copy, 2, 1, 7), (att_u_copy, 2, 0, 4),
                (exp, 2, 1, 0, 6), (exp, 2, 1, 1, 5), (exp, 2, 1, 2, 7), (exp, 2, 1, 3, 6), (att_u_copy, 2, 1, 5),
                (attT_copy, 2, 7), (nmT_copy, 3, 0, 5), (exp, 3, 0, 0, 4), (exp, 3, 0, 1, 7), (exp, 3, 0, 2, 5),
                (exp, 3, 0, 3, 4), (nmT_copy, 3, 1, 7), (att_u_copy, 3, 0, 5), (exp, 3, 1, 0, 6), (exp, 3, 1, 1, 4),
                (exp, 3, 1, 2, 7), (exp, 3, 1, 3, 5), (xnT_copy, 6, 4), (att_u_copy, 3, 1, 7), (router_exp, 0),
                (attT_copy, 3, 7), (xnT_copy, 7, 4), (xsel_copy, 0, 0, 0), (router_exp, 1), (xsel_copy, 0, 1, 2),
                (gatedT_copy, 0, 0, 5), (gelu, 0, 0, 0), (gelu, 0, 1, 2), (gatedT_copy, 0, 1, 4),
                (gatedT_copy, 0, 2, 7), (gatedT_copy, 0, 3, 6), (gelu, 0, 2, 0), (gelu, 0, 3, 2), (gelu, 0, 4, 0),
                (gelu, 0, 5, 2), (gelu, 0, 6, 0), (gelu, 0, 7, 2), (gatedT_copy, 0, 4, 5), (xsel_copy, 1, 0, 0),
                (xsel_copy, 1, 1, 2), (gelu, 1, 0, 2), (gelu, 1, 1, 0), (gelu, 1, 2, 0), (gelu, 1, 3, 2),
                (gelu, 1, 4, 0), (gelu, 1, 5, 2), (gelu, 1, 6, 0), (gelu, 1, 7, 2), (gatedT_copy, 1, 0, 5),
                (gatedT_copy, 1, 1, 6), (gatedT_copy, 1, 2, 4), (gatedT_copy, 1, 3, 7), (gatedT_copy, 1, 4, 5),
            ):
                step(*at)

        @block.vector
        def _(dve):
            steps = [0]

            def mark(ins):
                steps[0] += 1
                ins.then_inc(dve_step, 1)

            def settle():
                dve.wait_ge(dve_step, steps[0])

            def link(ins):
                mark(ins)
                settle()

            dve.memset(zeros_b[:], 0.0).then_inc(zeros_b_ready, 1)

            def stats(g):
                h = g % NH
                if g < NH:
                    dve.wait_ge(ld_x[h], 16)
                else:
                    dve.wait_ge(x_ready, g - 1)
                if g:
                    dve.wait_ge(stats_ready, g)
                for t in range(TH):
                    mark(dve.bn_stats(bn6[:, t, :], xs[h][:, t, :]))
                settle()
                for t in range(TH):
                    ins = dve.bn_aggr(mv[h][:, t, :], bn6[:, t, :])
                ins.then_inc(stats_ready, 1)

            def normalise(g):
                h = g % NH
                dve.wait_ge(rstd_ready, g + 1)
                for t in range(TH):
                    dve.tensor_scalar(xn[h][:, t, :], xs[h][:, t, :], mv[h][:, t, 0:1], rstd[h][:, t:t + 1],
                                      ALU.subtract, ALU.mult).then_inc(xn_ready, 1)

            def k_prep(l, bank):
                dve.wait_ge(k_done, l + 1)
                if l == 0:
                    dve.wait_ge(ld_rows, 16)
                    dve.wait_ge(ld_cols, 16)
                    dve.wait_ge(ld_cols, 16)
                    link(dve.tensor_scalar(tau_s[:], rows_sb[:, R_TAU:R_TAU + B], ISQ, None, ALU.mult))
                tau_k = tau_s[:, :, None].broadcast_to([P, B, S2])
                k_ps = ps[:, bank, 0:B * S2].rearrange("p (b k) -> p b k", b=B)
                if l:
                    dve.wait_ge(k_masked_ready, 2 * l)
                    dve.wait_ge(k_parts_ready, l)
                dve.scalar_tensor_tensor(k32[:], k_ps, cols_sb[:, C_BK + l:C_BK + l + 1], tau_k,
                                         ALU.add, ALU.mult).then_inc(k32_ready, 1)
                dve.wait_ge(k32_ready, l + 1)
                link(dve.tensor_copy(k_part[:, 2], k32[:]))
                link(dve.tensor_tensor(k_rest[:], k32[:], k_part[:, 2], ALU.subtract))
                link(dve.tensor_copy(k_part[:, 1], k_rest[:]))
                dve.tensor_tensor(k_part[:, 0], k_rest[:], k_part[:, 1], ALU.subtract).then_inc(k_parts_ready, 1)

            def v_prep(l, bank):
                dve.wait_ge(v_done, l + 1)
                if l == 0:
                    dve.wait_ge(ld_rows, 16)
                dve.wait_ge(fill_done, l + 1)
                v_ps = ps[:, bank, :].rearrange("p (b j e d) -> p b j e d", b=B, j=NP, e=2)
                bv = rows_sb[:, R_BV + l * D:R_BV + (l + 1) * D].rearrange("p (j e d) -> p j e d", j=NP, e=2)
                for e in range(2):
                    r = slice(S2 * e, S2 * (e + 1))
                    ins = dve.tensor_tensor(v_blk[l][r, :, :, e, 0:DK], v_ps[r, :, :, e, :],
                                            bv[r, :, e, :][:, None, :, :].broadcast_to([S2, B, NP, DK]), ALU.add)
                    ins.then_inc(v_ready, 1)

            def q_split(a, bank):
                l, h = a // NH, a % NH
                dve.wait_ge(q_hi_ready, a + 1)
                if a:
                    dve.wait_ge(q_lo_ready, a)
                dve.scalar_tensor_tensor(q_rest[:], ps[:, bank, :], cols_sb[:, C_BQ + l:C_BQ + l + 1], q_parts[h][:, 0, :],
                                         ALU.add, ALU.subtract).then_inc(q_rest_ready, 1)

            def q_split2(a):
                h = a % NH
                dve.wait_ge(q_rest_ready, a + 1)
                dve.tensor_copy(q_parts[h][:, 1, :], q_rest[:]).then_inc(q_mid_ready, 1)
                dve.wait_ge(q_mid_ready, a + 1)
                dve.tensor_tensor(q_parts[h][:, 2, :], q_rest[:], q_parts[h][:, 1, :], ALU.subtract).then_inc(q_lo_ready, 1)

            def score_max(a, t, bank):
                dve.wait_ge(s1_done, TH * a + t + 1)
                dve.tensor_reduce(negmax[:, t, :], ps[:, bank:bank + 2, :].rearrange("p n (e k) -> p (n e) k", k=S2),
                                  AX.X, ALU.max, negate=True).then_inc(max_ready, 1)

            def max_parts(a, bl):
                nm = negmax[:, QT * bl:QT * bl + QT, :]
                dve.wait_ge(max_ready, TH * a + QT * (bl + 1))
                parts = nm_parts[bl]
                if a or bl:
                    dve.wait_ge(nm_ready, BH * a + bl)
                link(dve.tensor_copy(parts[:, :, 0, :], nm))
                link(dve.tensor_tensor(nm_rest[:], nm, parts[:, :, 0, :], ALU.subtract))
                link(dve.tensor_copy(parts[:, :, 1, :], nm_rest[:]))
                dve.tensor_tensor(parts[:, :, 2, :], nm_rest[:], parts[:, :, 1, :], ALU.subtract).then_inc(nm_ready, 1)

            def normalise_att(a, bl, bank):
                dve.wait_ge(att_u_turned, BH * a + bl + 1)
                av = ps[:, bank, :].rearrange("p (x c) -> p x c", c=VC)[:, :, 0:2 * (DK + 1)]
                av = av.rearrange("p x (e d) -> p x e d", e=2)
                tiles = slice(QT * bl, QT * (bl + 1))
                if a:
                    dve.wait_ge(att_ready, BH * (a - 1) + bl + 1)
                rs = rsum[:, tiles, :].rearrange("p t (j e) -> p (t j) e", e=2)
                link(dve.reciprocal(rs, av[:, :, :, DK]))
                dve.tensor_tensor(att[:, tiles].rearrange("p t (j e) d -> p (t j) e d", e=2), av[:, :, :, 0:DK],
                                  rs[:, :, :, None].broadcast_to([P, QT * NP, 2, DK]), ALU.mult).then_inc(att_ready, 1)

            def residual(g, bank):
                h = g % NH
                if g in ATT_G:
                    dve.wait_ge(wo_done, ATT_G.index(g) + 1)
                else:
                    dve.wait_ge(down0_done, g - 1)
                dve.wait_ge(xb_ready, g + 1)
                dve.tensor_tensor(xs[h][:], ps[:, bank, :].rearrange("p (t d) -> p t d", t=TH), xb[h][:],
                                  ALU.add).then_inc(x_ready, 1)

            def gate_logits(f, bank):
                dve.wait_ge(gate_done, f + 1)
                gb = rows_sb[:, R_GB:R_GB + E0][:, None, :].broadcast_to([P, TH, E0])
                dve.tensor_tensor(lg[:], ps[:, bank, 0:TH * E0].rearrange("p (t e) -> p t e", t=TH), gb,
                                  ALU.add).then_inc(gate_lg, 1)

            def route(f):
                dve.wait_ge(gate_th, f + 1)
                if f:
                    dve.wait_ge(wgt_ready, f)
                link(dve.tensor_scalar(sig[:], th[:], 0.5, 0.5, ALU.mult, ALU.add))
                for t in range(TH):
                    mark(dve.max(top8[:, t, :], sig[:, t, :]))
                settle()
                for t in range(TH):
                    mark(dve.max_index(top_ix[:, t, :], top8[:, t, :], sig[:, t, :]))
                link(dve.tensor_tensor(vsum[:], top8[:, :, 0], top8[:, :, 1], ALU.add))
                mark(dve.tensor_copy(top_ixf[:], top_ix[:]))
                link(dve.reciprocal(vrec[:], vsum[:]))
                mark(dve.tensor_tensor(vnorm[:], top8[:, :, 0:2], vrec[:][:, :, None].broadcast_to([P, TH, 2]), ALU.mult))
                link(dve.tensor_tensor(pick[:], iota_e0[:, None, None, :].broadcast_to([P, TH, 2, E0]),
                                       top_ixf[:, :, 0:2][:, :, :, None].broadcast_to([P, TH, 2, E0]), ALU.is_equal))
                link(dve.tensor_tensor(pick[:], pick[:], vnorm[:][:, :, :, None].broadcast_to([P, TH, 2, E0]), ALU.mult))
                link(dve.tensor_tensor(wgt[:], pick[:, :, 0, :], pick[:, :, 1, :], ALU.add))
                link(dve.tensor_copy(wgt_parts[:, :, 0, :], wgt[:]))
                link(dve.tensor_tensor(wgt_rest[:], wgt[:], wgt_parts[:, :, 0, :], ALU.subtract))
                link(dve.tensor_copy(wgt_parts[:, :, 1, :], wgt_rest[:]))
                dve.tensor_tensor(wgt_parts[:, :, 2, :], wgt_rest[:], wgt_parts[:, :, 1, :],
                                  ALU.subtract).then_inc(wgt_ready, 1)

            def gate_up0(n, bank):
                f, u = n // (NC0 + 1), n % 2
                shared = n % (NC0 + 1) == 0
                m = I0 if shared else P
                dst = hid0[f][0:m, NC0, :] if shared else sg[u][:]
                dve.wait_ge(th0_ready, n + 1)
                link(dve.scalar_tensor_tensor(sg[u][0:m, :], sg[u][0:m, :], 1.0, ps[0:m, bank, :], ALU.add, ALU.mult))
                dve.scalar_tensor_tensor(dst, sg[u][0:m, :], 0.5, ps[0:m, bank + 1, :], ALU.mult,
                                         ALU.mult).then_inc(gu_ready, 1)

            def router_softmax(f, bank):
                dve.wait_ge(router_done, f + 1)
                r = ps[:, bank, 0:TH * E1].rearrange("p (t e) -> p t e", t=TH)
                if f:
                    dve.wait_ge(rexp_ready, f)
                link(dve.tensor_reduce(rmax[:], r, AX.X, ALU.max))
                dve.tensor_tensor(rdif[:], r, rmax[:][:, :, None].broadcast_to([P, TH, E1]),
                                  ALU.subtract).then_inc(rdif_ready, 1)

            def router_scores(f):
                dve.wait_ge(rexp_ready, f + 1)
                if f:
                    dve.wait_ge(score_ready, f)
                link(dve.tensor_reduce(rtot[:], rexp[:], AX.X, ALU.add))
                link(dve.reciprocal(rrec[:], rtot[:]))
                dve.tensor_tensor(score[f][:].rearrange("p q b e -> p b q e"),
                                  rexp[:].rearrange("p (b q) e -> p b q e", b=BH),
                                  rrec[:].rearrange("p (b q) -> p b q", b=BH)[:, :, :, None].broadcast_to([P, BH, QT, E1]),
                                  ALU.mult).then_inc(score_ready, 1)

            def choose_start(f, bank):
                dve.wait_ge(scoreT_done, f + 1)
                if f:
                    dve.wait_ge(slot_ready, f)
                dve.tensor_copy(sT, ps[0:BH * E1, bank, 0:S]).then_inc(sT_ready, 1)

            def choose_round(f, r):
                if r == 0:
                    dve.wait_ge(sT_ready, f + 1)
                cur = work if r else sT
                link(dve.max(m8[:], cur))
                link(dve.match_replace(work, m8[:], cur, -1.0))

            def choose_end(f):
                assert CAP % 8 == 1
                link(dve.max(m8[:], work))
                link(dve.max_index(m8ix[:], m8[:], work))
                link(dve.tensor_copy(m8ixf[:], m8ix[:]))
                link(dve.tensor_scalar(chosen, iota_s, m8ixf[:, 0:1], None, ALU.is_equal))
                link(dve.scalar_tensor_tensor(chosen, work, -1.0, chosen, ALU.is_equal, ALU.add))
                link(dve.tensor_tensor_scan(slot_n, ones_s[:], chosen, 0.0, ALU.mult, ALU.add))
                dve.tensor_tensor(slot[:], slot_n, chosen, ALU.mult).then_inc(slot_ready, 1)

            def slotT_copy(f, bank):
                dve.wait_ge(slotT_done, f + 1)
                if f:
                    dve.wait_ge(onehot_ready, BH * f)
                dve.tensor_copy(slotT[:].rearrange("p q b e -> p (q b e)"),
                                ps[:, bank, 0:TH * E1]).then_inc(slotT_ready, 1)

            def make_onehot(f, bl):
                dve.wait_ge(slotT_ready, f + 1)
                dve.tensor_tensor(onehot[f][:, :, bl], iota_slot[:, None, None, :].broadcast_to([P, QT, E1, CAP]),
                                  slotT[:, :, bl][:, :, :, None].broadcast_to([P, QT, E1, CAP]),
                                  ALU.is_equal).then_inc(onehot_ready, 1)

            def y_bias(f, e, bank):
                dve.wait_ge(down1_done, E1 * f + e + 1)
                if f and e == 0:
                    dve.wait_ge(yTT_done, 2 * f)
                src = ps[:, bank, 0:BH * CAP].rearrange("p (b c) -> p b c", b=BH)
                dve.tensor_scalar(yT[:, :, e, :], src, cols_sb[:, C_B2 + e:C_B2 + e + 1], None,
                                  ALU.add).then_inc(yT_ready, 1)

            def y_copy(f, u, bank):
                n = (8, 2)[u]
                dve.wait_ge(yTT_done, 2 * f + u + 1)
                if f and u == 0:
                    dve.wait_ge(scatter_done, TH * f)
                src = ps[0:MS, bank:bank + 2 - u, :].rearrange("m n (i d) -> m (n i) d", d=D)[:, 0:n, :]
                dve.tensor_copy(y[:, 8 * u:8 * u + n, :], src).then_inc(y_ready, 1)

            def finish(f, t, bank):
                dve.wait_ge(scatter_done, TH * f + t + 1)
                dve.tensor_tensor(xb[f][:, t, :], ps[:, bank, 0:D], xs[f][:, t, :], ALU.add).then_inc(out_ready, 1)

            for step, *at in (
                (stats, 0), (k_prep, 0, 7), (normalise, 0), (stats, 1), (v_prep, 0, 6), (v_prep, 1, 4),
                (normalise, 1), (q_split, 0, 7), (q_split2, 0), (k_prep, 1, 5), (q_split, 1, 4), (q_split2, 1),
                (score_max, 0, 0, 0), (score_max, 0, 1, 2), (max_parts, 0, 0), (score_max, 0, 2, 0),
                (score_max, 0, 3, 2), (max_parts, 0, 1), (score_max, 1, 0, 0), (score_max, 1, 1, 2),
                (max_parts, 1, 0), (score_max, 1, 2, 0), (score_max, 1, 3, 2), (normalise_att, 0, 0, 4),
                (max_parts, 1, 1), (normalise_att, 0, 1, 7), (residual, 0, 5), (stats, 2), (normalise_att, 1, 0, 7),
                (normalise, 2), (normalise_att, 1, 1, 5), (gate_logits, 0, 6), (route, 0), (gate_up0, 0, 0),
                (residual, 1, 7), (stats, 3), (gate_up0, 1, 2), (gate_up0, 2, 0), (normalise, 3), (gate_up0, 3, 2),
                (gate_up0, 4, 0), (gate_up0, 5, 2), (gate_up0, 6, 0), (gate_up0, 7, 2), (gate_logits, 1, 4),
                (gate_up0, 8, 0), (route, 1), (gate_up0, 9, 2), (gate_up0, 10, 0), (gate_up0, 11, 2),
                (gate_up0, 12, 0), (gate_up0, 13, 2), (residual, 2, 6), (stats, 4), (gate_up0, 14, 0),
                (gate_up0, 15, 2), (normalise, 4), (gate_up0, 16, 0), (gate_up0, 17, 2), (q_split, 2, 7),
                (q_split2, 2), (residual, 3, 5), (stats, 5), (score_max, 2, 0, 0), (score_max, 2, 1, 2),
                (normalise, 5), (max_parts, 2, 0), (score_max, 2, 2, 0), (score_max, 2, 3, 2), (q_split, 3, 7),
                (max_parts, 2, 1), (q_split2, 3), (normalise_att, 2, 0, 4), (score_max, 3, 0, 0),
                (normalise_att, 2, 1, 4), (score_max, 3, 1, 2), (max_parts, 3, 0), (score_max, 3, 2, 0),
                (score_max, 3, 3, 2), (max_parts, 3, 1), (residual, 4, 6), (stats, 6), (normalise, 6),
                (normalise_att, 3, 0, 6), (router_softmax, 0, 6), (router_scores, 0), (normalise_att, 3, 1, 5),
                (choose_start, 0, 4), (choose_round, 0, 0), (choose_round, 0, 1), (choose_round, 0, 2),
                (choose_round, 0, 3), (residual, 5, 6), (choose_round, 0, 4), (stats, 7), (choose_round, 0, 5),
                (choose_round, 0, 6), (choose_round, 0, 7), (choose_end, 0), (normalise, 7), (slotT_copy, 0, 5),
                (make_onehot, 0, 0), (make_onehot, 0, 1), (router_softmax, 1, 7), (router_scores, 1),
                (choose_start, 1, 6), (choose_round, 1, 0), (choose_round, 1, 1), (choose_round, 1, 2),
                (choose_round, 1, 3), (choose_round, 1, 4), (choose_round, 1, 5), (choose_round, 1, 6),
                (choose_round, 1, 7), (y_bias, 0, 0, 5), (choose_end, 1), (y_bias, 0, 1, 4), (y_bias, 0, 2, 7),
                (y_bias, 0, 3, 6), (y_bias, 0, 4, 5), (y_bias, 0, 5, 4), (slotT_copy, 1, 7), (make_onehot, 1, 0),
                (make_onehot, 1, 1), (y_bias, 0, 6, 6), (y_bias, 0, 7, 4), (y_copy, 0, 0, 0), (y_copy, 0, 1, 7),
                (finish, 0, 0, 5), (y_bias, 1, 0, 6), (y_bias, 1, 1, 4), (finish, 0, 1, 7), (y_bias, 1, 2, 5),
                (y_bias, 1, 3, 6), (finish, 0, 2, 4), (y_bias, 1, 4, 7), (y_bias, 1, 5, 5), (finish, 0, 3, 6),
                (y_bias, 1, 6, 4), (y_bias, 1, 7, 7), (y_copy, 1, 0, 0), (y_copy, 1, 1, 6), (finish, 1, 0, 4),
                (finish, 1, 1, 7), (finish, 1, 2, 6), (finish, 1, 3, 5),
            ):
                step(*at)

        @block.tensor
        def _(pe):
            reader = {}

            def claim(banks, read, count):
                for wait in {reader[b] for b in banks if b in reader}:
                    pe.wait_ge(*wait)
                for b in banks:
                    reader[b] = read, count

            def keep_warm(n, bank):
                if bank in reader:
                    pe.wait_ge(*reader.pop(bank))
                pe.wait_ge(zeros_b_ready, 1)
                for _ in range(n):
                    pe.matmul(ps[:, bank, :].rearrange("p (i c) -> p i c", c=P), zeros_b[:],
                              zeros_b[:, None, :].broadcast_to([P, 4, P]), start=True, stop=True)

            def turn_x(g, bank):
                h = g % NH
                claim([bank], xnT_ready, g + 1)
                if g == 0:
                    pe.wait_ge(ld_cols, 16)
                for t in range(TH):
                    pe.wait_ge(xn_ready, TH * g + t + 1)
                    ins = pe.transpose(ps[:, bank, t * P:(t + 1) * P], xn[h][:, t, :], ident)
                ins.then_inc(xT_done, 1)

            def project_q(a, bank):
                l, h = a // NH, a % NH
                claim([bank], q_rest_ready, a + 1)
                pe.wait_ge(xnT_ready, ATT_G[a] + 1)
                if h == 0:
                    pe.wait_ge(ld_wT[l], 16)
                pe.matmul(ps[:, bank, :], wT_sb[:, l, 0, :], xnT[h][:], start=True, stop=True).then_inc(q_done, 1)

            def project_k(l, bank):
                if l == 0:
                    pe.wait_ge(ld_ctx, 16)
                pe.wait_ge(ld_wT[l], 16)
                claim([bank], k32_ready, l + 1)
                pe.matmul(ps[:, bank, 0:B * S2].rearrange("p (b k) -> p b k", b=B), wT_sb[:, l, 1, :], ctx_sb[:, :, 0, :],
                          start=True, stop=True).then_inc(k_done, 1)

            def project_v(l, bank):
                claim([bank], v_ready, 2 * (l + 1))
                if l == 0:
                    pe.wait_ge(ld_ctx, 16)
                pe.wait_ge(ld_wT[l], 16)
                for b in range(B):
                    ins = pe.matmul(ps[:, bank, b * D:(b + 1) * D], ctx_sb[:, b].rearrange("d e k -> d (e k)"),
                                    wT_sb[:, l, 2, :], start=True, stop=True)
                ins.then_inc(v_done, 1)

            def scores(a, t, bank):
                l, h, b = a // NH, a % NH, BH * (a % NH) + t // QT
                claim([bank, bank + 1], max_ready, TH * a + t + 1)
                if t == 0:
                    pe.wait_ge(q_stacked[h], 16 * len(RUNS) * (l + 1))
                    if l == 0:
                        pe.wait_ge(ones_stacked[h], 16)
                    if h == 0:
                        pe.wait_ge(k_stacked[l], 16 * len(RUNS))
                        pe.wait_ge(delta_stacked[l], 16)
                for j in range(NP):
                    ins = pe.matmul(ps[:, bank + j // 4, (j % 4) * P:(j % 4 + 1) * P],
                                    q_stack[h][:, j, t * P:(t + 1) * P], k_stack[l][:, j, b, :], start=True, stop=True)
                ins.then_inc(s1_done, 1)

            def turn_max(a, bl, bank):
                claim([bank], nmT_ready, BH * a + bl + 1)
                pe.wait_ge(nm_ready, BH * a + bl + 1)
                if a == 0 and bl == 0:
                    pe.wait_ge(bf16_ready, 2)
                dst = ps[:, bank, :].bitcast(BF16)
                for qt in range(QT):
                    ins = pe.transpose(dst[0:PARTS * H, qt * P:(qt + 1) * P],
                                       nm_parts[bl][:, qt].rearrange("p c e -> p (c e)"), ident_b[:])
                ins.then_inc(nmT_done, 1)

            def scores_T(a, bl, n, bank):
                l, h, b = a // NH, a % NH, BH * (a % NH) + bl
                claim([bank], probs_ready, (NP // 2) * (BH * a + bl) + n + 1)
                if n == 0:
                    pe.wait_ge(nmT_ready, BH * a + bl + 1)
                for i in range(2):
                    j = 2 * n + i
                    dst = ps[:, bank, i * S:(i + 1) * S]
                    pe.matmul(dst, k_stack[l][:, j, b, :], q_stack[h][:, j, bl * S:(bl + 1) * S], start=True, stop=False)
                    ins = pe.matmul(dst, sel[:, j, :], nmT[bl][:], start=False, stop=True)
                ins.then_inc(s2_done, 1)

            def values(a, bl, bank):
                l, b = a // NH, BH * (a % NH) + bl
                claim([bank], att_u_ready, BH * a + bl + 1)
                if bl == 0 and a % NH == 0:
                    pe.wait_ge(v_ready, 2 * (l + 1))
                pe.wait_ge(probs_ready, (NP // 2) * (BH * a + bl + 1))
                for j in range(NP):
                    ins = pe.matmul(ps[VC * (j % 4):VC * (j % 4 + 1), bank, (j // 4) * S:(j // 4 + 1) * S],
                                    v_pad[l][:, b, j, :], probs[bl][:, j, :], start=True, stop=True,
                                    tile_position=(0, VC * (j % 4)))
                ins.then_inc(av_done, 1)

            def turn_values(a, bl, bank):
                claim([bank], att_ready, BH * a + bl + 1)
                pe.wait_ge(att_u_ready, BH * a + bl + 1)
                for qt in range(QT):
                    for i in range(2):
                        ins = pe.transpose(ps[:, bank, (2 * qt + i) * P:(2 * qt + i + 1) * P],
                                           att_u[bl][:, i * S + qt * P:i * S + (qt + 1) * P], ident)
                ins.then_inc(att_u_turned, 1)

            def turn_att(a, bank):
                claim([bank], attT_ready, a + 1)
                pe.wait_ge(att_ready, BH * (a + 1))
                for t in range(TH):
                    ins = pe.transpose(ps[:, bank, t * P:(t + 1) * P], att[:, t].rearrange("p e d -> p (e d)"), ident)
                ins.then_inc(attT_done, 1)

            def project_out(a, bank):
                claim([bank], x_ready, ATT_G[a] + 1)
                pe.wait_ge(attT_ready, a + 1)
                for t in range(TH):
                    ins = pe.matmul(ps[:, bank, t * D:(t + 1) * D], attT[:, t * P:(t + 1) * P], wT_sb[:, a // NH, 3, :],
                                    start=True, stop=True)
                ins.then_inc(wo_done, 1)

            def gate(f, bank):
                claim([bank], gate_lg, f + 1)
                pe.wait_ge(xnT_ready, NH + f + 1)
                for t in range(TH):
                    ins = pe.matmul(ps[:, bank, t * E0:(t + 1) * E0], xnT[f][:, t * P:(t + 1) * P],
                                    cols_sb[:, C_GW:C_GW + E0], start=True, stop=True)
                ins.then_inc(gate_done, 1)

            def turn_weights(f, bank):
                claim([bank], wgtT_ready, f + 1)
                pe.wait_ge(wgt_ready, f + 1)
                dst = ps[:, bank, :].bitcast(BF16)
                for t in range(TH):
                    ins = pe.transpose(dst[0:PARTS * E0, t * P:(t + 1) * P],
                                       wgt_parts[:, t].rearrange("p c e -> p (c e)"), ident_b[:])
                ins.then_inc(wgtT_done, 1)

            def up0(n, bank):
                f, i = divmod(n, NC0 + 1)
                c = (NC0, *range(NC0))[i]
                m = I0 if c == NC0 else P
                e = slice(2 * c, 2 * c + m // I0)
                claim([bank, bank + 1], gu_ready, n + 1)
                if n == 0:
                    pe.wait_ge(ld_gu, 32)
                    pe.wait_ge(delta_stacked[NL - 1], 16)
                    pe.wait_ge(ones_stacked[NH - 1], 16)
                if i == 0:
                    pe.wait_ge(xnT_ready, NH + f + 1)
                for k, w in enumerate((wg_sb, wu_sb)):
                    ins = pe.matmul(ps[0:m, bank + k, :], w[:, e, :].rearrange("d e i -> d (e i)"), xnT[f][:],
                                    start=True, stop=True)
                ins.then_inc(up0_done, 1)

            def spread_weights(f, c, bank):
                claim([bank], wb_ready, NC0 * f + c + 1)
                if c == 0:
                    pe.wait_ge(wgtT_ready, f + 1)
                pe.matmul(ps[:, bank, :], sel[:, c, :], wgtT[:], start=True, stop=True).then_inc(wb_done, 1)

            def down0(f, t, bank):
                if t == 0:
                    claim([bank], x_ready, NH + f + 1)
                    if f == 0:
                        pe.wait_ge(ld_down, 32)
                    pe.wait_ge(gu_ready, (NC0 + 1) * (f + 1))
                    pe.wait_ge(hid0_ready, NC0 * (f + 1))
                for c in range(NC0 + 1):
                    k = I0 if c == NC0 else P
                    ins = pe.matmul(ps[:, bank, t * D:(t + 1) * D], hid0[f][0:k, c, t * P:(t + 1) * P], wd_sb[0:k, c, :],
                                    start=(c == 0), stop=(c == NC0))
                if t == TH - 1:
                    ins.then_inc(down0_done, 1)

            def router(f, bank):
                claim([bank], rdif_ready, f + 1)
                pe.wait_ge(xnT_ready, 3 * NH + f + 1)
                for t in range(TH):
                    ins = pe.matmul(ps[:, bank, t * E1:(t + 1) * E1], xnT[f][:, t * P:(t + 1) * P],
                                    cols_sb[:, C_RW:C_RW + E1], start=True, stop=True)
                ins.then_inc(router_done, 1)

            def turn_scores(f, bank):
                claim([bank], sT_ready, f + 1)
                pe.wait_ge(score_ready, f + 1)
                for qt in range(QT):
                    ins = pe.transpose(ps[0:BH * E1, bank, qt * P:(qt + 1) * P],
                                       score[f][:, qt].rearrange("p b e -> p (b e)"), ident)
                ins.then_inc(scoreT_done, 1)

            def turn_slots(f, bank):
                claim([bank], slotT_ready, f + 1)
                pe.wait_ge(slot_ready, f + 1)
                for qt in range(QT):
                    ins = pe.transpose(ps[:, bank, qt * BH * E1:(qt + 1) * BH * E1], slot[:, qt * P:(qt + 1) * P],
                                       ident[0:BH * E1, 0:BH * E1])
                ins.then_inc(slotT_done, 1)

            def gather(f, bl, bank):
                claim([bank, bank + 1], xsel_ready, BH * f + bl + 1)
                pe.wait_ge(onehot_ready, BH * f + bl + 1)
                for k in range(2):
                    for qt in range(QT):
                        ins = pe.matmul(ps[:, bank + k, 0:4 * CAP], xn[f][:, QT * bl + qt, :],
                                        onehot[f][:, qt, bl, 4 * k:4 * k + 4].rearrange("p e c -> p (e c)"),
                                        start=(qt == 0), stop=(qt == QT - 1))
                    ins.then_inc(gather_done, 1)

            def turn_gated(f, n, bank):
                claim([bank], gatedT_ready, 5 * f + n + 1)
                pe.wait_ge(gated_ready, f + 1)
                for i in range(4 * n, 4 * n + 4):
                    t, m = divmod(i, NM)
                    src = gated[:, t % QT, t // QT].rearrange("p e c -> p (e c)")[:, m * MS:(m + 1) * MS]
                    ins = pe.transpose(ps[0:MS, bank, (i % 4) * P:(i % 4 + 1) * P], src, ident)
                ins.then_inc(gatedT_done, 1)

            def up1(f, e, bank):
                claim([bank, bank + 1], hid1_ready, E1 * f + e + 1)
                if e == 0:
                    pe.wait_ge(xsel_ready, BH * (f + 1))
                    if f == 0:
                        pe.wait_ge(ld_w1, 16)
                for j in range(NJ):
                    ins = pe.matmul(ps[:, bank + j // 2, (j % 2) * BH * CAP:(j % 2 + 1) * BH * CAP],
                                    w1_sb[:, e, j * P:(j + 1) * P], xsel[:, e].rearrange("p b c -> p (b c)"),
                                    start=True, stop=True)
                ins.then_inc(up1_done, 1)

            def down1(f, e, bank):
                claim([bank], yT_ready, E1 * f + e + 1)
                pe.wait_ge(hid1_ready, E1 * f + e + 1)
                if f == 0 and e == 0:
                    pe.wait_ge(ld_w2, 16)
                for j in range(NJ):
                    ins = pe.matmul(ps[:, bank, 0:BH * CAP], w2_sb[:, e, j, :], hid1[e % 2][:, j, :],
                                    start=(j == 0), stop=(j == NJ - 1))
                ins.then_inc(down1_done, 1)

            def turn_y(f, u, bank):
                claim([bank, bank + 1] if u == 0 else [bank], y_ready, 2 * f + u + 1)
                pe.wait_ge(yT_ready, E1 * (f + 1))
                for i in range((8, 2)[u]):
                    bl, m = divmod(8 * u + i, NM)
                    src = yT[:, bl].rearrange("p e c -> p (e c)")[:, m * MS:(m + 1) * MS]
                    ins = pe.transpose(ps[0:MS, bank + i // 4, (i % 4) * D:(i % 4 + 1) * D], src, ident)
                ins.then_inc(yTT_done, 1)

            def scatter(f, t, bank):
                claim([bank], out_ready, TH * f + t + 1)
                if t == 0:
                    pe.wait_ge(gatedT_ready, 5 * (f + 1))
                    pe.wait_ge(y_ready, 2 * (f + 1))
                for m in range(NM):
                    ins = pe.matmul(ps[:, bank, 0:D], gatedT[:, NM * t + m, :], y[:, NM * (t // QT) + m, :],
                                    start=(m == 0), stop=(m == NM - 1))
                ins.then_inc(scatter_done, 1)

            for step, *at in (
                (keep_warm, 12, 0), (project_k, 0, 7), (project_v, 0, 6), (project_k, 1, 5), (project_v, 1, 4),
                (turn_x, 0, 7), (project_q, 0, 7), (turn_x, 1, 6), (project_q, 1, 4), (keep_warm, 30, 0),
                (scores, 0, 0, 0), (scores, 0, 1, 2), (keep_warm, 5, 0), (scores, 0, 2, 0), (keep_warm, 3, 2),
                (scores, 0, 3, 2), (turn_max, 0, 0, 7), (scores_T, 0, 0, 0, 6), (scores_T, 0, 0, 1, 5),
                (scores_T, 0, 0, 2, 4), (scores_T, 0, 0, 3, 7), (turn_max, 0, 1, 6), (scores, 1, 0, 0),
                (scores, 1, 1, 2), (scores_T, 0, 1, 0, 5), (scores_T, 0, 1, 1, 6), (scores_T, 0, 1, 2, 4),
                (scores, 1, 2, 0), (values, 0, 0, 7), (scores_T, 0, 1, 3, 5), (scores, 1, 3, 2), (turn_max, 1, 0, 6),
                (turn_values, 0, 0, 4), (values, 0, 1, 7), (scores_T, 1, 0, 0, 5), (scores_T, 1, 0, 1, 6),
                (keep_warm, 3, 4), (scores_T, 1, 0, 2, 4), (turn_values, 0, 1, 7), (scores_T, 1, 0, 3, 5),
                (turn_max, 1, 1, 6), (turn_att, 0, 7), (values, 1, 0, 4), (project_out, 0, 5),
                (turn_values, 1, 0, 7), (scores_T, 1, 1, 0, 6), (scores_T, 1, 1, 1, 4), (scores_T, 1, 1, 2, 5),
                (scores_T, 1, 1, 3, 6), (values, 1, 1, 4), (turn_x, 2, 7), (turn_values, 1, 1, 5), (gate, 0, 6),
                (turn_att, 1, 4), (up0, 0, 0), (keep_warm, 2, 7), (project_out, 1, 7), (up0, 1, 2),
                (turn_weights, 0, 5), (up0, 2, 0), (spread_weights, 0, 0, 6), (keep_warm, 4, 4),
                (spread_weights, 0, 1, 4), (spread_weights, 0, 2, 7), (spread_weights, 0, 3, 5),
                (spread_weights, 0, 4, 6), (spread_weights, 0, 5, 4), (up0, 3, 2), (up0, 4, 0),
                (spread_weights, 0, 6, 7), (spread_weights, 0, 7, 5), (up0, 5, 2), (up0, 6, 0), (turn_x, 3, 6),
                (up0, 7, 2), (up0, 8, 0), (gate, 1, 4), (up0, 9, 2), (up0, 10, 0), (down0, 0, 0, 6),
                (turn_weights, 1, 7), (down0, 0, 1, 6), (spread_weights, 1, 0, 5), (spread_weights, 1, 1, 4),
                (spread_weights, 1, 2, 7), (up0, 11, 2), (spread_weights, 1, 3, 5), (up0, 12, 0),
                (spread_weights, 1, 4, 4), (spread_weights, 1, 5, 7), (down0, 0, 2, 6), (up0, 13, 2),
                (spread_weights, 1, 6, 5), (down0, 0, 3, 6), (spread_weights, 1, 7, 4), (up0, 14, 0), (up0, 15, 2),
                (up0, 16, 0), (up0, 17, 2), (turn_x, 4, 6), (keep_warm, 11, 7), (project_q, 2, 7), (down0, 1, 0, 5),
                (down0, 1, 1, 5), (down0, 1, 2, 5), (down0, 1, 3, 5), (scores, 2, 0, 0), (scores, 2, 1, 2),
                (keep_warm, 4, 0), (scores, 2, 2, 0), (scores, 2, 3, 2), (turn_x, 5, 4), (turn_max, 2, 0, 6),
                (project_q, 3, 7), (scores_T, 2, 0, 0, 5), (scores_T, 2, 0, 1, 4), (keep_warm, 10, 6),
                (scores_T, 2, 0, 2, 6), (scores_T, 2, 0, 3, 5), (turn_max, 2, 1, 7), (keep_warm, 3, 4),
                (values, 2, 0, 4), (scores_T, 2, 1, 0, 6), (scores_T, 2, 1, 1, 5), (scores_T, 2, 1, 2, 7),
                (turn_values, 2, 0, 4), (scores_T, 2, 1, 3, 6), (keep_warm, 5, 5), (values, 2, 1, 5),
                (scores, 3, 0, 0), (scores, 3, 1, 2), (turn_values, 2, 1, 4), (scores, 3, 2, 0), (turn_att, 2, 7),
                (project_out, 2, 6), (turn_max, 3, 0, 5), (scores, 3, 3, 2), (scores_T, 3, 0, 0, 4),
                (scores_T, 3, 0, 1, 7), (scores_T, 3, 0, 2, 5), (scores_T, 3, 0, 3, 4), (turn_max, 3, 1, 7),
                (values, 3, 0, 5), (scores_T, 3, 1, 0, 6), (scores_T, 3, 1, 1, 4), (scores_T, 3, 1, 2, 7),
                (scores_T, 3, 1, 3, 5), (turn_values, 3, 0, 6), (turn_x, 6, 4), (values, 3, 1, 7), (router, 0, 6),
                (keep_warm, 2, 5), (turn_values, 3, 1, 5), (keep_warm, 2, 4), (turn_scores, 0, 4), (turn_att, 3, 7),
                (project_out, 3, 6), (turn_slots, 0, 5), (keep_warm, 4, 4), (turn_x, 7, 4), (router, 1, 7),
                (gather, 0, 0, 0), (gather, 0, 1, 2), (turn_scores, 1, 6), (turn_gated, 0, 0, 5), (up1, 0, 0, 0),
                (up1, 0, 1, 2), (turn_gated, 0, 1, 4), (turn_gated, 0, 2, 7), (turn_gated, 0, 3, 6), (up1, 0, 2, 0),
                (down1, 0, 0, 5), (down1, 0, 1, 4), (up1, 0, 3, 2), (up1, 0, 4, 0), (down1, 0, 2, 7), (up1, 0, 5, 2),
                (down1, 0, 3, 6), (up1, 0, 6, 0), (down1, 0, 4, 5), (up1, 0, 7, 2), (down1, 0, 5, 4),
                (turn_slots, 1, 7), (down1, 0, 6, 6), (turn_gated, 0, 4, 5), (down1, 0, 7, 4), (gather, 1, 0, 0),
                (gather, 1, 1, 2), (turn_y, 0, 0, 0), (turn_y, 0, 1, 7), (up1, 1, 0, 2), (up1, 1, 1, 0),
                (scatter, 0, 0, 5), (down1, 1, 0, 6), (down1, 1, 1, 4), (up1, 1, 2, 0), (up1, 1, 3, 2),
                (scatter, 0, 1, 7), (down1, 1, 2, 5), (down1, 1, 3, 6), (up1, 1, 4, 0), (up1, 1, 5, 2),
                (scatter, 0, 2, 4), (down1, 1, 4, 7), (down1, 1, 5, 5), (up1, 1, 6, 0), (up1, 1, 7, 2),
                (scatter, 0, 3, 6), (down1, 1, 6, 4), (down1, 1, 7, 7), (turn_gated, 1, 0, 5), (turn_gated, 1, 1, 6),
                (turn_y, 1, 0, 0), (turn_gated, 1, 2, 4), (turn_gated, 1, 3, 7), (turn_gated, 1, 4, 5),
                (turn_y, 1, 1, 6), (keep_warm, 2, 4), (scatter, 1, 0, 4), (scatter, 1, 1, 7), (scatter, 1, 2, 6),
                (scatter, 1, 3, 5),
            ):
                step(*at)


def host_constants():
    f = np.zeros((P, F_N), np.float32)
    f[:, F_ID:F_ID + P] = np.eye(P)
    f[:, F_SLOT:F_SLOT + CAP] = np.arange(1, CAP + 1)
    f[:, F_E0:F_E0 + E0] = np.arange(E0)
    f[:, F_S:F_S + S] = np.arange(S)
    b = np.zeros((PARTS * H, NP * P), np.float32)
    for r in range(PARTS * H):
        j, e = divmod(r % H, 2)
        b[r, j * P + e * S2:j * P + (e + 1) * S2] = 1
    return f, b


def kernel(x, ctx_1024, condB_tau, fside_BxS2_0,
           L0_xcond_Wq, L0_xcond_bq, L0_xcond_Wk, L0_xcond_bk, L0_xcond_Wv, L0_xcond_bv, L0_xcond_Wo, L0_xcond_bo,
           L0_ffn_gate_w, L0_ffn_gate_b, L0_ffn_shared_wg, L0_ffn_shared_wu, L0_ffn_shared_wd,
           L0_ffn_experts_wg, L0_ffn_experts_wu, L0_ffn_experts_wd,
           L1_xcond_Wq, L1_xcond_bq, L1_xcond_Wk, L1_xcond_bk, L1_xcond_Wv, L1_xcond_bv, L1_xcond_Wo, L1_xcond_bo,
           L1_ffn_router_w, L1_ffn_w1, L1_ffn_b1, L1_ffn_w2, L1_ffn_b2):
    import concourse.bacc as _bacc
    from concourse.bass_utils import run_bass_kernel_spmd as _run

    a = np.ascontiguousarray
    fconst, selection = host_constants()
    by_row = np.arange(P).reshape(NP, PR).T.reshape(P)
    ws = [[np.asarray(L0_xcond_Wq)[by_row], np.asarray(L0_xcond_Wk)[by_row], L0_xcond_Wv, L0_xcond_Wo],
          [np.asarray(L1_xcond_Wq)[by_row], np.asarray(L1_xcond_Wk)[by_row], L1_xcond_Wv, L1_xcond_Wo]]
    arrays = {
        "x": a(x),
        "ctxT": a(np.asarray(ctx_1024).reshape(B * S2, D).T),
        "wT": a(np.stack([np.stack([np.asarray(w).T for w in l], 1) for l in ws], 1)),
        "cols": a(np.concatenate([
            np.stack([L0_xcond_bq, L1_xcond_bq, L0_xcond_bk, L1_xcond_bk], 1)[by_row],
            np.asarray(L1_ffn_b1).reshape(E1 * NJ, P).T, np.asarray(L1_ffn_b2).T,
            np.asarray(L0_ffn_gate_w), np.asarray(L1_ffn_router_w).T, fconst], 1)),
        "rows": a(np.concatenate([L0_xcond_bv, L1_xcond_bv, L0_xcond_bo, L1_xcond_bo, L0_ffn_gate_b, condB_tau])),
        "delta": a(fside_BxS2_0),
        "wg": a(np.concatenate([L0_ffn_experts_wg, np.asarray(L0_ffn_shared_wg)[None]]).transpose(1, 0, 2)),
        "wu": a(np.concatenate([L0_ffn_experts_wu, np.asarray(L0_ffn_shared_wu)[None]]).transpose(1, 0, 2)),
        "wd": a(np.asarray(L0_ffn_experts_wd).reshape(NC0, P, D).transpose(1, 0, 2)),
        "wds": a(L0_ffn_shared_wd),
        "w1": a(np.asarray(L1_ffn_w1).transpose(1, 0, 2)),
        "w2": a(np.asarray(L1_ffn_w2).reshape(E1, NJ, P, D).transpose(2, 0, 1, 3)),
        "selection": selection,
    }
    nc = _bacc.Bacc("TRN2", target_bir_lowering=False, num_devices=1)
    args = [nc.dram_tensor(f"in_{n}", v.shape, mybir.dt.from_np(v.dtype), kind="ExternalInput").ap()
            for n, v in arrays.items()]
    args.append(nc.dram_tensor("out_x", (B, S, D), F32, kind="ExternalOutput").ap())
    build(nc, *args)
    r = _run(nc, [{f"in_{n}": v for n, v in arrays.items()}], core_ids=[0])
    return r.results[0]["out_x"]
```
